# Optimizing a Trainium2 kernel written in Bass

```python
import numpy as np
import jax
import jax.numpy as jnp

def _softmax(x, axis=-1):
    return jax.nn.softmax(x, axis=axis)

def _gelu(x):
    return jax.nn.gelu(x, approximate=True)

def _silu(x):
    return jax.nn.silu(x)

def _sigmoid(x):
    return jax.nn.sigmoid(x)

def _layernorm(x, axis=-1, eps=1e-05):
    m = jnp.mean(x, axis=axis, keepdims=True)
    v = jnp.var(x, axis=axis, keepdims=True)
    return (x - m) / jnp.sqrt(v + eps)

def _scatter_add(tgt, idx, src, axis=0):
    return tgt.at[idx].add(src)

def _segment_sum(src, seg, n):
    return jax.ops.segment_sum(src, seg, n)
kernel_name = 'mk_adaln_attn_ffn_d1_seqx_r2_f6b2fd'

def setup_inputs(seed: int=0):
    np.random.seed(seed)
    _w = jnp.asarray

    def _rec_inputs():
        import jax
        import jax.numpy as jnp
        _rk = jax.random.key(seed)
        x = -7.109e-05 + 0.9999 * jax.random.normal(jax.random.fold_in(_rk, 1), (8, 512, 512), jnp.float32)
        _lenS = 512 - jax.random.randint(jax.random.fold_in(_rk, 7), (8,), 0, max(1, 512 // 4) + 1, jnp.int32)
        _lenS2 = 512 - jax.random.randint(jax.random.fold_in(_rk, 8), (8,), 0, max(1, 512 // 4) + 1, jnp.int32)
        itok_B_0_30 = jax.random.randint(jax.random.fold_in(_rk, 11), (8,), 0, 31, jnp.int32)
        condB_zX = jax.random.uniform(jax.random.fold_in(_rk, 12), (8,), jnp.float32, 0.0, 0.983423)
        condB_zY = jax.random.uniform(jax.random.fold_in(_rk, 13), (8,), jnp.float32, 0.0, 0.979075)
        condB_zR = jax.random.uniform(jax.random.fold_in(_rk, 14), (8,), jnp.float32, 0.0, 0.9968)
        return (x, itok_B_0_30, condB_zX, condB_zY, condB_zR)
    x, itok_B_0_30, condB_zX, condB_zY, condB_zR = _rec_inputs()

    def _L0_cond_setup():
        import jax, jax.numpy as jnp
        import numpy as np
        B, C, D, T, N_SUBJ = (64, 512, 512, 512, 32)
        key = jax.random.key(seed)
        k1, k2, k3 = jax.random.split(key, 3)
        x = jax.random.normal(k1, (B, C, T), dtype=jnp.float32)
        subjects = jax.random.randint(k2, (B,), 0, N_SUBJ, dtype=jnp.int64)
        weights = jax.random.normal(k3, (N_SUBJ, C, D), dtype=jnp.float32) / np.sqrt(C).astype(np.float32)
        return {'x': x, 'subjects': subjects, 'weights': weights}
    _L0_cond_all = _L0_cond_setup()
    _L0_cond_in = {k: v for k, v in _L0_cond_all.items() if k in ('weights',)}
    del _L0_cond_all

    def _L0_attn_setup():
        import jax, jax.numpy as jnp
        import numpy as np
        N_EMBD = 512
        N_HEAD = 16
        N_LAYER = 24
        LAYER_ID = 12
        B, T = (4, 2048)
        Q = 64
        EPS = 1e-05 * 64

        def _static_params():
            C, H = (N_EMBD, N_HEAD)
            r01 = LAYER_ID / (N_LAYER - 1)
            r1a0 = 1.0 - LAYER_ID / N_LAYER
            ddd = np.arange(C, dtype=np.float64) / C
            maa_k = (1.0 - ddd ** r1a0).astype(np.float32).reshape(1, 1, C)
            maa_v = (1.0 - (ddd ** r1a0 + 0.3 * r01)).astype(np.float32).reshape(1, 1, C)
            maa_r = (1.0 - ddd ** (0.5 * r1a0)).astype(np.float32).reshape(1, 1, C)
            maa_g = maa_r.copy()
            h = np.arange(H, dtype=np.float64)
            decay = (-6.0 + 5.0 * (h / (H - 1)) ** (0.7 + 1.3 * r01)).astype(np.float32).reshape(H, 1)
            faaaa = (r01 * (1.0 - h / (H - 1))).astype(np.float32).reshape(H, 1)
            return (maa_k, maa_v, maa_r, maa_g, decay, faaaa)

        def _rwkv_forward(x, time_maa_k, time_maa_v, time_maa_r, time_maa_g, time_decay, time_faaaa, Wr, Wk, Wv, Wg, Wo, ln_w, ln_b):
            Bv, Tv, C = x.shape
            H = N_HEAD
            N = C // H
            nC = Tv // Q
            xx = jnp.pad(x, ((0, 0), (1, 0), (0, 0)))[:, :Tv] - x
            xk = x + xx * time_maa_k
            xv = x + xx * time_maa_v
            xr = x + xx * time_maa_r
            xg = x + xx * time_maa_g
            r = (xr @ Wr.T).reshape(Bv, Tv, H, N).transpose(0, 2, 1, 3)
            k = (xk @ Wk.T).reshape(Bv, Tv, H, N).transpose(0, 2, 3, 1)
            v = (xv @ Wv.T).reshape(Bv, Tv, H, N).transpose(0, 2, 1, 3)
            g = jax.nn.gelu(xg @ Wg.T, approximate=False)
            w = jnp.exp(-jnp.exp(time_decay))[:, 0]
            u = time_faaaa[:, 0]
            q = jnp.arange(Q)
            ws = (w ** Q).reshape(1, H, 1, 1)
            wk = (w[:, None] ** (Q - 1 - q)).reshape(1, H, 1, Q)
            wb = (w[:, None] ** q).reshape(1, H, Q, 1)
            i_idx = q[:, None]
            j_idx = q[None, :]
            e = jnp.maximum(i_idx - j_idx - 1, 0)
            Wmat = jnp.where(i_idx > j_idx, w[:, None, None] ** e, 0.0)
            Wmat = Wmat + jnp.eye(Q, dtype=x.dtype) * u[:, None, None]
            Wmat = Wmat.reshape(1, H, Q, Q)
            rr = r.reshape(Bv, H, nC, Q, N).transpose(2, 0, 1, 3, 4)
            kk = k.reshape(Bv, H, N, nC, Q).transpose(3, 0, 1, 2, 4)
            vv = v.reshape(Bv, H, nC, Q, N).transpose(2, 0, 1, 3, 4)

            def step(state, inp):
                rc, kc, vc = inp
                att = rc @ kc
                yc = att * Wmat @ vc + rc @ state * wb
                new_state = ws * state + kc * wk @ vc
                return (new_state, yc)
            state0 = jnp.zeros((Bv, H, N, N), dtype=x.dtype)
            _, ys = jax.lax.scan(step, state0, (rr, kk, vv))
            y = ys.transpose(1, 2, 0, 3, 4).reshape(Bv, H, Tv, N)
            y = y.transpose(0, 2, 1, 3)
            mean = y.mean(axis=-1, keepdims=True)
            var = y.var(axis=-1, keepdims=True)
            yn = (y - mean) / jnp.sqrt(var + EPS)
            yn = yn * ln_w.reshape(1, 1, H, N) + ln_b.reshape(1, 1, H, N)
            yn = yn.reshape(Bv, Tv, C)
            out = yn * g @ Wo.T
            return out
        key = jax.random.key(seed)
        ks = jax.random.split(key, 8)
        C = N_EMBD
        maa_k, maa_v, maa_r, maa_g, decay, faaaa = _static_params()
        std = 0.02
        return {'x': jax.random.normal(ks[0], (B, T, C), dtype=jnp.float32), 'time_maa_k': jnp.asarray(maa_k), 'time_maa_v': jnp.asarray(maa_v), 'time_maa_r': jnp.asarray(maa_r), 'time_maa_g': jnp.asarray(maa_g), 'time_decay': jnp.asarray(decay), 'time_faaaa': jnp.asarray(faaaa), 'Wr': jax.random.normal(ks[1], (C, C), dtype=jnp.float32) * std, 'Wk': jax.random.normal(ks[2], (C, C), dtype=jnp.float32) * std, 'Wv': jax.random.normal(ks[3], (C, C), dtype=jnp.float32) * std, 'Wg': jax.random.normal(ks[4], (C, C), dtype=jnp.float32) * std, 'Wo': jax.random.normal(ks[5], (C, C), dtype=jnp.float32) * std, 'ln_w': jnp.ones((C,), dtype=jnp.float32), 'ln_b': jnp.zeros((C,), dtype=jnp.float32)}
    _L0_attn_all = _L0_attn_setup()
    _L0_attn_in = {k: v for k, v in _L0_attn_all.items() if k in ('time_maa_k', 'time_maa_v', 'time_maa_r', 'time_maa_g', 'time_decay', 'time_faaaa', 'Wr', 'Wk', 'Wv', 'Wg', 'Wo', 'ln_w', 'ln_b')}
    del _L0_attn_all

    def _L0_cond2_setup():
        import jax, jax.numpy as jnp
        import numpy as np
        key = jax.random.key(seed)
        k1, k2, k3, k4 = jax.random.split(key, 4)
        B, H, W = (64, 512, 512)
        return {'y': jax.random.uniform(k1, (B, H, W), dtype=jnp.float32), 'zX': jax.random.uniform(k2, (B, 1), dtype=jnp.float32), 'zY': jax.random.uniform(k3, (B, 1), dtype=jnp.float32), 'zR': jax.random.uniform(k4, (B, 1), dtype=jnp.float32), 'dx': 1, 'dy': 1}
    _L0_cond2_all = _L0_cond2_setup()
    _L0_cond2_in = {k: v for k, v in _L0_cond2_all.items() if k in ()}
    del _L0_cond2_all

    def _L0_ffn_setup():
        import jax, jax.numpy as jnp
        import numpy as np
        key = jax.random.key(seed)
        ks = jax.random.split(key, 5)
        B, T, D, E = (4, 1024, 512, 8)
        inputs = jax.random.normal(ks[0], (B, T, D), dtype=jnp.float32)
        Wr = jax.random.normal(ks[1], (D, E), dtype=jnp.float32) * 0.02
        br = jnp.zeros((E,), dtype=jnp.float32)
        W1 = jax.random.normal(ks[2], (E, D, D), dtype=jnp.float32) * 0.02
        b1 = jnp.zeros((E, D), dtype=jnp.float32)
        W2 = jax.random.normal(ks[3], (E, D, D), dtype=jnp.float32) * 0.02
        b2 = jnp.zeros((E, D), dtype=jnp.float32)
        return {'inputs': inputs, 'Wr': Wr, 'br': br, 'W1': W1, 'b1': b1, 'W2': W2, 'b2': b2}
    _L0_ffn_all = _L0_ffn_setup()
    _L0_ffn_in = {k: v for k, v in _L0_ffn_all.items() if k in ('Wr', 'br', 'W1', 'b1', 'W2', 'b2')}
    del _L0_ffn_all
    return {'x': x, 'itok_B_0_30': itok_B_0_30, 'condB_zX': condB_zX, 'condB_zY': condB_zY, 'condB_zR': condB_zR, 'L0_cond_weights': _L0_cond_in['weights'], 'L0_attn_time_maa_k': _L0_attn_in['time_maa_k'], 'L0_attn_time_maa_v': _L0_attn_in['time_maa_v'], 'L0_attn_time_maa_r': _L0_attn_in['time_maa_r'], 'L0_attn_time_maa_g': _L0_attn_in['time_maa_g'], 'L0_attn_time_decay': _L0_attn_in['time_decay'], 'L0_attn_time_faaaa': _L0_attn_in['time_faaaa'], 'L0_attn_Wr': _L0_attn_in['Wr'], 'L0_attn_Wk': _L0_attn_in['Wk'], 'L0_attn_Wv': _L0_attn_in['Wv'], 'L0_attn_Wg': _L0_attn_in['Wg'], 'L0_attn_Wo': _L0_attn_in['Wo'], 'L0_attn_ln_w': _L0_attn_in['ln_w'], 'L0_attn_ln_b': _L0_attn_in['ln_b'], 'L0_ffn_Wr': _L0_ffn_in['Wr'], 'L0_ffn_br': _L0_ffn_in['br'], 'L0_ffn_W1': _L0_ffn_in['W1'], 'L0_ffn_b1': _L0_ffn_in['b1'], 'L0_ffn_W2': _L0_ffn_in['W2'], 'L0_ffn_b2': _L0_ffn_in['b2']}

def reference(x, itok_B_0_30, condB_zX, condB_zY, condB_zR, L0_cond_weights, L0_attn_time_maa_k, L0_attn_time_maa_v, L0_attn_time_maa_r, L0_attn_time_maa_g, L0_attn_time_decay, L0_attn_time_faaaa, L0_attn_Wr, L0_attn_Wk, L0_attn_Wv, L0_attn_Wg, L0_attn_Wo, L0_attn_ln_w, L0_attn_ln_b, L0_ffn_Wr, L0_ffn_br, L0_ffn_W1, L0_ffn_b1, L0_ffn_W2, L0_ffn_b2):
    import jax
    import jax.numpy as jnp

    def _L0_cond_ref(x, subjects, weights):
        import jax, jax.numpy as jnp
        import numpy as np
        B, C, D, T, N_SUBJ = (64, 512, 512, 512, 32)
        w = weights[subjects]
        return jnp.einsum('bct,bcd->bdt', x, w)

    def _L0_attn_ref(x, time_maa_k, time_maa_v, time_maa_r, time_maa_g, time_decay, time_faaaa, Wr, Wk, Wv, Wg, Wo, ln_w, ln_b):
        import jax, jax.numpy as jnp
        import numpy as np
        N_EMBD = 512
        N_HEAD = 16
        N_LAYER = 24
        LAYER_ID = 12
        B, T = (4, 2048)
        Q = 64
        EPS = 1e-05 * 64

        def _static_params():
            C, H = (N_EMBD, N_HEAD)
            r01 = LAYER_ID / (N_LAYER - 1)
            r1a0 = 1.0 - LAYER_ID / N_LAYER
            ddd = np.arange(C, dtype=np.float64) / C
            maa_k = (1.0 - ddd ** r1a0).astype(np.float32).reshape(1, 1, C)
            maa_v = (1.0 - (ddd ** r1a0 + 0.3 * r01)).astype(np.float32).reshape(1, 1, C)
            maa_r = (1.0 - ddd ** (0.5 * r1a0)).astype(np.float32).reshape(1, 1, C)
            maa_g = maa_r.copy()
            h = np.arange(H, dtype=np.float64)
            decay = (-6.0 + 5.0 * (h / (H - 1)) ** (0.7 + 1.3 * r01)).astype(np.float32).reshape(H, 1)
            faaaa = (r01 * (1.0 - h / (H - 1))).astype(np.float32).reshape(H, 1)
            return (maa_k, maa_v, maa_r, maa_g, decay, faaaa)

        def _rwkv_forward(x, time_maa_k, time_maa_v, time_maa_r, time_maa_g, time_decay, time_faaaa, Wr, Wk, Wv, Wg, Wo, ln_w, ln_b):
            Bv, Tv, C = x.shape
            H = N_HEAD
            N = C // H
            nC = Tv // Q
            xx = jnp.pad(x, ((0, 0), (1, 0), (0, 0)))[:, :Tv] - x
            xk = x + xx * time_maa_k
            xv = x + xx * time_maa_v
            xr = x + xx * time_maa_r
            xg = x + xx * time_maa_g
            r = (xr @ Wr.T).reshape(Bv, Tv, H, N).transpose(0, 2, 1, 3)
            k = (xk @ Wk.T).reshape(Bv, Tv, H, N).transpose(0, 2, 3, 1)
            v = (xv @ Wv.T).reshape(Bv, Tv, H, N).transpose(0, 2, 1, 3)
            g = jax.nn.gelu(xg @ Wg.T, approximate=False)
            w = jnp.exp(-jnp.exp(time_decay))[:, 0]
            u = time_faaaa[:, 0]
            q = jnp.arange(Q)
            ws = (w ** Q).reshape(1, H, 1, 1)
            wk = (w[:, None] ** (Q - 1 - q)).reshape(1, H, 1, Q)
            wb = (w[:, None] ** q).reshape(1, H, Q, 1)
            i_idx = q[:, None]
            j_idx = q[None, :]
            e = jnp.maximum(i_idx - j_idx - 1, 0)
            Wmat = jnp.where(i_idx > j_idx, w[:, None, None] ** e, 0.0)
            Wmat = Wmat + jnp.eye(Q, dtype=x.dtype) * u[:, None, None]
            Wmat = Wmat.reshape(1, H, Q, Q)
            rr = r.reshape(Bv, H, nC, Q, N).transpose(2, 0, 1, 3, 4)
            kk = k.reshape(Bv, H, N, nC, Q).transpose(3, 0, 1, 2, 4)
            vv = v.reshape(Bv, H, nC, Q, N).transpose(2, 0, 1, 3, 4)

            def step(state, inp):
                rc, kc, vc = inp
                att = rc @ kc
                yc = att * Wmat @ vc + rc @ state * wb
                new_state = ws * state + kc * wk @ vc
                return (new_state, yc)
            state0 = jnp.zeros((Bv, H, N, N), dtype=x.dtype)
            _, ys = jax.lax.scan(step, state0, (rr, kk, vv))
            y = ys.transpose(1, 2, 0, 3, 4).reshape(Bv, H, Tv, N)
            y = y.transpose(0, 2, 1, 3)
            mean = y.mean(axis=-1, keepdims=True)
            var = y.var(axis=-1, keepdims=True)
            yn = (y - mean) / jnp.sqrt(var + EPS)
            yn = yn * ln_w.reshape(1, 1, H, N) + ln_b.reshape(1, 1, H, N)
            yn = yn.reshape(Bv, Tv, C)
            out = yn * g @ Wo.T
            return out
        return _rwkv_forward(x, time_maa_k, time_maa_v, time_maa_r, time_maa_g, time_decay, time_faaaa, Wr, Wk, Wv, Wg, Wo, ln_w, ln_b)

    def _L0_cond2_ref(y, zX, zY, zR, dx, dy):
        import jax, jax.numpy as jnp
        import numpy as np
        yp_x = jnp.pad(y, ((0, 0), (0, 0), (1, 1)), mode='reflect')
        lap_x = (yp_x[:, :, :-2] - 2.0 * y + yp_x[:, :, 2:]) / (dx * dx)
        yp_y = jnp.pad(y, ((0, 0), (1, 1), (0, 0)), mode='reflect')
        lap_y = (yp_y[:, :-2, :] - 2.0 * y + yp_y[:, 2:, :]) / (dy * dy)
        du_dt = zX[:, :, None] * lap_x + zY[:, :, None] * lap_y + zR[:, :, None] * y * (1.0 - y)
        return du_dt

    def _L0_ffn_ref(inputs, Wr, br, W1, b1, W2, b2):
        import jax, jax.numpy as jnp
        import numpy as np
        B, T, D = inputs.shape
        E = Wr.shape[1]
        x = inputs.reshape(B * T, D)
        N = x.shape[0]
        C = N // E
        logits = x @ Wr + br
        probs = jax.nn.softmax(logits, axis=-1)
        gate = jnp.max(probs, axis=-1, keepdims=True)
        idx = jnp.argmax(probs, axis=-1)
        mask = jax.nn.one_hot(idx, E, dtype=jnp.float32)
        pos = (jnp.cumsum(mask, axis=0) * mask).astype(jnp.int32)
        mask = mask * (pos < C).astype(jnp.float32)
        mask_flat = jnp.sum(mask, axis=-1, keepdims=True)
        gate = gate * mask_flat
        combine = (gate * mask_flat * jax.nn.one_hot(idx, E, dtype=jnp.float32))[..., None] * jax.nn.one_hot(pos, C, dtype=jnp.float32)
        dispatch = combine
        expert_in = jnp.einsum('nd,nec->ecd', x, dispatch)
        h = jax.nn.relu(jnp.einsum('ecd,edf->ecf', expert_in, W1) + b1[:, None, :])
        eo = jnp.einsum('ecf,efd->ecd', h, W2) + b2[:, None, :]
        out = jnp.einsum('ecd,nec->nd', eo, combine)
        return out.reshape(B, T, D)
    x = x + _L0_attn_ref(_L0_cond_ref(x, itok_B_0_30, L0_cond_weights), L0_attn_time_maa_k, L0_attn_time_maa_v, L0_attn_time_maa_r, L0_attn_time_maa_g, L0_attn_time_decay, L0_attn_time_faaaa, L0_attn_Wr, L0_attn_Wk, L0_attn_Wv, L0_attn_Wg, L0_attn_Wo, L0_attn_ln_w, L0_attn_ln_b)
    x = x + _L0_ffn_ref(_L0_cond2_ref(x, condB_zX[:, None], condB_zY[:, None], condB_zR[:, None], 1, 1), L0_ffn_Wr, L0_ffn_br, L0_ffn_W1, L0_ffn_b1, L0_ffn_W2, L0_ffn_b2)
    return x

_drawn_inputs = setup_inputs


def setup_inputs(seed=0):
    import zlib

    import numpy as np

    out = dict(_drawn_inputs(seed))
    spreads = {'L0_attn_ln_w': (1.0, 0.6),
     'L0_attn_ln_b': (0.0, 0.6),
     'L0_ffn_br': (0.0, 0.1),
     'L0_ffn_b1': (0.0, 0.664),
     'L0_ffn_b2': (0.0, 0.1)}
    factors = {'L0_attn_time_faaaa': 6.676}
    for name, (base, spread) in spreads.items():
        noise = np.random.default_rng([zlib.crc32(name.encode()), seed]).standard_normal(out[name].shape)
        drawn = base * np.exp(spread * noise) if base else spread * noise
        out[name] = jnp.asarray(drawn.astype(out[name].dtype))
    for name, factor in factors.items():
        out[name] = (out[name] * factor).astype(out[name].dtype)
    return out
```

```python
from contextlib import ExitStack

import numpy as np

import concourse.bass as bass
from concourse import mybir

F32 = mybir.dt.float32
I32 = mybir.dt.int32
ACT = mybir.ActivationFunctionType
ALU = mybir.AluOpType
AX = mybir.AxisListType

P = 128
B, T, D = 8, 512, 512
KT = D // P
H, N = 16, 32
G = P // N
E = 8
CAP = B * T // E
EW = D + 4
META_GATE, META_TOKEN = D, D + 1
TRASH_ROWS = 2 * CAP
GN_EPS = 1e-5 * 64
HUGE_RATE = 1e30

PV_, PK_, PR_, PG_ = range(4)
RING = 8

C_ID, C_TRI, C_BLK, C_LAG, C_GT, C_Q = (128 * i for i in range(6))
C_TAIL = 6 * 128
C_PRI = C_TAIL + 1
C_EOFF = C_PRI + E
C_TOK = C_EOFF + E
C_TRASH = C_TOK + KT
CW = C_TRASH + 2 * KT


def shape_constants():
    p = np.arange(P)[:, None]
    q = np.arange(P)[None, :]
    r = np.arange(KT)[None, :]
    one = np.ones((P, 1))
    parts = [p == q, p < q, p // N == q // N, np.maximum(q - p - 1, 0), q > p, q + 0 * p,
             P - 1 - p, one * (E - np.arange(E)), one * (CAP * np.arange(E)), B * T + KT * p + r,
             B * T + KT * p + r + 1, B * T + CAP + KT * p + r + 1]
    out = np.concatenate([np.asarray(x, np.float32) for x in parts], axis=1)
    assert out.shape == (P, CW)
    return out


class Step:

    def __init__(self, reg, off):
        self.reg, self.off = reg, off

    def __sub__(self, k):
        return Step(self.reg, self.off - k)

    def __add__(self, k):
        return Step(self.reg, self.off + k)

    def at(self, per, k):
        return self.reg * per + (self.off * per + k)

    def exists(self):
        return not isinstance(self.reg, int) or 0 <= self.reg + self.off < B

    def index(self):
        return self.reg + self.off


def wait(eng, sem, value):
    if isinstance(value, int) and value <= 0:
        return
    eng.wait_ge(sem, value)


def build(nc, x, subj, zxyr, wcond, maa, wproj, wo, decay_heads, decay_rows, bonus, ln_wb, router_w,
          router_b, w1, b1, w2, b2, consts, out):
    slots = nc.dram_tensor("slots", (2 * B * T, EW), F32).ap()
    ctx = ExitStack()
    with ctx:
        def sb(name, shape, dt=F32):
            return ctx.enter_context(nc.sbuf_tensor(name, shape, dt))

        def sem(name):
            return ctx.enter_context(nc.semaphore(name))

        wts = sb("wts", [P, 5, KT, D])
        xw = sb("xw", [P, 2, KT * EW])
        hs = sb("hs", [P, KT, T + 1])
        diff = sb("diff", [P, KT, T])
        mix = sb("mix", [P, RING, T])
        kr = sb("kr", [P, 2, KT, T])
        v_sb = sb("v_sb", [P, KT, D])
        g_sb = sb("g_sb", [P, KT, D])
        decay = sb("decay", [P, G, KT, P])
        att = sb("att", [P, G, KT * P])
        rdec = sb("rdec", [P, 2, KT, P])
        kdec = sb("kdec", [P, D])
        state = sb("state", [P, 2, KT, P])
        st_new = kdec
        st_old = sb("st_old", [P, D])
        yc = sb("yc", [P, 2, D])
        sq = sb("sq", [P, D])
        stat = sb("stat", [P, 2, 6, H])
        zt = sb("zt", [P, KT, T])
        x1h = sb("x1h", [P, KT + 2, D])
        du = sb("du", [P, KT, EW])
        lh = sb("lh", [P, 2, D])
        lv = sb("lv", [P, 2, D])
        lq = sb("lq", [P, 2, D])
        dut = lh
        cst = sb("cst", [P, CW])
        ones = sb("ones", [P, P])
        lnwb = sb("lnwb", [P, 2, D])
        maa_sb = sb("maa_sb", [P, 4, KT])
        rate_h = sb("rate_h", [P, 2, H])
        rate_p = sb("rate_p", [P, 2, KT])
        bonus_sb = sb("bonus_sb", [P, H])
        kpow = sb("kpow", [P, H])
        rpow = sb("rpow", [P, KT, P])
        wpow = sb("wpow", [P, KT])
        zs = sb("zs", [P, 3, B])
        zq = sb("zq", [P, 2, B])
        rw_sb = sb("rw_sb", [P, KT, E])
        rb_sb = sb("rb_sb", [P, E])
        subj_sb = sb("subj_sb", [1, B], I32)
        lg = sb("lg", [P, 8, KT, E])
        rs = sb("rs", [P, 12, KT])
        cnt = sb("cnt", [P, E])
        base = sb("base", [P, E])
        trash = sb("trash", [P, KT])
        slot_i = sb("slot_i", [P, KT], I32)
        b1_sb = sb("b1_sb", [P, E, KT])
        b2_sb = yc
        tok_f = sb("tok_f", [P, 2, KT])
        tok_i = sb("tok_i", [P, 2, KT], I32)
        gate_e = sb("gate_e", [P, 2, KT])

        bank = [ctx.enter_context(nc.psum_tensor(f"bank{i}", [P, 512], F32)) for i in range(8)]
        LOW, HIGH = bank[:4], bank[4:]

        ident = cst[:, C_ID:C_ID + P]
        tri = cst[:, C_TRI:C_TRI + P]
        blk = cst[:, C_BLK:C_BLK + P]

        s_cst = sem("s_cst")
        s_cst2 = sem("s_cst2")
        s_subj = sem("s_subj")
        s_xw = sem("s_xw")
        s_wp = [sem(f"s_wp{i}") for i in range(5)]
        s_resid = sem("s_resid")
        s_store = sem("s_store")
        s_halo = sem("s_halo")
        s_scat = sem("s_scat")
        s_init = sem("s_init")
        s_tab = sem("s_tab")
        s_exp = sem("s_exp")
        s_cond = sem("s_cond")
        s_used = sem("s_used")
        s_proj = sem("s_proj")
        s_ztr = sem("s_ztr")
        s_o = sem("s_o")
        s_dtr = sem("s_dtr")
        s_log = sem("s_log")
        s_pre = sem("s_pre")
        s_sc = sem("s_sc")
        s_ktr = sem("s_ktr")
        s_kv = sem("s_kv")
        s_inter = sem("s_inter")
        s_pv = sem("s_pv")
        s_pev = sem("s_pev")
        s_hev = sem("s_hev")
        s_zev = sem("s_zev")
        s_dev = sem("s_dev")
        s_sq = sem("s_sq")
        s_sd = sem("s_sd")
        s_lq = sem("s_lq")
        s_rex = sem("s_rex")
        s_diff = sem("s_diff")
        s_mix = sem("s_mix")
        s_mask = sem("s_mask")
        s_kdec = sem("s_kdec")
        s_st = sem("s_st")
        s_nrm = sem("s_nrm")
        s_vs = sem("s_vs")
        s_x1 = sem("s_x1")
        s_lap = sem("s_lap")
        NR = 31
        s_rt = sem("s_rt")
        s_rdec = sem("s_rdec")
        s_wst = sem("s_wst")
        s_z = sem("s_z")
        s_lv = sem("s_lv")
        s_act_on = sem("s_act_on")
        s_pool_on = sem("s_pool_on")
        s_we = [sem(f"s_we{i}") for i in range(2)]
        s_ein = [sem(f"s_ein{i}") for i in range(2)]
        s_add = [sem(f"s_add{i}") for i in range(2)]
        s_etr = sem("s_etr")
        s_eev = sem("s_eev")
        s_up = sem("s_up")
        s_relu = sem("s_relu")
        s_down = sem("s_down")
        s_b2 = sem("s_b2")
        s_gate = sem("s_gate")
        s_tok = sem("s_tok")

        block = ctx.enter_context(nc.Block())

        N_ZERO = 16 * (E + 2)
        N_TAB = 2 + 2 * H + 3
        n_cst, n_cst2 = 6 * 16, 5 * 16

        def used_wait(eng, b, p, tt):
            if tt < KT - 1:
                wait(eng, s_used, b.at(12, 3 * p + tt + 1))
            else:
                wait(eng, s_proj, b.at(16, 4 * p + 4))

        def attention_bodies(eng, body):
            for b in range(2):
                body(Step(0, b))
            with eng.Fori(0, B - 3) as i:
                body(Step(i, 2))
            for b in range(B - 1, B + 2):
                body(Step(0, b))

        def load_weights(sp, t, e):
            n = t.index() * 2 + e
            sp.dma_start(wts[:, 2 * e, :, :],
                         w1[bass.ds(n, 1)].rearrange("a (k p) f -> p (a k) f", p=P)).then_inc(s_we[e], 16)
            sp.dma_start(wts[:, 2 * e + 1, :, :],
                         w2[bass.ds(n, 1)].rearrange("a (k p) f -> p (a k) f", p=P)).then_inc(s_we[e], 16)

        def load_rows(sp, t, e):
            n = t.index() * 2 + e
            sp.dma_start(xw[:, e, :],
                         slots[bass.ds(n * CAP, CAP)].rearrange("(p r) c -> p (r c)", r=KT)).then_inc(s_ein[e], 16)
            sp.dma_start(b2_sb[:, e, :], b2[bass.ds(n, 1)].to_broadcast([P, D])).then_inc(s_ein[e], 16)

        @block.sync
        def _(sp):
            sp.dma_start(subj_sb[:], subj).then_inc(s_subj, 16)
            sp.dma_start(cst[:], consts).then_inc(s_cst, 16)
            sp.dma_start(rate_h[:, 1, :], decay_heads.to_broadcast([P, H])).then_inc(s_cst, 16)
            sp.dma_start(rate_p[:, 1, :], decay_rows).then_inc(s_cst, 16)
            sp.dma_start(bonus_sb[:], bonus.to_broadcast([P, H])).then_inc(s_cst, 16)
            sp.dma_start(maa_sb[:], maa).then_inc(s_cst, 16)
            sp.dma_start(zs[:], zxyr.to_broadcast([P, 3, B])).then_inc(s_cst, 16)
            sp.wait_ge(s_subj, 16)

            def load_xw(b):
                s = sp.value_load(subj_sb[0:1, bass.ds(b.index(), 1)], min_val=0, max_val=wcond.shape[0] - 1)
                sp.dma_start(xw[:, 0, 0:KT * T],
                             x[bass.ds(b.index(), 1)].rearrange("a (p r) t -> (a p) (r t)", r=KT)).then_inc(s_xw, 16)
                sp.dma_start(xw[:, 1, 0:KT * T],
                             wcond[bass.ds(s, 1)].rearrange("a (p r) t -> (a p) (r t)", r=KT)).then_inc(s_xw, 16)

            load_xw(Step(0, 0))
            sp.dma_start(lnwb[:], ln_wb.to_broadcast([P, 2, D])).then_inc(s_cst2, 16)
            sp.dma_start(rw_sb[:], router_w.rearrange("(k p) e -> p k e", p=P)).then_inc(s_cst2, 16)
            sp.dma_start(rb_sb[:], router_b.to_broadcast([P, E])).then_inc(s_cst2, 16)
            sp.dma_start(b1_sb[:], b1).then_inc(s_cst2, 16)
            sp.dma_start(trash[:], consts[:, C_TOK:C_TOK + KT]).then_inc(s_cst2, 16)
            for p in range(5):
                src = wproj[p] if p < 4 else wo
                sp.dma_start(wts[:, p, :, :], src.rearrange("(k p) o -> p k o", p=P)).then_inc(s_wp[p], 16)
            sp.wait_ge(s_cond, 4)
            load_xw(Step(0, 1))

            def body(b):
                if (b - 1).exists():
                    wait(sp, s_lap, (b - 2).at(20, 20))
                    wait(sp, s_lv, (b - 2).at(4, 4))
                    wait(sp, s_lq, (b - 2).at(4, 4))
                    wait(sp, s_store, (b - 2).at(16, 16))
                    sp.dma_start(x1h[:, 1:KT + 1, :],
                                 x[bass.ds((b - 1).index(), 1)].rearrange("a (p r) t -> (a p) r t", r=KT)
                                 ).then_inc(s_resid, 16)
                    sp.wait_ge(s_x1, (b - 1).at(4, 4))
                    sp.dma_start(out[bass.ds((b - 1).index() * T, T)].rearrange("(p r) t -> p r t", r=KT),
                                 x1h[:, 1:KT + 1, :]).then_inc(s_store, 16)
                    for lo, hi in ((1, 113), (113, P)):
                        sp.dma_start(x1h[lo:hi, 0, :], x1h[lo - 1:hi - 1, KT, :]).then_inc(s_halo, 16)
                    for lo, hi in ((0, 112), (112, P - 1)):
                        sp.dma_start(x1h[lo:hi, KT + 1, :], x1h[lo + 1:hi + 1, 1, :]).then_inc(s_halo, 16)
                    sp.dma_start(x1h[0:1, 0, :], x1h[0:1, 2, :]).then_inc(s_halo, 16)
                    sp.dma_start(x1h[P - 1:P, KT + 1, :], x1h[P - 1:P, KT - 1, :]).then_inc(s_halo, 16)
                if (b + 2).exists():
                    sp.wait_ge(s_cond, (b + 1).at(4, 4))
                    load_xw(b + 2)

            for b in range(2):
                body(Step(0, b))
            with sp.Fori(0, B - 4) as i:
                body(Step(i, 2))
            for b in range(B - 2, B + 2):
                if b == B:
                    sp.wait_ge(s_proj, 16 * B)
                    for e in range(2):
                        load_weights(sp, Step(0, 0), e)
                body(Step(0, b))

            sp.wait_ge(s_scat, 64 * B + N_ZERO)
            for e in range(2):
                load_rows(sp, Step(0, 0), e)
            with sp.Fori(0, E // 2 - 1) as i:
                for e in range(2):
                    sp.wait_ge(s_down, Step(i, 0).at(8, 4 * e + 4))
                    load_weights(sp, Step(i, 1), e)
                    sp.wait_ge(s_etr, Step(i, 0).at(8, 4 * e + 4))
                    sp.wait_ge(s_tok, Step(i, 0).at(8, 4 * e + 4))
                    sp.wait_ge(s_b2, Step(i, 0).at(8, 4 * e + 4))
                    load_rows(sp, Step(i, 1), e)
            sp.wait_ge(s_store, 16 * B)

        @block.tensor
        def _(pe):
            def cond_tile(b, m, dst):
                xv = xw[:, 0, 0:KT * T].rearrange("p (r t) -> p r t", r=KT)
                wv = xw[:, 1, 0:KT * T].rearrange("p (r t) -> p r t", r=KT)
                if m == 0:
                    pe.wait_ge(s_xw, b.at(32, 32))
                for r in range(KT):
                    last = pe.matmul(dst[:], xv[:, r, m * P:(m + 1) * P], wv[:, r, :], start=r == 0, stop=r == KT - 1)
                last.then_inc(s_cond, 1)

            def project(b, p, banks, free):
                wait(pe, s_wp[p], 16)
                for tt in range(KT):
                    pe.wait_ge(s_mix, b.at(16, 4 * p + tt + 1))
                    mx = mix[:, (4 * p + tt) % RING, :]
                    for m in range(KT):
                        if tt == 0:
                            free(m)
                        if p in (PV_, PG_):
                            lhs, rhs = mx[:, m * P:(m + 1) * P], wts[:, p, tt, :]
                        else:
                            lhs, rhs = wts[:, p, tt, m * P:(m + 1) * P], mx
                        ins = pe.matmul(banks[m][:], lhs, rhs, start=tt == 0, stop=tt == KT - 1)
                        if tt == KT - 1:
                            ins.then_inc(s_proj, 1)
                    if tt < KT - 1:
                        ins.then_inc(s_used, 1)

            def z_transpose(b):
                pe.wait_ge(s_z, b.at(8, 8))
                for k in range(KT):
                    if (b + 1).exists():
                        pe.wait_ge(s_pev, (b + 1).at(16, k + 1))
                    else:
                        pe.wait_ge(s_mask, b.at(16, 16))
                    for c in range(KT):
                        last = pe.transpose(HIGH[k][:, c * P:(c + 1) * P], g_sb[:, c, k * P:(k + 1) * P], ident)
                    last.then_inc(s_ztr, 1)

            def output_product(b):
                pe.wait_ge(s_wp[4], 16)
                pe.wait_ge(s_zev, b.at(4, 4))
                for r in range(KT):
                    nxt = b + 1
                    if nxt.exists():
                        pe.wait_ge(s_pev, nxt.at(16, 4 * PR_ + r + 1))
                    else:
                        wait(pe, s_nrm, b.at(28, 7 * 3 + 3) if r == 1 else b.at(28, 7 * 2 + 3))
                        wait(pe, s_st, b.at(5, 5))
                    for k in range(KT):
                        last = pe.matmul(LOW[r][:], zt[:, k, r * P:(r + 1) * P], wts[:, 4, k, :],
                                         start=k == 0, stop=k == KT - 1)
                    last.then_inc(s_o, 1)

            def logits(b):
                for k in range(KT):
                    if (b + 2).exists():
                        wait(pe, s_pev, (b + 2).at(16, 4 * PG_ + k + 1))
                    elif (b + 1).exists():
                        wait(pe, s_zev, (b + 1).at(4, k + 1))
                    else:
                        pe.wait_ge(s_dev, (b - 1).at(4, k + 1))
                    if k == 0:
                        pe.wait_ge(s_lap, b.at(20, 20))
                    for r in range(KT):
                        last = pe.transpose(HIGH[k][:, r * P:(r + 1) * P], du[:, r, k * P:(k + 1) * P], ident)
                    last.then_inc(s_dtr, 1)
                if (b + 1).exists():
                    pe.wait_ge(s_x1, (b + 1).at(4, 1))
                else:
                    pe.wait_ge(s_rt, (b - 1).at(NR, 12))
                pe.wait_ge(s_cst2, n_cst2)
                for k in range(KT):
                    pe.wait_ge(s_dev, b.at(4, k + 1))
                    for r in range(KT):
                        last = pe.matmul(LOW[0][:, r * E:(r + 1) * E], dut[:, k % 2, r * P:(r + 1) * P],
                                         rw_sb[:, k, :], start=k == 0 and r == 0, stop=k == KT - 1,
                                         skip_group_check=True)
                    last.then_inc(s_log, 1)

            def prefix(b):
                pe.wait_ge(s_rt, b.at(NR, 8))
                if (b + 1).exists():
                    pe.wait_ge(s_x1, (b + 1).at(4, 2))
                pe.matmul(LOW[1][:, 0:E], tri, cnt[:], start=True, stop=False, skip_group_check=True)
                pe.matmul(LOW[1][:, E:2 * E], ones[:], cnt[:], start=False, stop=True,
                          skip_group_check=True).then_inc(s_pre, 1)

            def scores(b, c):
                if c == 0:
                    pe.wait_ge(s_pev, b.at(16, 12))
                for g in range(KT):
                    for i in range(G):
                        if g == 0:
                            if c > 0:
                                pe.wait_ge(s_mask, b.at(16, 4 * (c - 1) + i + 1))
                            elif (b - 2).exists():
                                pe.wait_ge(s_dev, (b - 2).at(4, i + 1))
                            else:
                                pe.wait_ge(s_pev, b.at(16, 4 * PG_ + i + 1))
                        hp = slice(N * i, N * (i + 1))
                        ins = pe.matmul(HIGH[i][:, g * P:(g + 1) * P], kr[hp, 0, g, c * P:(c + 1) * P],
                                        kr[hp, 1, g, c * P:(c + 1) * P], start=True, stop=True)
                        if g == KT - 1:
                            ins.then_inc(s_sc, 1)

            def bank_of_state(b, c):
                if c > 0:
                    wait(pe, s_st, b.at(5, (1, 2)[c - 1]))
                elif (b - 1).exists():
                    pe.wait_ge(s_x1, (b - 1).at(4, 3))
                else:
                    pe.wait_ge(s_pev, b.at(16, 4 * PR_ + 3))

            def k_transpose(b, c):
                bank_of_state(b, c)
                for g in range(KT):
                    last = pe.transpose(LOW[2][:, g * P:(g + 1) * P], kr[:, 0, g, c * P:(c + 1) * P], ident)
                last.then_inc(s_ktr, 1)

            def state_product(b, c):
                pe.wait_ge(s_kdec, b.at(3, c + 1))
                for g in range(KT):
                    last = pe.matmul(LOW[2][:, g * P:(g + 1) * P], kdec[:, g * P:(g + 1) * P],
                                     v_sb[:, c, g * P:(g + 1) * P], start=True, stop=True)
                last.then_inc(s_kv, 1)

            def bank_of_y(b, c):
                if c >= 2:
                    pe.wait_ge(s_nrm, b.at(28, 7 * (c - 2) + 3))
                elif (b - 2).exists():
                    pe.wait_ge(s_rt, (b - 2).at(NR, 1 if c == 0 else 12))
                elif (b - 1).exists():
                    pe.wait_ge(s_x1, (b - 1).at(4, c + 1))
                else:
                    pe.wait_ge(s_pev, b.at(16, 4 * PR_ + c + 1))

            def from_state(b, c):
                bank_of_y(b, c)
                pe.wait_ge(s_st, b.at(5, (1, 3, 5)[c - 1]))
                pe.wait_ge(s_rdec, b.at(3, c))
                for g in range(KT):
                    last = pe.matmul(LOW[c % 2][:, g * P:(g + 1) * P], rdec[:, c % 2, g, :], state[:, c % 2, g, :],
                                     start=g == 0, stop=False, skip_group_check=True)
                last.then_inc(s_inter, 1)

            def from_scores(b, c):
                if c == 0:
                    bank_of_y(b, 0)
                for i in range(G):
                    pe.wait_ge(s_mask, b.at(16, 4 * c + i + 1))
                    for g in range(KT):
                        h0 = g * P + i * N
                        last = pe.matmul(LOW[c % 2][:, h0:h0 + N], att[:, i, g * P:(g + 1) * P],
                                         v_sb[:, c, h0:h0 + N], start=c == 0 and i == 0 and g == 0,
                                         stop=i == G - 1, skip_group_check=True)
                    last.then_inc(s_pv, 1)

            def cond_bank(b, m):
                if m > 0:
                    pe.wait_ge(s_hev, (b + 1).at(4, m))
                elif (b - 1).exists():
                    pe.wait_ge(s_x1, (b - 1).at(4, 4))
                else:
                    pe.wait_ge(s_pev, b.at(16, 4 * PR_ + 4))

            def body(b):
                if b.exists():
                    def free_v(m):
                        wait(pe, s_mask, b.at(16, 0))

                    def free_k(m):
                        if not (b - 1).exists():
                            if m == 0:
                                pe.wait_ge(s_hev, 4)
                        elif m < 2:
                            pe.wait_ge(s_nrm, (b - 1).at(28, 7 * (m + 2) + 3))
                        elif m == 2:
                            pe.wait_ge(s_st, (b - 1).at(5, 5))
                        else:
                            pe.wait_ge(s_hev, b.at(4, 4))

                    def free_r(m):
                        pe.wait_ge(s_pev, b.at(16, 4 * PK_ + m + 1))

                    def free_g(m):
                        if (b - 1).exists():
                            pe.wait_ge(s_zev, (b - 1).at(4, m + 1))
                        else:
                            pe.wait_ge(s_pev, b.at(16, m + 1))

                    project(b, PV_, HIGH, free_v)
                    project(b, PK_, LOW, free_k)
                if (b - 1).exists():
                    z_transpose(b - 1)
                if b.exists():
                    project(b, PR_, LOW, free_r)
                    project(b, PG_, HIGH, free_g)
                if (b - 1).exists():
                    output_product(b - 1)
                if (b - 2).exists():
                    logits(b - 2)
                if not b.exists():
                    if (b - 2).exists():
                        prefix(b - 2)
                    return
                for c in range(KT):
                    scores(b, c)
                    if c < KT - 1:
                        k_transpose(b, c)
                    if c > 0:
                        from_scores(b, c - 1)
                    elif (b - 2).exists():
                        prefix(b - 2)
                    if (b + 1).exists():
                        cond_bank(b, c)
                        cond_tile(b + 1, c, LOW[3])
                    if c < KT - 1:
                        state_product(b, c)
                    if c > 0:
                        from_state(b, c)
                from_scores(b, KT - 1)

            for m in range(KT):
                if m == 0:
                    pe.wait_ge(s_cst, n_cst)
                    pe.wait_ge(s_init, 2)
                cond_tile(Step(0, 0), m, LOW[m])
            attention_bodies(pe, body)

            def e_transpose(t, e):
                pe.wait_ge(s_ein[e], t.at(32, 32))
                rows = xw[:, e, :].rearrange("p (r c) -> p r c", r=KT)
                for k in range(KT):
                    pe.wait_ge(s_eev, t.at(8, 4 * e + k + 1 - 4)) if not (
                        isinstance(t.reg, int) and t.reg + t.off == 0 and e == 0) else None
                    for r in range(KT):
                        last = pe.transpose(HIGH[k][:, r * P:(r + 1) * P], rows[:, r, k * P:(k + 1) * P], ident)
                    last.then_inc(s_etr, 1)

            def e_up(t, e, first):
                pe.wait_ge(s_we[e], t.at(32, 32))
                for k in range(KT):
                    pe.wait_ge(s_eev, t.at(8, 4 * e + k + 1))
                    for m in range(KT):
                        if k == 0 and not first:
                            pe.wait_ge(s_b2, t.at(8, 4 * e + m + 1 - 4))
                        ins = pe.matmul(LOW[m][:], wts[:, 2 * e, k, m * P:(m + 1) * P], mix[:, k, :],
                                        start=k == 0, stop=k == KT - 1)
                        if k == KT - 1:
                            ins.then_inc(s_up, 1)

            def e_down(t, e):
                pe.wait_ge(s_relu, t.at(8, 4 * e + 4))
                for r in range(KT):
                    for m in range(KT):
                        last = pe.matmul(LOW[r][:], mix[:, 4 + m, r * P:(r + 1) * P], wts[:, 2 * e + 1, m, :],
                                         start=m == 0, stop=m == KT - 1)
                    last.then_inc(s_down, 1)

            def pair(t, first, last):
                e_up(t, 0, first)
                e_transpose(t, 1)
                e_down(t, 0)
                e_up(t, 1, False)
                if not last:
                    e_transpose(t + 1, 0)
                e_down(t, 1)

            pe.wait_ge(s_dev, 4 * B)
            pe.wait_ge(s_rt, NR * B)
            e_transpose(Step(0, 0), 0)
            pair(Step(0, 0), True, False)
            with pe.Fori(0, E // 2 - 2) as i:
                pair(Step(i, 1), False, False)
            pair(Step(0, E // 2 - 1), False, True)

        @block.scalar
        def _(act):
            act.wait_ge(s_cst, n_cst)
            act.activation(rate_h[:, 0, :], rate_h[:, 1, :], ACT.Exp).then_inc(s_exp, 1)
            act.activation(rate_p[:, 0, :], rate_p[:, 1, :], ACT.Exp).then_inc(s_exp, 1)
            act.wait_ge(s_tab, 2)
            for h in range(H):
                act.activation(decay[:, h % G, h // G, :], cst[:, C_LAG:C_LAG + P], ACT.Exp,
                               scale=rate_h[:, 1, h:h + 1]).then_inc(s_exp, 1)
            act.activation(kpow[:], rate_h[:, 1, :], ACT.Exp, scale=cst[:, C_TAIL:C_TAIL + 1]).then_inc(s_exp, 1)
            for g in range(KT):
                act.activation(rpow[:, g, :], cst[:, C_Q:C_Q + P], ACT.Exp,
                               scale=rate_p[:, 1, g:g + 1]).then_inc(s_exp, 1)
            act.activation(wpow[:], rate_p[:, 1, :], ACT.Exp, scale=float(P)).then_inc(s_exp, 1)

            def h_evac(b, m, src):
                if m == 0:
                    wait(act, s_mix, (b - 1).at(16, 16))
                act.wait_ge(s_cond, b.at(4, m + 1))
                act.activation(hs[:, m, 1:T + 1], src[:], ACT.Copy).then_inc(s_hev, 1)

            act.wait_ge(s_init, 2)
            for m in range(KT):
                h_evac(Step(0, 0), m, LOW[m])

            def proj_evac(b, p, banks):
                dst = {PV_: v_sb, PG_: g_sb}.get(p)
                for m in range(KT):
                    act.wait_ge(s_proj, b.at(16, 4 * p + m + 1))
                    if m == 0:
                        if p == PV_:
                            wait(act, s_pv, b.at(16, 0))
                        if p == PR_:
                            wait(act, s_rdec, b.at(3, 0))
                        if p == PG_:
                            wait(act, s_ztr, b.at(4, 0))
                    o = dst[:, m, :] if dst is not None else kr[:, p - PK_, m, :]
                    act.activation(o, banks[m][:], ACT.Gelu if p == PG_ else ACT.Copy).then_inc(s_pev, 1)

            def z_evac(b):
                for k in range(KT):
                    act.wait_ge(s_ztr, b.at(4, k + 1))
                    if k == 0:
                        wait(act, s_o, b.at(4, 0))
                    act.activation(zt[:, k, :].rearrange("p (r q) -> p r q", r=KT),
                                   HIGH[k][:].rearrange("p (q r) -> p r q", r=KT), ACT.Copy).then_inc(s_zev, 1)

            def lap_factor(b, r):
                if r == 0:
                    act.wait_ge(s_x1, b.at(4, 4))
                if r >= 2:
                    act.wait_ge(s_lap, b.at(20, 5 * (r - 2) + 5))
                act.sem_inc(s_act_on, 1)
                act.wait_ge(s_tab, N_TAB)
                act.activation(lq[:, r % 2, :], x1h[:, r + 1, :], ACT.Identity, bias=zq[:, 1, bass.ds(b.index(), 1)],
                               scale=zq[:, 0, bass.ds(b.index(), 1)]).then_inc(s_lq, 1)

            def du_evac(b):
                for k in range(KT):
                    act.wait_ge(s_dtr, b.at(4, k + 1))
                    if k >= 2:
                        act.wait_ge(s_log, b.at(4, k - 1))
                    act.activation(dut[:, k % 2, :], HIGH[k][:], ACT.Copy).then_inc(s_dev, 1)

            def body(b):
                if b.exists():
                    proj_evac(b, PV_, HIGH)
                if (b - 2).exists():
                    lap_factor(b - 2, 0)
                    lap_factor(b - 2, 1)
                if b.exists():
                    proj_evac(b, PK_, LOW)
                if (b - 1).exists():
                    z_evac(b - 1)
                if (b - 2).exists():
                    lap_factor(b - 2, 2)
                    lap_factor(b - 2, 3)
                if b.exists():
                    proj_evac(b, PR_, LOW)
                    proj_evac(b, PG_, HIGH)
                if (b - 2).exists():
                    du_evac(b - 2)
                    act.wait_ge(s_rt, (b - 2).at(NR, 3))
                    act.activation(lg[:, 2, :, :], lg[:, 1, :, :], ACT.Exp).then_inc(s_rex, 1)
                if b.exists():
                    for c in range(KT + 1):
                        if c < KT and (b + 1).exists():
                            h_evac(b + 1, c, LOW[3])
                        if c > 0:
                            norm_act(b, c - 1)

            def norm_act(b, c):
                act.wait_ge(s_nrm, b.at(28, 7 * c + 3))
                wait(act, s_vs, b.at(4, c))
                act.activation(sq[:], yc[:, c % 2, :], ACT.Square).then_inc(s_sq, 1)
                act.wait_ge(s_nrm, b.at(28, 7 * c + 4))
                act.activation(stat[:, c % 2, 3, :], stat[:, c % 2, 2, :], ACT.Sqrt).then_inc(s_sd, 1)

            attention_bodies(act, body)

            def e_evac(t, e):
                for k in range(KT):
                    act.wait_ge(s_etr, t.at(8, 4 * e + k + 1))
                    if k == 0 and not (isinstance(t.reg, int) and t.reg + t.off == 0 and e == 0):
                        act.wait_ge(s_up, t.at(8, 4 * e))
                    act.activation(mix[:, k, :], HIGH[k][:], ACT.Copy).then_inc(s_eev, 1)

            def e_relu(t, e, first):
                for m in range(KT):
                    act.wait_ge(s_up, t.at(8, 4 * e + m + 1))
                    if m == 0 and not first:
                        act.wait_ge(s_down, t.at(8, 4 * e))
                    act.sem_inc(s_act_on, 1)
                    act.wait_ge(s_cst2, n_cst2)
                    act.activation(mix[:, 4 + m, :], LOW[m][:], ACT.Relu,
                                   bias=b1_sb[:, bass.ds(t.index() * 2 + e, 1), m]).then_inc(s_relu, 1)

            def pair(t, first, last):
                e_relu(t, 0, first)
                e_evac(t, 1)
                e_relu(t, 1, False)
                if not last:
                    e_evac(t + 1, 0)

            e_evac(Step(0, 0), 0)
            pair(Step(0, 0), True, False)
            with act.Fori(0, E // 2 - 2) as i:
                pair(Step(i, 1), False, False)
            pair(Step(0, E // 2 - 1), False, True)

        @block.vector
        def _(dve):
            dve.memset(hs[:, :, 0:1], 0.0).then_inc(s_init, 1)
            dve.memset(ones[:], 1.0).then_inc(s_init, 1)
            dve.memset(base[:], 1.0).then_inc(s_init, 1)
            dve.memset(du[:], 0.0).then_inc(s_init, 1)
            dve.wait_ge(s_exp, 2)
            dve.tensor_scalar(rate_h[:, 1, :], rate_h[:, 0, :], HUGE_RATE, -1.0, ALU.min, ALU.mult).then_inc(s_tab, 1)
            dve.tensor_scalar(rate_p[:, 1, :], rate_p[:, 0, :], HUGE_RATE, -1.0, ALU.min, ALU.mult).then_inc(s_tab, 1)
            for h in range(H):
                d = decay[:, h % G, h // G, :]
                dve.wait_ge(s_exp, 2 + h + 1)
                dve.tensor_tensor(d, d, cst[:, C_GT:C_GT + P], ALU.mult).then_inc(s_tab, 1)
            for h in range(H):
                d = decay[:, h % G, h // G, :]
                dve.wait_ge(s_tab, 2 + h + 1)
                dve.scalar_tensor_tensor(d, ident, bonus_sb[:, h:h + 1], d, ALU.mult, ALU.add).then_inc(s_tab, 1)
            n_tab = N_TAB - 3
            dve.tensor_scalar(zq[:, 0, :], zs[:, 2, :], -1.0, None, ALU.mult).then_inc(s_tab, 1)
            dve.tensor_tensor(zq[:, 1, :], zs[:, 0, :], zs[:, 1, :], ALU.add).then_inc(s_tab, 1)
            dve.wait_ge(s_tab, n_tab + 2)
            dve.scalar_tensor_tensor(zq[:, 1, :], zq[:, 1, :], -2.0, zs[:, 2, :], ALU.mult, ALU.add).then_inc(s_tab, 1)

            def difference(b):
                dve.wait_ge(s_hev, b.at(4, 4))
                wait(dve, s_mix, b.at(16, 0))
                dve.tensor_tensor(diff[:], hs[:, :, 0:T], hs[:, :, 1:T + 1], ALU.subtract).then_inc(s_diff, 1)

            def mixing(b, p):
                if p == PV_:
                    dve.wait_ge(s_diff, b.at(1, 1))
                for tt in range(KT):
                    j = 4 * p + tt - RING
                    used_wait(dve, b if j >= 0 else b - 1, (j % 16) // 4, j % 4)
                    dve.scalar_tensor_tensor(mix[:, (4 * p + tt) % RING, :], diff[:, tt, :],
                                             maa_sb[:, p, tt:tt + 1], hs[:, tt, 1:T + 1],
                                             ALU.mult, ALU.add).then_inc(s_mix, 1)

            def laplacian(b, r):
                y = x1h[:, r + 1, :]
                s = b.index()
                lhr, lvr, lqr = lh[:, r % 2, :], lv[:, r % 2, :], lq[:, r % 2, :]
                dve.tensor_tensor(lhr[:, 1:D - 1], y[:, 0:D - 2], y[:, 2:D], ALU.add).then_inc(s_lap, 1)
                dve.tensor_scalar(lhr[:, 0:D:D - 1], y[:, 1:D - 1:D - 3], 2.0, None, ALU.mult).then_inc(s_lap, 1)
                dve.wait_ge(s_lq, b.at(4, r + 1))
                dve.tensor_tensor(lqr, lqr, y, ALU.mult).then_inc(s_lap, 1)
                dve.wait_ge(s_lap, b.at(20, 5 * r + 3))
                dve.scalar_tensor_tensor(lqr, lhr, zs[:, 0, bass.ds(s, 1)], lqr, ALU.mult, ALU.add).then_inc(s_lap, 1)
                dve.wait_ge(s_lap, b.at(20, 5 * r + 4))
                dve.wait_ge(s_lv, b.at(4, r + 1))
                dve.scalar_tensor_tensor(du[:, r, 0:D], lvr, zs[:, 1, bass.ds(s, 1)], lqr, ALU.mult,
                                         ALU.add).then_inc(s_lap, 1)

            def residual(b):
                dve.wait_ge(s_resid, b.at(16, 16))
                for r in range(KT):
                    dve.wait_ge(s_o, b.at(4, r + 1))
                    dve.tensor_tensor(x1h[:, r + 1, :], LOW[r][:], x1h[:, r + 1, :], ALU.add).then_inc(s_x1, 1)

            def bc_e(v):
                return v.unsqueeze(2).to_broadcast([P, KT, E])

            def bc_r(v):
                return v.unsqueeze(1).to_broadcast([P, KT, E])

            def router(b, part):
                n = [8 * part]

                def step(ins):
                    n[0] += 1
                    ins.then_inc(s_rt, 1)
                    return n[0]

                def after(k):
                    dve.wait_ge(s_rt, b.at(NR, k))

                L, S_, X_, EQ, CA, MK, PO, W_ = (lg[:, i, :, :] for i in range(8))
                mx, cm, se, gate, pn, en, keep, slot = (rs[:, i, :] for i in range(8))
                if part == 0:
                    dve.wait_ge(s_log, b.at(4, 4))
                    a = step(dve.tensor_tensor(L, LOW[0][:, 0:KT * E].rearrange("p (r e) -> p r e", r=KT),
                                               bc_r(rb_sb[:]), ALU.add))
                    after(a)
                    a = step(dve.tensor_reduce(mx, L, AX.X, ALU.max))
                    after(a)
                    step(dve.tensor_tensor(S_, L, bc_e(mx), ALU.subtract))
                    a = step(dve.tensor_tensor(EQ, L, bc_e(mx), ALU.is_equal))
                    after(a)
                    a = step(dve.tensor_tensor(CA, EQ, bc_r(cst[:, C_PRI:C_PRI + E]), ALU.mult))
                    after(a)
                    a = step(dve.tensor_reduce(cm, CA, AX.X, ALU.max))
                    after(a)
                    a = step(dve.tensor_tensor(MK, CA, bc_e(cm), ALU.is_equal))
                    after(a)
                    a = step(dve.tensor_reduce(cnt[:], MK.rearrange("p r e -> p e r"), AX.X, ALU.add))
                    assert a == 8
                    return
                dve.wait_ge(s_rex, b.at(1, 1))
                a = step(dve.tensor_reduce(se, X_, AX.X, ALU.add))
                after(a)
                step(dve.reciprocal(gate, se))
                dve.wait_ge(s_pre, b.at(1, 1))
                step(dve.tensor_tensor(PO[:, 0, :], LOW[1][:, 0:E], base[:], ALU.add))
                after(11)
                a = step(dve.tensor_tensor(base[:], LOW[1][:, E:2 * E], base[:], ALU.add))
                assert a == 12
                for r in range(1, KT):
                    after(a)
                    a = step(dve.tensor_tensor(PO[:, r, :], PO[:, r - 1, :], MK[:, r - 1, :], ALU.add))
                after(a)
                a = step(dve.tensor_tensor(W_, MK, PO, ALU.mult))
                after(a)
                a = step(dve.tensor_reduce(pn, W_, AX.X, ALU.add))
                after(a)
                a = step(dve.tensor_tensor(W_, MK, bc_r(cst[:, C_EOFF:C_EOFF + E]), ALU.mult))
                after(a)
                a = step(dve.tensor_reduce(en, W_, AX.X, ALU.add))
                after(a)
                step(dve.tensor_scalar(keep, pn, float(CAP), None, ALU.is_lt))
                a = step(dve.tensor_tensor(slot, pn, en, ALU.add))
                after(a)
                a = step(dve.tensor_tensor(slot, slot, trash[:], ALU.subtract))
                after(a)
                a = step(dve.tensor_tensor(slot, slot, keep, ALU.mult))
                after(a)
                dve.wait_ge(s_scat, b.at(64, N_ZERO))
                a = step(dve.tensor_tensor(slot_i[:], slot, trash[:], ALU.add))
                assert a == 24
                step(dve.tensor_scalar(du[:, :, META_TOKEN], trash[:], 1.0 - B * T, None, ALU.add))
                after(25)
                step(dve.tensor_scalar(trash[:], trash[:], float(T), None, ALU.add))
                step(dve.tensor_copy(du[:, :, META_GATE], gate))
                for r in range(KT):
                    step(dve.tensor_scalar(du[:, r, 0:D], du[:, r, 0:D], gate[:, r:r + 1], None, ALU.mult))
                assert n[0] == NR

            def mask(b, c, i):
                dve.wait_ge(s_sc, b.at(16, 4 * c + i + 1))
                if c > 0:
                    dve.wait_ge(s_pv, b.at(16, 4 * (c - 1) + i + 1))
                else:
                    wait(dve, s_pv, b.at(16, i - 3))
                dve.tensor_tensor(att[:, i, :], HIGH[i][:], decay[:, i, :, :].rearrange("p g q -> p (g q)"),
                                  ALU.mult).then_inc(s_mask, 1)

            def k_decay(b, c):
                dve.wait_ge(s_ktr, b.at(3, c + 1))
                wait(dve, s_kv, b.at(3, c))
                dve.tensor_tensor(kdec[:].rearrange("p (h n) -> p h n", n=N), LOW[2][:].rearrange("p (h n) -> p h n", n=N),
                                  kpow[:].unsqueeze(2).to_broadcast([P, H, N]), ALU.mult).then_inc(s_kdec, 1)

            def state_step(b, c):
                dve.wait_ge(s_kv, b.at(3, c + 1))
                new = st_new[:] if c else state[:, 1, :, :].rearrange("p g q -> p (g q)")
                if c == 0:
                    wait(dve, s_inter, b.at(3, 0))
                    wait(dve, s_wst, b.at(2, 0))
                dve.tensor_tensor(new.rearrange("p (g q) -> p g q", g=KT), LOW[2][:].rearrange("p (g q) -> p g q", g=KT),
                                  blk.unsqueeze(1).to_broadcast([P, KT, P]), ALU.mult).then_inc(s_st, 1)
                if c:
                    dve.wait_ge(s_st, b.at(5, 2 * c))
                    dve.wait_ge(s_wst, b.at(2, c))
                    dst = state[:, (c + 1) % 2, :, :].rearrange("p g q -> p (g q)")
                    dve.tensor_tensor(dst, st_new[:], st_old[:], ALU.add).then_inc(s_st, 1)

            def bc_n(v):
                return v.unsqueeze(2).to_broadcast([P, H, N])

            def norm_centre(b, c):
                y = LOW[c % 2][:].rearrange("p (h n) -> p h n", n=N)
                st = stat[:, c % 2]
                dve.wait_ge(s_pv, b.at(16, 4 * c + 4))
                dve.tensor_reduce(st[:, 0, :], y, AX.X, ALU.add).then_inc(s_nrm, 1)
                dve.wait_ge(s_nrm, b.at(28, 7 * c + 1))
                dve.tensor_scalar(st[:, 1, :], st[:, 0, :], -1.0 / N, None, ALU.mult).then_inc(s_nrm, 1)
                dve.wait_ge(s_nrm, b.at(28, 7 * c + 2))
                if c >= 2:
                    dve.wait_ge(s_z, b.at(8, 2 * (c - 2) + 2))
                else:
                    wait(dve, s_z, b.at(8, 2 * (c - 2) + 2))
                dve.tensor_tensor(yc[:, c % 2, :].rearrange("p (h n) -> p h n", n=N), y, bc_n(st[:, 1, :]),
                                  ALU.add).then_inc(s_nrm, 1)

            def norm_var(b, c):
                st = stat[:, c % 2]
                dve.wait_ge(s_sq, b.at(4, c + 1))
                dve.tensor_reduce(st[:, 4, :], sq[:].rearrange("p (h n) -> p h n", n=N), AX.X, ALU.add).then_inc(s_vs, 1)
                dve.wait_ge(s_vs, b.at(4, c + 1))
                dve.tensor_scalar(st[:, 2, :], st[:, 4, :], 1.0 / N, GN_EPS, ALU.mult, ALU.add).then_inc(s_nrm, 1)

            def norm_scale(b, c):
                st = stat[:, c % 2]
                ycc = yc[:, c % 2, :]
                dve.wait_ge(s_sd, b.at(4, c + 1))
                dve.reciprocal(st[:, 5, :], st[:, 3, :]).then_inc(s_nrm, 1)
                dve.wait_ge(s_nrm, b.at(28, 7 * c + 5))
                dve.tensor_tensor(ycc.rearrange("p (h n) -> p h n", n=N), ycc.rearrange("p (h n) -> p h n", n=N),
                                  bc_n(st[:, 5, :]), ALU.mult).then_inc(s_nrm, 1)
                dve.wait_ge(s_nrm, b.at(28, 7 * c + 6))
                dve.tensor_tensor(ycc, ycc, lnwb[:, 0, :], ALU.mult).then_inc(s_nrm, 1)

            def body(b):
                if (b - 2).exists():
                    dve.wait_ge(s_halo, (b - 2).at(96, 96))
                    dve.wait_ge(s_scat, (b - 2).at(64, N_ZERO))
                for p in (PK_, PR_, PG_):
                    if b.exists():
                        mixing(b, p)
                    if (b - 2).exists():
                        laplacian(b - 2, p - 1)
                if (b - 2).exists():
                    laplacian(b - 2, 3)
                if (b - 1).exists():
                    residual(b - 1)
                if (b - 2).exists():
                    router(b - 2, 0)
                if not b.exists():
                    router(b - 2, 1)
                    return
                for c in range(KT):
                    for i in range(G):
                        mask(b, c, i)
                        if i == 0 and c < KT - 1:
                            k_decay(b, c)
                        if i == 1 and c > 0:
                            norm_centre(b, c - 1)
                        if i == 2 and c > 0:
                            norm_var(b, c - 1)
                    if c < KT - 1:
                        state_step(b, c)
                    if c > 0:
                        norm_scale(b, c - 1)
                    if c == 0 and (b - 2).exists():
                        router(b - 2, 1)
                if (b + 1).exists():
                    difference(b + 1)
                    mixing(b + 1, PV_)
                norm_centre(b, KT - 1)
                norm_var(b, KT - 1)
                norm_scale(b, KT - 1)

            dve.wait_ge(s_cst2, n_cst2)
            difference(Step(0, 0))
            mixing(Step(0, 0), PV_)
            attention_bodies(dve, body)

            def tokens(t, e):
                rows = xw[:, e, :].rearrange("p (r c) -> p r c", r=KT)
                dve.wait_ge(s_ein[e], t.at(32, 32))
                wait(dve, s_add[e], t.at(64, 0))
                dve.tensor_scalar(tok_f[:, e, :], rows[:, :, META_TOKEN], 0.0, None, ALU.is_equal).then_inc(s_tok, 1)
                dve.wait_ge(s_tok, t.at(8, 4 * e + 1))
                dve.tensor_tensor(tok_f[:, e, :], tok_f[:, e, :],
                                  cst[:, C_TRASH + e * KT:C_TRASH + (e + 1) * KT], ALU.mult).then_inc(s_tok, 1)
                dve.tensor_copy(gate_e[:, e, :], rows[:, :, META_GATE]).then_inc(s_tok, 1)
                dve.wait_ge(s_tok, t.at(8, 4 * e + 3))
                dve.scalar_tensor_tensor(tok_i[:, e, :], tok_f[:, e, :], -1.0, rows[:, :, META_TOKEN], ALU.add,
                                         ALU.add).then_inc(s_tok, 1)

            def results(t, e):
                for r in range(KT):
                    dve.wait_ge(s_down, t.at(8, 4 * e + r + 1))
                    dve.tensor_tensor(kr[:, e, r, :], LOW[r][:], b2_sb[:, e, :], ALU.add).then_inc(s_b2, 1)
                for r in range(KT):
                    dve.wait_ge(s_b2, t.at(8, 4 * e + r + 1))
                    dve.tensor_scalar(kr[:, e, r, :], kr[:, e, r, :], gate_e[:, e, r:r + 1], None,
                                      ALU.mult).then_inc(s_gate, 1)

            def pair(t):
                for e in range(2):
                    tokens(t, e)
                    results(t, e)

            pair(Step(0, 0))
            with dve.Fori(0, E // 2 - 1) as i:
                pair(Step(i, 1))

        @block.gpsimd
        def _(pool):
            pool.wait_ge(s_init, 4)
            for e in range(E):
                pool.dma_start(slots[e * CAP:(e + 1) * CAP].rearrange("(p r) c -> p r c", r=KT), du[:]).then_inc(s_scat, 16)
            for e in range(2):
                at = B * T + e * CAP
                pool.dma_start(out[at:at + CAP].rearrange("(p r) c -> p r c", r=KT), du[:, :, 0:D]).then_inc(s_scat, 16)
            pool.wait_ge(s_cst2, n_cst2)
            pool.wait_ge(s_exp, 2 + H + 1 + KT + 1)

            def vertical(b, r):
                pool.wait_ge(s_halo, b.at(96, 96))
                if r >= 2:
                    pool.wait_ge(s_lap, b.at(20, 5 * (r - 2) + 5))
                pool.tensor_tensor(lv[:, r % 2, :], x1h[:, r, :], x1h[:, r + 2, :], ALU.add).then_inc(s_lv, 1)

            def r_decay(b, c):
                pool.wait_ge(s_pev, b.at(16, 12))
                if c >= 3:
                    pool.wait_ge(s_inter, b.at(3, c - 2))
                else:
                    wait(pool, s_inter, b.at(3, 0))
                pool.tensor_tensor(rdec[:, c % 2, :, :], kr[:, 1, :, c * P:(c + 1) * P], rpow[:], ALU.mult).then_inc(s_rdec, 1)

            def state_decay(b, c):
                pool.wait_ge(s_st, b.at(5, 2 * c - 1))
                pool.tensor_tensor(st_old[:].rearrange("p (g q) -> p g q", g=KT), state[:, c % 2, :, :],
                                   wpow[:].unsqueeze(2).to_broadcast([P, KT, P]), ALU.mult).then_inc(s_wst, 1)

            def z_rows(b, c):
                pool.wait_ge(s_nrm, b.at(28, 7 * c + 7))
                pool.tensor_tensor(yc[:, c % 2, :], yc[:, c % 2, :], lnwb[:, 1, :], ALU.add).then_inc(s_z, 1)
                pool.wait_ge(s_z, b.at(8, 2 * c + 1))
                pool.wait_ge(s_pev, b.at(16, 16))
                pool.tensor_tensor(g_sb[:, c, :], yc[:, c % 2, :], g_sb[:, c, :], ALU.mult).then_inc(s_z, 1)

            def scatter(b):
                pool.wait_ge(s_rt, b.at(NR, NR))
                pool.sem_inc(s_pool_on, 1)
                pool.wait_ge(s_scat, N_ZERO)
                for r in range(KT):
                    pool.indirect_dma_start(slots, bass.IndirectOffsetOnAxis(slot_i[:, r:r + 1], 0),
                                            du[:, r, :], None).then_inc(s_scat, 16)

            def body(b):
                if (b - 2).exists():
                    for r in range(KT):
                        vertical(b - 2, r)
                if b.exists():
                    r_decay(b, 1)
                    r_decay(b, 2)
                if (b - 2).exists():
                    scatter(b - 2)
                if b.exists():
                    state_decay(b, 1)
                    z_rows(b, 0)
                    r_decay(b, 3)
                    state_decay(b, 2)
                    for c in range(1, KT):
                        z_rows(b, c)

            attention_bodies(pool, body)

            def add_rows(t, e):
                pool.wait_ge(s_tok, t.at(8, 4 * e + 4))
                for r in range(KT):
                    pool.wait_ge(s_gate, t.at(8, 4 * e + r + 1))
                    pool.sem_inc(s_pool_on, 1)
                    pool.wait_ge(s_store, 16 * B)
                    pool.indirect_dma_start(out, bass.IndirectOffsetOnAxis(tok_i[:, e, r:r + 1], 0),
                                            kr[:, e, r, :], None, compute_op=ALU.add).then_inc(s_add[e], 16)

            with pool.Fori(0, E // 2) as i:
                for e in range(2):
                    add_rows(Step(i, 0), e)
            for e in range(2):
                pool.wait_ge(s_add[e], 64 * (E // 2))


def kernel(x, itok_B_0_30, condB_zX, condB_zY, condB_zR, L0_cond_weights, L0_attn_time_maa_k, L0_attn_time_maa_v,
           L0_attn_time_maa_r, L0_attn_time_maa_g, L0_attn_time_decay, L0_attn_time_faaaa, L0_attn_Wr, L0_attn_Wk,
           L0_attn_Wv, L0_attn_Wg, L0_attn_Wo, L0_attn_ln_w, L0_attn_ln_b, L0_ffn_Wr, L0_ffn_br, L0_ffn_W1,
           L0_ffn_b1, L0_ffn_W2, L0_ffn_b2):
    import concourse.bacc as bacc
    from concourse.bass_utils import run_bass_kernel_spmd

    def channels(a):
        return np.asarray(a).reshape(KT, P).T

    maas = (L0_attn_time_maa_v, L0_attn_time_maa_k, L0_attn_time_maa_r, L0_attn_time_maa_g)
    projections = (L0_attn_Wv, L0_attn_Wk, L0_attn_Wr, L0_attn_Wg)
    arrays = {
        "x": x,
        "subj": np.asarray(itok_B_0_30).reshape(1, B),
        "zxyr": np.stack([condB_zX, condB_zY, condB_zR])[None],
        "wcond": L0_cond_weights,
        "maa": np.stack([channels(a) for a in maas], axis=1),
        "wproj": np.stack([np.asarray(a).T for a in projections]),
        "wo": np.asarray(L0_attn_Wo).T,
        "decay_heads": np.asarray(L0_attn_time_decay).reshape(1, H),
        "decay_rows": np.repeat(np.asarray(L0_attn_time_decay).reshape(KT, G).T, N, axis=0),
        "bonus": np.asarray(L0_attn_time_faaaa).reshape(1, H),
        "ln_wb": np.stack([L0_attn_ln_w, L0_attn_ln_b])[None],
        "router_w": L0_ffn_Wr,
        "router_b": np.asarray(L0_ffn_br).reshape(1, E),
        "w1": L0_ffn_W1,
        "b1": np.asarray(L0_ffn_b1).reshape(E, KT, P).transpose(2, 0, 1),
        "w2": L0_ffn_W2,
        "b2": L0_ffn_b2,
        "consts": shape_constants(),
    }
    arrays = {f"in_{k}": np.ascontiguousarray(v) for k, v in arrays.items()}
    nc = bacc.Bacc("TRN2", target_bir_lowering=False, num_devices=1)
    args = [nc.dram_tensor(k, a.shape, mybir.dt.from_np(a.dtype), kind="ExternalInput").ap()
            for k, a in arrays.items()]
    out = nc.dram_tensor("out_rows", (B * T + TRASH_ROWS, D), F32, kind="ExternalOutput").ap()
    build(nc, *args, out)
    result = run_bass_kernel_spmd(nc, [arrays], core_ids=[0])
    return result.results[0]["out_rows"][:B * T].reshape(B, T, D)
```

```python
from contextlib import ExitStack

import numpy as np

import concourse.bass as bass
from concourse import mybir

F32 = mybir.dt.float32
F32R = mybir.dt.float32r
I32 = mybir.dt.int32
ACT = mybir.ActivationFunctionType
ALU = mybir.AluOpType
AX = mybir.AxisListType

P = 128
B, T, D = 8, 512, 512
KT = D // P
H, N = 16, 32
G = P // N
E = 8
CAP = B * T // E
EW = D + 4
META_GATE, META_TOKEN = D, D + 1
TRASH_ROWS = 2 * CAP
GN_EPS = 1e-5 * 64
HUGE_RATE = 1e30

PV_, PK_, PR_, PG_ = range(4)
RING = 8

C_ID, C_TRI, C_BLK, C_LAG, C_GT, C_Q = (128 * i for i in range(6))
C_TAIL = 6 * 128
C_PRI = C_TAIL + 1
C_EOFF = C_PRI + E
C_TOK = C_EOFF + E
C_TRASH = C_TOK + KT
CW = C_TRASH + 2 * KT


def shape_constants():
    p = np.arange(P)[:, None]
    q = np.arange(P)[None, :]
    r = np.arange(KT)[None, :]
    one = np.ones((P, 1))
    parts = [p == q, p < q, p // N == q // N, np.maximum(q - p - 1, 0), q > p, q + 0 * p,
             P - 1 - p, one * (E - np.arange(E)), one * (CAP * np.arange(E)), B * T + KT * p + r,
             B * T + KT * p + r + 1, B * T + CAP + KT * p + r + 1]
    out = np.concatenate([np.asarray(x, np.float32) for x in parts], axis=1)
    assert out.shape == (P, CW)
    return out


class Step:

    def __init__(self, reg, off):
        self.reg, self.off = reg, off

    def __sub__(self, k):
        return Step(self.reg, self.off - k)

    def __add__(self, k):
        return Step(self.reg, self.off + k)

    def at(self, per, k):
        return self.reg * per + (self.off * per + k)

    def exists(self):
        return not isinstance(self.reg, int) or 0 <= self.reg + self.off < B

    def index(self):
        return self.reg + self.off


def wait(eng, sem, value):
    if isinstance(value, int) and value <= 0:
        return
    eng.wait_ge(sem, value)


def build(nc, x, subj, zxyr, wcond, maa, wproj, wo, decay_heads, decay_rows, bonus, ln_wb, router_w,
          router_b, w1, b1, w2, b2, consts, out):
    slots = nc.dram_tensor("slots", (2 * B * T, EW), F32).ap()
    ctx, attention_memory, experts_memory = ExitStack(), ExitStack(), ExitStack()
    with ctx:
        def sb(name, shape, dt=F32):
            return ctx.enter_context(nc.sbuf_tensor(name, shape, dt))

        def sb_a(name, shape, dt=F32):
            return attention_memory.enter_context(nc.sbuf_tensor(name, shape, dt))

        def sb_e(name, shape, dt=F32):
            return experts_memory.enter_context(nc.sbuf_tensor(name, shape, dt))

        def sem(name):
            return ctx.enter_context(nc.semaphore(name))

        vmean = sb("vmean", [P, KT, H])
        cst = sb("cst", [P, CW])
        ones = sb("ones", [P, P])
        lnwb = sb("lnwb", [P, 2, KT])
        eps = sb("eps", [P, 1])
        blk_mean = sb("blk_mean", [P, P])
        maa_sb = sb("maa_sb", [P, 4, KT])
        rate_h = sb("rate_h", [P, 2, H])
        rate_p = sb("rate_p", [P, 2, KT])
        bonus_sb = sb("bonus_sb", [P, H])
        kpow = sb("kpow", [P, H])
        wpow = sb("wpow", [P, KT])
        zs = sb("zs", [P, 3, B])
        zq = sb("zq", [P, 2, B])
        rw_sb = sb("rw_sb", [P, KT, E])
        rb_sb = sb("rb_sb", [P, E])
        subj_sb = sb("subj_sb", [1, B], I32)
        lg = sb("lg", [P, 8, KT, E])
        rs = sb("rs", [P, 12, KT])
        cnt = sb("cnt", [P, E])
        base = sb("base", [P, E])
        trash = sb("trash", [P, KT])
        slot_i = sb("slot_i", [P, KT], I32)
        b1_sb = sb("b1_sb", [P, E, KT])
        tok_f = sb("tok_f", [P, 2, KT])
        tok_i = sb("tok_i", [P, 2, KT], I32)
        gate_e = sb("gate_e", [P, 2, KT])

        wts = sb_a("wts", [P, 5, KT, D])
        xw = sb_a("xw", [P, 2, KT * EW])
        hs = sb_a("hs", [P, KT, T + 1])
        mix = sb_a("mix", [P, RING, T])
        kr = sb_a("kr", [P, 2, KT, T])
        v_sb = sb_a("v_sb", [P, KT, D])
        decay = sb_a("decay", [P, KT, G, P])
        att = sb_a("att", [P, KT, G * P])
        rbd = sb_a("rbd", [P, 2, KT, G, P])
        rdec = sb_a("rdec", [P, 2, KT, P])
        kdec = sb_a("kdec", [P, D])
        state = sb_a("state", [P, 2, KT, P])
        st_new = kdec
        st_old = sb_a("st_old", [P, D])
        zt = sb_a("zt", [P, KT, T])
        yc = sb_a("yc", [P, 2, D])
        sq = sb_a("sq", [P, D])
        x1h = sb_a("x1h", [P, KT + 2, D])
        du = sb_a("du", [P, KT, EW])
        lh = sb_a("lh", [P, 2, D])
        lv = sb_a("lv", [P, 2, D])
        lq = sb_a("lq", [P, 2, D])
        dut = lh
        rpow = sb_a("rpow", [P, KT, P])
        attention_memory.close()

        w_raw = sb_e("w_raw", [P, 2, 2, KT, D])
        sb_e("o_weights", [P, KT, D])
        rows_sb = sb_e("rows_sb", [P, 2, KT * EW])
        w_hi = sb_e("w_hi", [P, 2, 2, KT, D], F32R)
        w_lo = sb_e("w_lo", [P, 2, 2, KT, D], F32R)
        xt_hi = sb_e("xt_hi", [P, KT, CAP], F32R)
        xt_lo = sb_e("xt_lo", [P, KT, CAP], F32R)
        ht = sb_e("ht", [P, KT, CAP])
        ht_hi = sb_e("ht_hi", [P, KT, CAP], F32R)
        ht_lo = sb_e("ht_lo", [P, KT, CAP], F32R)
        res = sb_e("res", [P, 2, KT, D])
        b2_sb = sb_e("b2_sb", [P, 2, D])
        experts_memory.close()

        bank = [ctx.enter_context(nc.psum_tensor(f"bank{i}", [P, 512], F32)) for i in range(8)]
        LOW, HIGH = bank[:4], bank[4:]

        ident = cst[:, C_ID:C_ID + P]
        tri = cst[:, C_TRI:C_TRI + P]
        blk = cst[:, C_BLK:C_BLK + P]

        s_cst = sem("s_cst")
        s_cst2 = sem("s_cst2")
        s_subj = sem("s_subj")
        s_xw = sem("s_xw")
        s_wp = [sem(f"s_wp{i}") for i in range(5)]
        s_resid = sem("s_resid")
        s_store = sem("s_store")
        s_halo = sem("s_halo")
        s_scat = sem("s_scat")
        s_init = sem("s_init")
        s_tab = sem("s_tab")
        s_exp = sem("s_exp")
        s_cond = sem("s_cond")
        s_used = sem("s_used")
        s_proj = sem("s_proj")
        s_o = sem("s_o")
        s_dtr = sem("s_dtr")
        s_log = sem("s_log")
        s_pre = sem("s_pre")
        s_sc = sem("s_sc")
        s_ktr = sem("s_ktr")
        s_kv = sem("s_kv")
        s_inter = sem("s_inter")
        s_pv = sem("s_pv")
        s_var = sem("s_var")
        s_pev = sem("s_pev")
        s_hev = sem("s_hev")
        s_dev = sem("s_dev")
        s_sq = sem("s_sq")
        s_sd = sem("s_sd")
        s_aff = sem("s_aff")
        s_lq = sem("s_lq")
        s_rex = sem("s_rex")
        s_diff = sem("s_diff")
        s_mix = sem("s_mix")
        s_mask = sem("s_mask")
        s_kdec = sem("s_kdec")
        s_st = sem("s_st")
        s_nrm = sem("s_nrm")
        s_wv = sem("s_wv")
        s_x1 = sem("s_x1")
        s_lap = sem("s_lap")
        NR = 31
        s_rt = sem("s_rt")
        s_rdec = sem("s_rdec")
        s_wst = sem("s_wst")
        s_rbd = sem("s_rbd")
        s_z = sem("s_z")
        s_lv = sem("s_lv")
        s_act_on = sem("s_act_on")
        s_pool_on = sem("s_pool_on")
        s_we = [sem(f"s_we{i}") for i in range(2)]
        s_ein = [sem(f"s_ein{i}") for i in range(2)]
        s_add = [sem(f"s_add{i}") for i in range(2)]
        s_whi = sem("s_whi")
        s_wlo = sem("s_wlo")
        s_etr = sem("s_etr")
        s_xhi = sem("s_xhi")
        s_xlo = sem("s_xlo")
        s_up = sem("s_up")
        s_relu = sem("s_relu")
        s_hlo = sem("s_hlo")
        s_down = sem("s_down")
        s_b2 = sem("s_b2")
        s_gate = sem("s_gate")
        s_tok = sem("s_tok")

        block = ctx.enter_context(nc.Block())

        N_ZERO = 16 * (E + 2)
        N_TAB = 2 + 2 * H + 3
        n_cst, n_cst2 = 6 * 16, 5 * 16

        def used_wait(eng, b, p, tt):
            if tt < KT - 1:
                wait(eng, s_used, b.at(12, 3 * p + tt + 1))
            else:
                wait(eng, s_proj, b.at(16, 4 * p + 4))

        def attention_bodies(eng, body):
            for b in range(2):
                body(Step(0, b))
            with eng.Fori(0, B - 3) as i:
                body(Step(i, 2))
            for b in range(B - 1, B + 2):
                body(Step(0, b))

        def load_weights(sp, t, e):
            n = t.index() * 2 + e
            sp.dma_start(w_raw[:, e, 0, :, :],
                         w1[bass.ds(n, 1)].rearrange("a (k p) f -> p (a k) f", p=P)).then_inc(s_we[e], 16)
            sp.dma_start(w_raw[:, e, 1, :, :],
                         w2[bass.ds(n, 1)].rearrange("a (k p) f -> p (a k) f", p=P)).then_inc(s_we[e], 16)

        def load_rows(sp, t, e):
            n = t.index() * 2 + e
            sp.dma_start(rows_sb[:, e, :],
                         slots[bass.ds(n * CAP, CAP)].rearrange("(p r) c -> p (r c)", r=KT)).then_inc(s_ein[e], 16)
            sp.dma_start(b2_sb[:, e, :], b2[bass.ds(n, 1)].to_broadcast([P, D])).then_inc(s_ein[e], 16)

        @block.sync
        def _(sp):
            sp.dma_start(subj_sb[:], subj).then_inc(s_subj, 16)
            sp.dma_start(cst[:], consts).then_inc(s_cst, 16)
            sp.dma_start(rate_h[:, 1, :], decay_heads.to_broadcast([P, H])).then_inc(s_cst, 16)
            sp.dma_start(rate_p[:, 1, :], decay_rows).then_inc(s_cst, 16)
            sp.dma_start(bonus_sb[:], bonus.to_broadcast([P, H])).then_inc(s_cst, 16)
            sp.dma_start(maa_sb[:], maa).then_inc(s_cst, 16)
            sp.dma_start(zs[:], zxyr.to_broadcast([P, 3, B])).then_inc(s_cst, 16)
            sp.wait_ge(s_subj, 16)

            def load_xw(b):
                s = sp.value_load(subj_sb[0:1, bass.ds(b.index(), 1)], min_val=0, max_val=wcond.shape[0] - 1)
                sp.dma_start(xw[:, 0, 0:KT * T],
                             x[bass.ds(b.index(), 1)].rearrange("a (p r) t -> (a p) (r t)", r=KT)).then_inc(s_xw, 16)
                sp.dma_start(xw[:, 1, 0:KT * T],
                             wcond[bass.ds(s, 1)].rearrange("a (p r) t -> (a p) (r t)", r=KT)).then_inc(s_xw, 16)

            load_xw(Step(0, 0))
            sp.dma_start(lnwb[:], ln_wb).then_inc(s_cst2, 16)
            sp.dma_start(rw_sb[:], router_w.rearrange("(k p) e -> p k e", p=P)).then_inc(s_cst2, 16)
            sp.dma_start(rb_sb[:], router_b.to_broadcast([P, E])).then_inc(s_cst2, 16)
            sp.dma_start(b1_sb[:], b1).then_inc(s_cst2, 16)
            sp.dma_start(trash[:], consts[:, C_TOK:C_TOK + KT]).then_inc(s_cst2, 16)
            for p in range(5):
                src = wproj[p] if p < 4 else wo
                sp.dma_start(wts[:, p, :, :], src.rearrange("(k p) o -> p k o", p=P)).then_inc(s_wp[p], 16)
            sp.wait_ge(s_cond, 4)
            load_xw(Step(0, 1))

            def body(b):
                if (b - 1).exists():
                    wait(sp, s_lap, (b - 2).at(20, 20))
                    wait(sp, s_lv, (b - 2).at(4, 4))
                    wait(sp, s_lq, (b - 2).at(4, 4))
                    wait(sp, s_store, (b - 2).at(16, 16))
                    sp.dma_start(x1h[:, 1:KT + 1, :],
                                 x[bass.ds((b - 1).index(), 1)].rearrange("a (p r) t -> (a p) r t", r=KT)
                                 ).then_inc(s_resid, 16)
                    sp.wait_ge(s_x1, (b - 1).at(4, 4))
                    sp.dma_start(out[bass.ds((b - 1).index() * T, T)].rearrange("(p r) t -> p r t", r=KT),
                                 x1h[:, 1:KT + 1, :]).then_inc(s_store, 16)
                    for lo, hi in ((1, 113), (113, P)):
                        sp.dma_start(x1h[lo:hi, 0, :], x1h[lo - 1:hi - 1, KT, :]).then_inc(s_halo, 16)
                    for lo, hi in ((0, 112), (112, P - 1)):
                        sp.dma_start(x1h[lo:hi, KT + 1, :], x1h[lo + 1:hi + 1, 1, :]).then_inc(s_halo, 16)
                    sp.dma_start(x1h[0:1, 0, :], x1h[0:1, 2, :]).then_inc(s_halo, 16)
                    sp.dma_start(x1h[P - 1:P, KT + 1, :], x1h[P - 1:P, KT - 1, :]).then_inc(s_halo, 16)
                if (b + 2).exists():
                    sp.wait_ge(s_cond, (b + 1).at(4, 4))
                    load_xw(b + 2)

            for b in range(2):
                body(Step(0, b))
            with sp.Fori(0, B - 4) as i:
                body(Step(i, 2))
            for b in range(B - 2, B + 2):
                if b == B:
                    sp.wait_ge(s_proj, 16 * B)
                    for e in range(2):
                        load_weights(sp, Step(0, 0), e)
                body(Step(0, b))

            sp.wait_ge(s_scat, 64 * B + N_ZERO)
            for e in range(2):
                load_rows(sp, Step(0, 0), e)
            with sp.Fori(0, E // 2 - 1) as i:
                for e in range(2):
                    sp.wait_ge(s_wlo, Step(i, 0).at(4, 2 * e + 2))
                    load_weights(sp, Step(i, 1), e)
                for e in range(2):
                    sp.wait_ge(s_etr, Step(i, 0).at(8, 4 * e + 4))
                    sp.wait_ge(s_tok, Step(i, 0).at(8, 4 * e + 4))
                    sp.wait_ge(s_b2, Step(i, 0).at(8, 4 * e + 4))
                    load_rows(sp, Step(i, 1), e)
            sp.wait_ge(s_store, 16 * B)

        @block.tensor
        def _(pe):
            def cond_tile(b, m, dst):
                xv = xw[:, 0, 0:KT * T].rearrange("p (r t) -> p r t", r=KT)
                wv = xw[:, 1, 0:KT * T].rearrange("p (r t) -> p r t", r=KT)
                if m == 0:
                    pe.wait_ge(s_xw, b.at(32, 32))
                for r in range(KT):
                    last = pe.matmul(dst[:], xv[:, r, m * P:(m + 1) * P], wv[:, r, :], start=r == 0, stop=r == KT - 1)
                last.then_inc(s_cond, 1)

            def project(b, p, banks, free):
                wait(pe, s_wp[p], 16)
                if p == PV_:
                    pe.wait_ge(s_wv, 3)
                for tt in range(KT):
                    pe.wait_ge(s_mix, b.at(16, 4 * p + tt + 1))
                    mx = mix[:, (4 * p + tt) % RING, :]
                    for m in range(KT):
                        if tt == 0:
                            free(m)
                        if p == PV_:
                            lhs, rhs = mx[:, m * P:(m + 1) * P], wts[:, p, tt, :]
                        else:
                            lhs, rhs = wts[:, p, tt, m * P:(m + 1) * P], mx
                        ins = pe.matmul(banks[m][:], lhs, rhs, start=tt == 0, stop=tt == KT - 1)
                        if tt == KT - 1:
                            ins.then_inc(s_proj, 1)
                    if tt < KT - 1:
                        ins.then_inc(s_used, 1)

            def output_product(b):
                pe.wait_ge(s_wp[4], 16)
                pe.wait_ge(s_z, b.at(4, 4))
                for r in range(KT):
                    nxt = b + 1
                    if nxt.exists():
                        pe.wait_ge(s_pev, nxt.at(16, 4 * PR_ + r + 1))
                    else:
                        wait(pe, s_sd, b.at(4, 4))
                        wait(pe, s_st, b.at(5, 5))
                    for k in range(KT):
                        last = pe.matmul(LOW[r][:], zt[:, k, r * P:(r + 1) * P], wts[:, 4, k, :],
                                         start=k == 0, stop=k == KT - 1)
                    last.then_inc(s_o, 1)

            def logits(b):
                for k in range(KT):
                    if (b + 2).exists():
                        wait(pe, s_pev, (b + 2).at(16, 4 * PG_ + k + 1))
                    elif (b + 1).exists():
                        pe.wait_ge(s_mask, (b + 1).at(16, 16))
                    else:
                        pe.wait_ge(s_dev, (b - 1).at(4, k + 1))
                    if k == 0:
                        pe.wait_ge(s_lap, b.at(20, 20))
                    for r in range(KT):
                        last = pe.transpose(HIGH[k][:, r * P:(r + 1) * P], du[:, r, k * P:(k + 1) * P], ident)
                    last.then_inc(s_dtr, 1)
                if (b + 1).exists():
                    pe.wait_ge(s_x1, (b + 1).at(4, 1))
                else:
                    pe.wait_ge(s_rt, (b - 1).at(NR, 12))
                pe.wait_ge(s_cst2, n_cst2)
                for k in range(KT):
                    pe.wait_ge(s_dev, b.at(4, k + 1))
                    for r in range(KT):
                        last = pe.matmul(LOW[0][:, r * E:(r + 1) * E], dut[:, k % 2, r * P:(r + 1) * P],
                                         rw_sb[:, k, :], start=k == 0 and r == 0, stop=k == KT - 1,
                                         skip_group_check=True)
                    last.then_inc(s_log, 1)

            def prefix(b):
                pe.wait_ge(s_rt, b.at(NR, 8))
                if (b + 1).exists():
                    pe.wait_ge(s_x1, (b + 1).at(4, 2))
                pe.matmul(LOW[1][:, 0:E], tri, cnt[:], start=True, stop=False, skip_group_check=True)
                pe.matmul(LOW[1][:, E:2 * E], ones[:], cnt[:], start=False, stop=True,
                          skip_group_check=True).then_inc(s_pre, 1)

            def scores(b, c):
                for g in range(KT):
                    if c > 0:
                        pe.wait_ge(s_mask, b.at(16, 4 * (c - 1) + g + 1))
                    elif (b - 2).exists():
                        pe.wait_ge(s_dev, (b - 2).at(4, g + 1))
                    else:
                        pe.wait_ge(s_pev, b.at(16, 4 * PG_ + g + 1))
                    if g == 0:
                        pe.wait_ge(s_rbd, b.at(16, 4 * c + 4))
                    pe.matmul(HIGH[g][:], kr[:, 0, g, c * P:(c + 1) * P],
                              rbd[:, c % 2, g, :, :].rearrange("p i q -> p (i q)"), start=True,
                              stop=True).then_inc(s_sc, 1)

            def bank_of_state(b, c):
                if c > 0:
                    wait(pe, s_st, b.at(5, (1, 2)[c - 1]))
                elif (b - 1).exists():
                    pe.wait_ge(s_x1, (b - 1).at(4, 3))
                else:
                    pe.wait_ge(s_pev, b.at(16, 4 * PR_ + 3))

            def k_transpose(b, c):
                bank_of_state(b, c)
                for g in range(KT):
                    last = pe.transpose(LOW[2][:, g * P:(g + 1) * P], kr[:, 0, g, c * P:(c + 1) * P], ident)
                last.then_inc(s_ktr, 1)

            def state_product(b, c):
                pe.wait_ge(s_kdec, b.at(3, c + 1))
                for g in range(KT):
                    last = pe.matmul(LOW[2][:, g * P:(g + 1) * P], kdec[:, g * P:(g + 1) * P],
                                     v_sb[:, c, g * P:(g + 1) * P], start=True, stop=True)
                last.then_inc(s_kv, 1)

            def bank_of_y(b, c):
                if c >= 2:
                    pe.wait_ge(s_sd, b.at(4, c - 1))
                elif (b - 2).exists():
                    pe.wait_ge(s_rt, (b - 2).at(NR, 1 if c == 0 else 12))
                elif (b - 1).exists():
                    pe.wait_ge(s_x1, (b - 1).at(4, c + 1))
                else:
                    pe.wait_ge(s_pev, b.at(16, 4 * PR_ + c + 1))

            def from_state(b, c):
                bank_of_y(b, c)
                pe.wait_ge(s_st, b.at(5, (1, 3, 5)[c - 1]))
                pe.wait_ge(s_rdec, b.at(3, c))
                for g in range(KT):
                    last = pe.matmul(LOW[c % 2][:, g * P:(g + 1) * P], state[:, c % 2, g, :], rdec[:, c % 2, g, :],
                                     start=g == 0, stop=False, skip_group_check=True)
                last.then_inc(s_inter, 1)

            def from_scores(b, c):
                if c == 0:
                    bank_of_y(b, 0)
                for g in range(KT):
                    pe.wait_ge(s_mask, b.at(16, 4 * c + g + 1))
                    for i in range(G):
                        h0 = g * P + i * N
                        last = pe.matmul(LOW[c % 2][i * N:(i + 1) * N, g * P:(g + 1) * P], v_sb[:, c, h0:h0 + N],
                                         att[:, g, i * P:(i + 1) * P], start=c == 0 and g == 0,
                                         stop=g == KT - 1, skip_group_check=True)
                    last.then_inc(s_pv, 1)

            def variance(b, c):
                pe.wait_ge(s_sq, b.at(8, 2 * c + 2))
                pe.matmul(LOW[c % 2][:], blk_mean[:], sq[:], start=True, stop=True).then_inc(s_var, 1)

            def cond_bank(b, m):
                if m > 0:
                    pe.wait_ge(s_hev, (b + 1).at(4, m))
                elif (b - 1).exists():
                    pe.wait_ge(s_x1, (b - 1).at(4, 4))
                else:
                    pe.wait_ge(s_pev, b.at(16, 4 * PR_ + 4))

            def body(b):
                if b.exists():
                    def free_v(m):
                        wait(pe, s_mask, b.at(16, 0))

                    def free_k(m):
                        if not (b - 1).exists():
                            if m == 0:
                                pe.wait_ge(s_hev, 4)
                        elif m < 2:
                            pe.wait_ge(s_sd, (b - 1).at(4, m + 3))
                        elif m == 2:
                            pe.wait_ge(s_st, (b - 1).at(5, 5))
                        else:
                            pe.wait_ge(s_hev, b.at(4, 4))

                    def free_r(m):
                        pe.wait_ge(s_pev, b.at(16, 4 * PK_ + m + 1))

                    def free_g(m):
                        pe.wait_ge(s_pev, b.at(16, m + 1))

                    project(b, PV_, HIGH, free_v)
                if (b - 1).exists():
                    variance(b - 1, KT - 1)
                if b.exists():
                    project(b, PK_, LOW, free_k)
                    project(b, PR_, LOW, free_r)
                if (b - 1).exists():
                    output_product(b - 1)
                if b.exists():
                    project(b, PG_, HIGH, free_g)
                if (b - 2).exists():
                    logits(b - 2)
                if not b.exists():
                    if (b - 2).exists():
                        prefix(b - 2)
                    return
                for c in range(KT):
                    scores(b, c)
                    if c < KT - 1:
                        k_transpose(b, c)
                    if c > 0:
                        from_scores(b, c - 1)
                    elif (b - 2).exists():
                        prefix(b - 2)
                    if (b + 1).exists():
                        cond_bank(b, c)
                        cond_tile(b + 1, c, LOW[3])
                    if c > 0:
                        variance(b, c - 1)
                    if c < KT - 1:
                        state_product(b, c)
                    if c > 0:
                        from_state(b, c)
                from_scores(b, KT - 1)

            for m in range(KT):
                if m == 0:
                    pe.wait_ge(s_cst, n_cst)
                    pe.wait_ge(s_init, 2)
                cond_tile(Step(0, 0), m, LOW[m])
            attention_bodies(pe, body)

            def split_product(dst, lhs_hi, lhs_lo, rhs_hi, rhs_lo, start, stop):
                pe.matmul(dst, lhs_hi, rhs_hi, start=start, stop=False)
                pe.matmul(dst, lhs_hi, rhs_lo, start=False, stop=False)
                return pe.matmul(dst, lhs_lo, rhs_hi, start=False, stop=stop)

            def e_transpose(t, e, first):
                pe.wait_ge(s_ein[e], t.at(32, 32))
                rows = rows_sb[:, e, :].rearrange("p (r c) -> p r c", r=KT)
                for k in range(KT):
                    if not first:
                        pe.wait_ge(s_relu, t.at(16, 8 * (e - 1) + 2 * k + 2))
                    for r in range(KT):
                        last = pe.transpose(LOW[k][:, r * P:(r + 1) * P], rows[:, r, k * P:(k + 1) * P], ident)
                    last.then_inc(s_etr, 1)

            def e_up(t, e):
                pe.wait_ge(s_wlo, t.at(4, 2 * e + 1))
                pe.wait_ge(s_xlo, t.at(8, 4 * e + 4))
                for k in range(KT):
                    for m in range(KT):
                        ins = split_product(LOW[m][:], w_hi[:, e, 0, k, m * P:(m + 1) * P],
                                            w_lo[:, e, 0, k, m * P:(m + 1) * P], xt_hi[:, k, :], xt_lo[:, k, :],
                                            k == 0, k == KT - 1)
                        if k == KT - 1:
                            ins.then_inc(s_up, 1)

            def e_down(t, e, part, first):
                if part == 0:
                    pe.wait_ge(s_wlo, t.at(4, 2 * e + 2))
                for m in (2 * part, 2 * part + 1):
                    pe.wait_ge(s_hlo, t.at(8, 4 * e + m + 1))
                    for r in range(KT):
                        if m == 0 and not first:
                            pe.wait_ge(s_b2, t.at(8, 4 * (e - 1) + r + 1))
                        ins = split_product(HIGH[r][:], ht_hi[:, m, r * P:(r + 1) * P],
                                            ht_lo[:, m, r * P:(r + 1) * P], w_hi[:, e, 1, m, :], w_lo[:, e, 1, m, :],
                                            m == 0, m == KT - 1)
                        if m == KT - 1:
                            ins.then_inc(s_down, 1)

            def pair(t, first, last):
                e_up(t, 0)
                e_down(t, 0, 0, first)
                e_transpose(t, 1, False)
                e_down(t, 0, 1, first)
                e_up(t, 1)
                e_down(t, 1, 0, False)
                if not last:
                    e_transpose(t + 1, 0, False)
                e_down(t, 1, 1, False)

            pe.wait_ge(s_dev, 4 * B)
            pe.wait_ge(s_rt, NR * B)
            e_transpose(Step(0, 0), 0, True)
            pair(Step(0, 0), True, False)
            with pe.Fori(0, E // 2 - 2) as i:
                pair(Step(i, 1), False, False)
            pair(Step(0, E // 2 - 1), False, True)

        @block.scalar
        def _(act):
            act.wait_ge(s_cst, n_cst)
            act.activation(rate_h[:, 0, :], rate_h[:, 1, :], ACT.Exp).then_inc(s_exp, 1)
            act.activation(rate_p[:, 0, :], rate_p[:, 1, :], ACT.Exp).then_inc(s_exp, 1)
            act.wait_ge(s_tab, 2)
            for h in range(H):
                act.activation(decay[:, h // G, h % G, :], cst[:, C_LAG:C_LAG + P], ACT.Exp,
                               scale=rate_h[:, 1, h:h + 1]).then_inc(s_exp, 1)
            act.activation(kpow[:], rate_h[:, 1, :], ACT.Exp, scale=cst[:, C_TAIL:C_TAIL + 1]).then_inc(s_exp, 1)
            for g in range(KT):
                act.activation(rpow[:, g, :], cst[:, C_Q:C_Q + P], ACT.Exp,
                               scale=rate_p[:, 1, g:g + 1]).then_inc(s_exp, 1)
            act.activation(wpow[:], rate_p[:, 1, :], ACT.Exp, scale=float(P)).then_inc(s_exp, 1)

            def h_evac(b, m, src):
                if m == 0:
                    wait(act, s_mix, (b - 1).at(16, 16))
                act.wait_ge(s_cond, b.at(4, m + 1))
                act.activation(hs[:, m, 1:T + 1], src[:], ACT.Copy).then_inc(s_hev, 1)

            def w_high(t, e, w):
                if w == 0:
                    act.wait_ge(s_we[e], t.at(32, 32))
                act.activation(w_hi[:, e, w, :, :], w_raw[:, e, w, :, :], ACT.Copy).then_inc(s_whi, 1)

            act.wait_ge(s_init, 2)
            for m in range(KT):
                h_evac(Step(0, 0), m, LOW[m])

            def proj_evac(b, p, banks):
                for m in range(KT):
                    act.wait_ge(s_proj, b.at(16, 4 * p + m + 1))
                    if m == 0:
                        if p == PV_:
                            wait(act, s_pv, b.at(16, 0))
                        if p == PR_:
                            wait(act, s_rbd, b.at(16, 0))
                        if p == PG_:
                            wait(act, s_o, b.at(4, 0))
                    if p == PG_:
                        act.activation(zt[:, m, :].rearrange("p (r q) -> p r q", r=KT),
                                       banks[m][:].rearrange("p (q r) -> p r q", r=KT), ACT.Gelu).then_inc(s_pev, 1)
                    else:
                        o = v_sb[:, m, :] if p == PV_ else kr[:, p - PK_, m, :]
                        act.activation(o, banks[m][:], ACT.Copy).then_inc(s_pev, 1)

            def lap_factor(b, r):
                if r == 0:
                    act.wait_ge(s_x1, b.at(4, 4))
                if r >= 2:
                    act.wait_ge(s_lap, b.at(20, 5 * (r - 2) + 5))
                act.sem_inc(s_act_on, 1)
                act.wait_ge(s_tab, N_TAB)
                act.activation(lq[:, r % 2, :], x1h[:, r + 1, :], ACT.Identity, bias=zq[:, 1, bass.ds(b.index(), 1)],
                               scale=zq[:, 0, bass.ds(b.index(), 1)]).then_inc(s_lq, 1)

            def du_evac(b):
                for k in range(KT):
                    act.wait_ge(s_dtr, b.at(4, k + 1))
                    if k >= 2:
                        act.wait_ge(s_log, b.at(4, k - 1))
                    act.activation(dut[:, k % 2, :], HIGH[k][:], ACT.Copy).then_inc(s_dev, 1)

            def body(b):
                if b.exists():
                    proj_evac(b, PV_, HIGH)
                if (b - 1).exists():
                    deviation(b - 1, KT - 1)
                if not b.exists() and (b - 1).exists():
                    act.wait_ge(s_pv, 16 * B)
                    for e in range(2):
                        for w in range(2):
                            w_high(Step(0, 0), e, w)
                if (b - 2).exists():
                    lap_factor(b - 2, 0)
                    lap_factor(b - 2, 1)
                if b.exists():
                    proj_evac(b, PK_, LOW)
                if (b - 2).exists():
                    lap_factor(b - 2, 2)
                    lap_factor(b - 2, 3)
                if b.exists():
                    proj_evac(b, PR_, LOW)
                    proj_evac(b, PG_, HIGH)
                if (b - 2).exists():
                    du_evac(b - 2)
                    act.wait_ge(s_rt, (b - 2).at(NR, 3))
                    act.activation(lg[:, 2, :, :], lg[:, 1, :, :], ACT.Exp).then_inc(s_rex, 1)
                if b.exists():
                    for c in range(KT + 1):
                        if c > 0:
                            squares(b, c - 1)
                        if c < KT and (b + 1).exists():
                            h_evac(b + 1, c, LOW[3])
                        if 0 < c < KT:
                            deviation(b, c - 1)

            def squares(b, c):
                act.wait_ge(s_pv, b.at(16, 4 * c + 4))
                if c >= 2:
                    act.wait_ge(s_z, b.at(4, c - 1))
                else:
                    wait(act, s_z, b.at(4, c - 2 + 1))
                act.activation(yc[:, c % 2, :], LOW[c % 2][:], ACT.Copy).then_inc(s_sq, 1)
                wait(act, s_nrm, b.at(8, 2 * c))
                act.activation(sq[:], LOW[c % 2][:], ACT.Square).then_inc(s_sq, 1)

            def deviation(b, c):
                act.wait_ge(s_var, b.at(4, c + 1))
                act.activation(sq[:], LOW[c % 2][:], ACT.Sqrt, bias=eps[:]).then_inc(s_sd, 1)
                act.wait_ge(s_nrm, b.at(8, 2 * c + 2))
                for g in range(KT):
                    y = yc[:, c % 2, g * P:(g + 1) * P]
                    act.activation(y, y, ACT.Identity, bias=lnwb[:, 1, g:g + 1], scale=lnwb[:, 0, g:g + 1]).then_inc(s_aff, 1)

            attention_bodies(act, body)

            def e_evac(t, e):
                for k in range(KT):
                    act.wait_ge(s_etr, t.at(8, 4 * e + k + 1))
                    act.activation(xt_hi[:, k, :], LOW[k][:], ACT.Copy).then_inc(s_xhi, 1)

            def e_relu(t, e, first):
                for m in range(KT):
                    act.wait_ge(s_up, t.at(8, 4 * e + m + 1))
                    if m == 0 and not first:
                        act.wait_ge(s_down, t.at(8, 4 * e))
                    act.sem_inc(s_act_on, 1)
                    act.wait_ge(s_cst2, n_cst2)
                    b1_col = b1_sb[:, bass.ds(t.index() * 2 + e, 1), m]
                    act.activation(ht[:, m, :], LOW[m][:], ACT.Relu, bias=b1_col).then_inc(s_relu, 1)
                    act.activation(ht_hi[:, m, :], LOW[m][:], ACT.Relu, bias=b1_col).then_inc(s_relu, 1)

            def pair(t, last):
                for e in range(2):
                    e_relu(t, e, isinstance(t.reg, int) and t.off == 0 and e == 0)
                    if not last:
                        act.wait_ge(s_up, t.at(8, 4 * e + 4))
                        w_high(t + 1, e, 0)
                    if e == 0:
                        e_evac(t, 1)
                    elif not last:
                        e_evac(t + 1, 0)
                    if not last:
                        act.wait_ge(s_down, t.at(8, 4 * e + 4))
                        w_high(t + 1, e, 1)

            e_evac(Step(0, 0), 0)
            pair(Step(0, 0), False)
            with act.Fori(0, E // 2 - 2) as i:
                pair(Step(i, 1), False)
            pair(Step(0, E // 2 - 1), True)

        @block.vector
        def _(dve):
            dve.memset(hs[:, :, 0:1], 0.0).then_inc(s_init, 1)
            dve.memset(ones[:], 1.0).then_inc(s_init, 1)
            dve.memset(base[:], 1.0).then_inc(s_init, 1)
            dve.memset(du[:], 0.0).then_inc(s_init, 1)
            dve.memset(eps[:], GN_EPS).then_inc(s_init, 1)
            dve.memset(rbd[:], 0.0).then_inc(s_init, 1)
            dve.wait_ge(s_cst, n_cst)
            dve.tensor_scalar(blk_mean[:], blk, 1.0 / N, None, ALU.mult).then_inc(s_init, 1)
            dve.wait_ge(s_exp, 2)
            dve.tensor_scalar(rate_h[:, 1, :], rate_h[:, 0, :], HUGE_RATE, -1.0, ALU.min, ALU.mult).then_inc(s_tab, 1)
            dve.tensor_scalar(rate_p[:, 1, :], rate_p[:, 0, :], HUGE_RATE, -1.0, ALU.min, ALU.mult).then_inc(s_tab, 1)
            for h in range(H):
                d = decay[:, h // G, h % G, :]
                dve.wait_ge(s_exp, 2 + h + 1)
                dve.tensor_tensor(d, d, cst[:, C_GT:C_GT + P], ALU.mult).then_inc(s_tab, 1)
            for h in range(H):
                d = decay[:, h // G, h % G, :]
                dve.wait_ge(s_tab, 2 + h + 1)
                dve.scalar_tensor_tensor(d, ident, bonus_sb[:, h:h + 1], d, ALU.mult, ALU.add).then_inc(s_tab, 1)
            n_tab = N_TAB - 3
            dve.tensor_scalar(zq[:, 0, :], zs[:, 2, :], -1.0, None, ALU.mult).then_inc(s_tab, 1)
            dve.tensor_tensor(zq[:, 1, :], zs[:, 0, :], zs[:, 1, :], ALU.add).then_inc(s_tab, 1)
            dve.wait_ge(s_tab, n_tab + 2)
            dve.scalar_tensor_tensor(zq[:, 1, :], zq[:, 1, :], -2.0, zs[:, 2, :], ALU.mult, ALU.add).then_inc(s_tab, 1)

            def mixing(b, p):
                for tt in range(KT):
                    j = 4 * p + tt - RING
                    m = mix[:, (4 * p + tt) % RING, :]
                    if p == PV_:
                        dve.wait_ge(s_hev, b.at(4, tt + 1))
                    used_wait(dve, b if j >= 0 else b - 1, (j % 16) // 4, j % 4)
                    dve.tensor_tensor(m, hs[:, tt, 0:T], hs[:, tt, 1:T + 1], ALU.subtract).then_inc(s_diff, 1)
                    dve.wait_ge(s_diff, b.at(16, 4 * p + tt + 1))
                    dve.scalar_tensor_tensor(m, m, maa_sb[:, p, tt:tt + 1], hs[:, tt, 1:T + 1],
                                             ALU.mult, ALU.add).then_inc(s_mix, 1)

            def laplacian(b, r):
                y = x1h[:, r + 1, :]
                s = b.index()
                lhr, lvr, lqr = lh[:, r % 2, :], lv[:, r % 2, :], lq[:, r % 2, :]
                dve.tensor_tensor(lhr[:, 1:D - 1], y[:, 0:D - 2], y[:, 2:D], ALU.add).then_inc(s_lap, 1)
                dve.tensor_scalar(lhr[:, 0:D:D - 1], y[:, 1:D - 1:D - 3], 2.0, None, ALU.mult).then_inc(s_lap, 1)
                dve.wait_ge(s_lq, b.at(4, r + 1))
                dve.tensor_tensor(lqr, lqr, y, ALU.mult).then_inc(s_lap, 1)
                dve.wait_ge(s_lap, b.at(20, 5 * r + 3))
                dve.scalar_tensor_tensor(lqr, lhr, zs[:, 0, bass.ds(s, 1)], lqr, ALU.mult, ALU.add).then_inc(s_lap, 1)
                dve.wait_ge(s_lap, b.at(20, 5 * r + 4))
                dve.wait_ge(s_lv, b.at(4, r + 1))
                dve.scalar_tensor_tensor(du[:, r, 0:D], lvr, zs[:, 1, bass.ds(s, 1)], lqr, ALU.mult,
                                         ALU.add).then_inc(s_lap, 1)

            def residual(b):
                dve.wait_ge(s_resid, b.at(16, 16))
                for r in range(KT):
                    dve.wait_ge(s_o, b.at(4, r + 1))
                    dve.tensor_tensor(x1h[:, r + 1, :], LOW[r][:], x1h[:, r + 1, :], ALU.add).then_inc(s_x1, 1)

            def bc_e(v):
                return v.unsqueeze(2).to_broadcast([P, KT, E])

            def bc_r(v):
                return v.unsqueeze(1).to_broadcast([P, KT, E])

            def router(b, part):
                n = [8 * part]

                def step(ins):
                    n[0] += 1
                    ins.then_inc(s_rt, 1)
                    return n[0]

                def after(k):
                    dve.wait_ge(s_rt, b.at(NR, k))

                L, S_, X_, EQ, CA, MK, PO, W_ = (lg[:, i, :, :] for i in range(8))
                mx, cm, se, gate, pn, en, keep, slot = (rs[:, i, :] for i in range(8))
                if part == 0:
                    dve.wait_ge(s_log, b.at(4, 4))
                    a = step(dve.tensor_tensor(L, LOW[0][:, 0:KT * E].rearrange("p (r e) -> p r e", r=KT),
                                               bc_r(rb_sb[:]), ALU.add))
                    after(a)
                    a = step(dve.tensor_reduce(mx, L, AX.X, ALU.max))
                    after(a)
                    step(dve.tensor_tensor(S_, L, bc_e(mx), ALU.subtract))
                    a = step(dve.tensor_tensor(EQ, L, bc_e(mx), ALU.is_equal))
                    after(a)
                    a = step(dve.tensor_tensor(CA, EQ, bc_r(cst[:, C_PRI:C_PRI + E]), ALU.mult))
                    after(a)
                    a = step(dve.tensor_reduce(cm, CA, AX.X, ALU.max))
                    after(a)
                    a = step(dve.tensor_tensor(MK, CA, bc_e(cm), ALU.is_equal))
                    after(a)
                    a = step(dve.tensor_reduce(cnt[:], MK.rearrange("p r e -> p e r"), AX.X, ALU.add))
                    assert a == 8
                    return
                dve.wait_ge(s_rex, b.at(1, 1))
                a = step(dve.tensor_reduce(se, X_, AX.X, ALU.add))
                after(a)
                step(dve.reciprocal(gate, se))
                dve.wait_ge(s_pre, b.at(1, 1))
                step(dve.tensor_tensor(PO[:, 0, :], LOW[1][:, 0:E], base[:], ALU.add))
                after(11)
                a = step(dve.tensor_tensor(base[:], LOW[1][:, E:2 * E], base[:], ALU.add))
                assert a == 12
                for r in range(1, KT):
                    after(a)
                    a = step(dve.tensor_tensor(PO[:, r, :], PO[:, r - 1, :], MK[:, r - 1, :], ALU.add))
                after(a)
                a = step(dve.tensor_tensor(W_, MK, PO, ALU.mult))
                after(a)
                a = step(dve.tensor_reduce(pn, W_, AX.X, ALU.add))
                after(a)
                a = step(dve.tensor_tensor(W_, MK, bc_r(cst[:, C_EOFF:C_EOFF + E]), ALU.mult))
                after(a)
                a = step(dve.tensor_reduce(en, W_, AX.X, ALU.add))
                after(a)
                step(dve.tensor_scalar(keep, pn, float(CAP), None, ALU.is_lt))
                a = step(dve.tensor_tensor(slot, pn, en, ALU.add))
                after(a)
                a = step(dve.tensor_tensor(slot, slot, trash[:], ALU.subtract))
                after(a)
                a = step(dve.tensor_tensor(slot, slot, keep, ALU.mult))
                after(a)
                dve.wait_ge(s_scat, b.at(64, N_ZERO))
                a = step(dve.tensor_tensor(slot_i[:], slot, trash[:], ALU.add))
                assert a == 24
                step(dve.tensor_scalar(du[:, :, META_TOKEN], trash[:], 1.0 - B * T, None, ALU.add))
                after(25)
                step(dve.tensor_scalar(trash[:], trash[:], float(T), None, ALU.add))
                step(dve.tensor_copy(du[:, :, META_GATE], gate))
                for r in range(KT):
                    step(dve.tensor_scalar(du[:, r, 0:D], du[:, r, 0:D], gate[:, r:r + 1], None, ALU.mult))
                assert n[0] == NR

            def r_spread(b, c):
                dve.wait_ge(s_pev, b.at(16, 12))
                if c >= 2:
                    dve.wait_ge(s_sc, b.at(16, 4 * (c - 2) + 4))
                else:
                    wait(dve, s_sc, b.at(16, 4 * (c - 2) + 4))
                for i in range(G):
                    hp = slice(i * N, (i + 1) * N)
                    dve.tensor_copy(rbd[hp, c % 2, :, i, :], kr[hp, 1, :, c * P:(c + 1) * P]).then_inc(s_rbd, 1)

            def mask(b, c, i):
                dve.wait_ge(s_sc, b.at(16, 4 * c + i + 1))
                if c > 0:
                    dve.wait_ge(s_pv, b.at(16, 4 * (c - 1) + i + 1))
                else:
                    wait(dve, s_pv, b.at(16, i - 3))
                dve.tensor_tensor(att[:, i, :], HIGH[i][:], decay[:, i, :, :].rearrange("p h q -> p (h q)"),
                                  ALU.mult).then_inc(s_mask, 1)

            def k_decay(b, c):
                dve.wait_ge(s_ktr, b.at(3, c + 1))
                wait(dve, s_kv, b.at(3, c))
                dve.tensor_tensor(kdec[:].rearrange("p (h n) -> p h n", n=N), LOW[2][:].rearrange("p (h n) -> p h n", n=N),
                                  kpow[:].unsqueeze(2).to_broadcast([P, H, N]), ALU.mult).then_inc(s_kdec, 1)

            def state_step(b, c):
                dve.wait_ge(s_kv, b.at(3, c + 1))
                new = st_new[:] if c else state[:, 1, :, :].rearrange("p g q -> p (g q)")
                if c == 0:
                    wait(dve, s_inter, b.at(3, 0))
                    wait(dve, s_wst, b.at(2, 0))
                dve.tensor_tensor(new.rearrange("p (g q) -> p g q", g=KT), LOW[2][:].rearrange("p (g q) -> p g q", g=KT),
                                  blk.unsqueeze(1).to_broadcast([P, KT, P]), ALU.mult).then_inc(s_st, 1)
                if c:
                    dve.wait_ge(s_st, b.at(5, 2 * c))
                    dve.wait_ge(s_wst, b.at(2, c))
                    dst = state[:, (c + 1) % 2, :, :].rearrange("p g q -> p (g q)")
                    dve.tensor_tensor(dst, st_new[:], st_old[:], ALU.add).then_inc(s_st, 1)

            def w_low(t, e, w):
                dve.wait_ge(s_whi, t.at(4, 2 * e + w + 1))
                dve.tensor_tensor(w_lo[:, e, w, :, :], w_raw[:, e, w, :, :], w_hi[:, e, w, :, :].bitcast(F32),
                                  ALU.subtract).then_inc(s_wlo, 1)

            def divide(b, c):
                dve.wait_ge(s_sd, b.at(4, c + 1))
                dve.reciprocal(sq[:], sq[:]).then_inc(s_nrm, 1)
                dve.wait_ge(s_nrm, b.at(8, 2 * c + 1))
                dve.tensor_tensor(yc[:, c % 2, :], yc[:, c % 2, :], sq[:], ALU.mult).then_inc(s_nrm, 1)

            def body(b):
                if (b - 2).exists():
                    dve.wait_ge(s_halo, (b - 2).at(96, 96))
                    dve.wait_ge(s_scat, (b - 2).at(64, N_ZERO))
                for p in (PK_, PR_, PG_):
                    if b.exists():
                        mixing(b, p)
                    if p == PK_ and (b - 1).exists():
                        divide(b - 1, KT - 1)
                    if (b - 2).exists():
                        laplacian(b - 2, p - 1)
                if (b - 2).exists():
                    laplacian(b - 2, 3)
                if b.exists():
                    r_spread(b, 0)
                    r_spread(b, 1)
                if (b - 1).exists():
                    residual(b - 1)
                if (b - 2).exists():
                    router(b - 2, 0)
                if not b.exists() and (b - 1).exists():
                    for e in range(2):
                        for w in range(2):
                            w_low(Step(0, 0), e, w)
                if not b.exists():
                    router(b - 2, 1)
                    return
                for c in range(KT):
                    for i in range(G):
                        mask(b, c, i)
                        if i == 0 and c < KT - 1:
                            k_decay(b, c)
                    if c < 2:
                        r_spread(b, c + 2)
                    if c < KT - 1:
                        state_step(b, c)
                    if c > 0:
                        divide(b, c - 1)
                    if c == 0 and (b - 2).exists():
                        router(b - 2, 1)
                if (b + 1).exists():
                    mixing(b + 1, PV_)

            dve.wait_ge(s_cst2, n_cst2)
            wv = wts[:, PV_, :, :].rearrange("p k (h n) -> p k h n", n=N)
            dve.wait_ge(s_wp[PV_], 16)
            dve.tensor_reduce(vmean[:], wv, AX.X, ALU.add).then_inc(s_wv, 1)
            dve.wait_ge(s_wv, 1)
            dve.tensor_scalar(vmean[:], vmean[:], 1.0 / N, None, ALU.mult).then_inc(s_wv, 1)
            dve.wait_ge(s_wv, 2)
            dve.tensor_tensor(wv, wv, vmean[:].unsqueeze(3).to_broadcast([P, KT, H, N]), ALU.subtract).then_inc(s_wv, 1)
            mixing(Step(0, 0), PV_)
            attention_bodies(dve, body)

            def tokens(t, e):
                rows = rows_sb[:, e, :].rearrange("p (r c) -> p r c", r=KT)
                dve.wait_ge(s_ein[e], t.at(32, 32))
                wait(dve, s_add[e], t.at(64, 0))
                dve.tensor_scalar(tok_f[:, e, :], rows[:, :, META_TOKEN], 0.0, None, ALU.is_equal).then_inc(s_tok, 1)
                dve.wait_ge(s_tok, t.at(8, 4 * e + 1))
                dve.tensor_tensor(tok_f[:, e, :], tok_f[:, e, :],
                                  cst[:, C_TRASH + e * KT:C_TRASH + (e + 1) * KT], ALU.mult).then_inc(s_tok, 1)
                dve.tensor_copy(gate_e[:, e, :], rows[:, :, META_GATE]).then_inc(s_tok, 1)
                dve.wait_ge(s_tok, t.at(8, 4 * e + 3))
                dve.scalar_tensor_tensor(tok_i[:, e, :], tok_f[:, e, :], -1.0, rows[:, :, META_TOKEN], ALU.add,
                                         ALU.add).then_inc(s_tok, 1)

            def x_low(t, e):
                for k in range(KT):
                    dve.wait_ge(s_xhi, t.at(8, 4 * e + k + 1))
                    dve.tensor_tensor(xt_lo[:, k, :], LOW[k][:], xt_hi[:, k, :].bitcast(F32),
                                      ALU.subtract).then_inc(s_xlo, 1)

            def hidden_low(t, e):
                for m in range(KT):
                    dve.wait_ge(s_relu, t.at(16, 8 * e + 2 * m + 2))
                    dve.tensor_tensor(ht_lo[:, m, :], ht[:, m, :], ht_hi[:, m, :].bitcast(F32),
                                      ALU.subtract).then_inc(s_hlo, 1)

            def results(t, e):
                for r in range(KT):
                    dve.wait_ge(s_down, t.at(8, 4 * e + r + 1))
                    dve.tensor_tensor(res[:, e, r, :], HIGH[r][:], b2_sb[:, e, :], ALU.add).then_inc(s_b2, 1)
                for r in range(KT):
                    dve.wait_ge(s_b2, t.at(8, 4 * e + r + 1))
                    dve.tensor_scalar(res[:, e, r, :], res[:, e, r, :], gate_e[:, e, r:r + 1], None,
                                      ALU.mult).then_inc(s_gate, 1)

            def pair(t, last):
                for e in range(2):
                    tokens(t, e)
                    hidden_low(t, e)
                    if not last:
                        w_low(t + 1, e, 0)
                    if e == 0:
                        x_low(t, 1)
                    elif not last:
                        x_low(t + 1, 0)
                    results(t, e)
                    if not last:
                        w_low(t + 1, e, 1)

            x_low(Step(0, 0), 0)
            pair(Step(0, 0), False)
            with dve.Fori(0, E // 2 - 2) as i:
                pair(Step(i, 1), False)
            pair(Step(0, E // 2 - 1), True)

        @block.gpsimd
        def _(pool):
            pool.wait_ge(s_init, 6)
            for e in range(E):
                pool.dma_start(slots[e * CAP:(e + 1) * CAP].rearrange("(p r) c -> p r c", r=KT), du[:]).then_inc(s_scat, 16)
            for e in range(2):
                at = B * T + e * CAP
                pool.dma_start(out[at:at + CAP].rearrange("(p r) c -> p r c", r=KT), du[:, :, 0:D]).then_inc(s_scat, 16)
            pool.wait_ge(s_cst2, n_cst2)
            pool.wait_ge(s_exp, 2 + H + 1 + KT + 1)

            def vertical(b, r):
                pool.wait_ge(s_halo, b.at(96, 96))
                if r >= 2:
                    pool.wait_ge(s_lap, b.at(20, 5 * (r - 2) + 5))
                pool.tensor_tensor(lv[:, r % 2, :], x1h[:, r, :], x1h[:, r + 2, :], ALU.add).then_inc(s_lv, 1)

            def r_decay(b, c):
                pool.wait_ge(s_pev, b.at(16, 12))
                if c >= 3:
                    pool.wait_ge(s_inter, b.at(3, c - 2))
                else:
                    wait(pool, s_inter, b.at(3, 0))
                pool.tensor_tensor(rdec[:, c % 2, :, :], kr[:, 1, :, c * P:(c + 1) * P], rpow[:], ALU.mult).then_inc(s_rdec, 1)

            def state_decay(b, c):
                pool.wait_ge(s_st, b.at(5, 2 * c - 1))
                pool.tensor_tensor(st_old[:].rearrange("p (g q) -> p g q", g=KT), state[:, c % 2, :, :],
                                   wpow[:].unsqueeze(2).to_broadcast([P, KT, P]), ALU.mult).then_inc(s_wst, 1)

            def z_product(b, c):
                pool.wait_ge(s_aff, b.at(16, 4 * c + 4))
                pool.wait_ge(s_pev, b.at(16, 16))
                q = P // KT
                z = zt[:].rearrange("p g (r q) -> p g r q", r=KT)[:, :, :, c * q:(c + 1) * q]
                pool.tensor_tensor(z, yc[:, c % 2, :].rearrange("p (g q r) -> p g r q", g=KT, r=KT), z,
                                   ALU.mult).then_inc(s_z, 1)

            def scatter(b):
                pool.wait_ge(s_rt, b.at(NR, NR))
                pool.sem_inc(s_pool_on, 1)
                pool.wait_ge(s_scat, N_ZERO)
                for r in range(KT):
                    pool.indirect_dma_start(slots, bass.IndirectOffsetOnAxis(slot_i[:, r:r + 1], 0),
                                            du[:, r, :], None).then_inc(s_scat, 16)

            def body(b):
                if (b - 2).exists():
                    for r in range(KT):
                        vertical(b - 2, r)
                if b.exists():
                    r_decay(b, 1)
                    r_decay(b, 2)
                if (b - 2).exists():
                    scatter(b - 2)
                if b.exists():
                    state_decay(b, 1)
                    z_product(b, 0)
                    r_decay(b, 3)
                    state_decay(b, 2)
                    for c in range(1, KT):
                        z_product(b, c)

            attention_bodies(pool, body)

            def add_rows(t, e):
                pool.wait_ge(s_tok, t.at(8, 4 * e + 4))
                for r in range(KT):
                    pool.wait_ge(s_gate, t.at(8, 4 * e + r + 1))
                    pool.sem_inc(s_pool_on, 1)
                    pool.wait_ge(s_store, 16 * B)
                    pool.indirect_dma_start(out, bass.IndirectOffsetOnAxis(tok_i[:, e, r:r + 1], 0),
                                            res[:, e, r, :], None, compute_op=ALU.add).then_inc(s_add[e], 16)

            with pool.Fori(0, E // 2) as i:
                for e in range(2):
                    add_rows(Step(i, 0), e)
            for e in range(2):
                pool.wait_ge(s_add[e], 64 * (E // 2))


def kernel(x, itok_B_0_30, condB_zX, condB_zY, condB_zR, L0_cond_weights, L0_attn_time_maa_k, L0_attn_time_maa_v,
           L0_attn_time_maa_r, L0_attn_time_maa_g, L0_attn_time_decay, L0_attn_time_faaaa, L0_attn_Wr, L0_attn_Wk,
           L0_attn_Wv, L0_attn_Wg, L0_attn_Wo, L0_attn_ln_w, L0_attn_ln_b, L0_ffn_Wr, L0_ffn_br, L0_ffn_W1,
           L0_ffn_b1, L0_ffn_W2, L0_ffn_b2):
    import concourse.bacc as bacc
    from concourse.bass_utils import run_bass_kernel_spmd

    def channels(a):
        return np.asarray(a).reshape(KT, P).T

    maas = (L0_attn_time_maa_v, L0_attn_time_maa_k, L0_attn_time_maa_r, L0_attn_time_maa_g)
    projections = (L0_attn_Wv, L0_attn_Wk, L0_attn_Wr, L0_attn_Wg)
    arrays = {
        "x": x,
        "subj": np.asarray(itok_B_0_30).reshape(1, B),
        "zxyr": np.stack([condB_zX, condB_zY, condB_zR])[None],
        "wcond": L0_cond_weights,
        "maa": np.stack([channels(a) for a in maas], axis=1),
        "wproj": np.stack([np.asarray(a).T for a in projections]),
        "wo": np.asarray(L0_attn_Wo).T,
        "decay_heads": np.asarray(L0_attn_time_decay).reshape(1, H),
        "decay_rows": np.repeat(np.asarray(L0_attn_time_decay).reshape(KT, G).T, N, axis=0),
        "bonus": np.asarray(L0_attn_time_faaaa).reshape(1, H),
        "ln_wb": np.stack([channels(a) for a in (L0_attn_ln_w, L0_attn_ln_b)], axis=1),
        "router_w": L0_ffn_Wr,
        "router_b": np.asarray(L0_ffn_br).reshape(1, E),
        "w1": L0_ffn_W1,
        "b1": np.asarray(L0_ffn_b1).reshape(E, KT, P).transpose(2, 0, 1),
        "w2": L0_ffn_W2,
        "b2": L0_ffn_b2,
        "consts": shape_constants(),
    }
    arrays = {f"in_{k}": np.ascontiguousarray(v) for k, v in arrays.items()}
    nc = bacc.Bacc("TRN2", target_bir_lowering=False, num_devices=1)
    args = [nc.dram_tensor(k, a.shape, mybir.dt.from_np(a.dtype), kind="ExternalInput").ap()
            for k, a in arrays.items()]
    out = nc.dram_tensor("out_rows", (B * T + TRASH_ROWS, D), F32, kind="ExternalOutput").ap()
    build(nc, *args, out)
    result = run_bass_kernel_spmd(nc, [arrays], core_ids=[0])
    return result.results[0]["out_rows"][:B * T].reshape(B, T, D)
```

```python
from contextlib import ExitStack

import numpy as np

import concourse.bass as bass
from concourse import mybir

F32 = mybir.dt.float32
F32R = mybir.dt.float32r
I32 = mybir.dt.int32
ACT = mybir.ActivationFunctionType
ALU = mybir.AluOpType
AX = mybir.AxisListType

P = 128
B, T, D = 8, 512, 512
KT = D // P
H, N = 16, 32
G = P // N
E = 8
CAP = B * T // E
EW = D + 4
META_GATE, META_TOKEN = D, D + 1
TRASH_ROWS = 2 * CAP
GN_EPS = 1e-5 * 64
HUGE_RATE = 1e30

PV_, PK_, PR_, PG_ = range(4)
LAP_ORDER = (1, 2, 0, 3)
RING = 4

C_ID, C_TRI, C_BLK = (128 * i for i in range(3))
C_TAIL = 3 * 128
C_PRI = C_TAIL + 1
C_EOFF = C_PRI + E
C_TOK = C_EOFF + E
C_TRASH = C_TOK + KT
CW = C_TRASH + 2 * KT
C_LAG, C_GT, C_Q = (128 * i for i in range(3))


def shape_constants():
    p = np.arange(P)[:, None]
    q = np.arange(P)[None, :]
    r = np.arange(KT)[None, :]
    one = np.ones((P, 1))
    parts = [p == q, p < q, p // N == q // N,
             P - 1 - p, one * (E - np.arange(E)), one * (CAP * np.arange(E)), B * T + KT * p + r,
             B * T + KT * p + r + 1, B * T + CAP + KT * p + r + 1,
             np.maximum(q - p - 1, 0), q > p, q + 0 * p]
    out = np.concatenate([np.asarray(x, np.float32) for x in parts], axis=1)
    assert out.shape == (P, CW + 3 * 128)
    return out


class Step:

    def __init__(self, reg, off):
        self.reg, self.off = reg, off

    def __sub__(self, k):
        return Step(self.reg, self.off - k)

    def __add__(self, k):
        return Step(self.reg, self.off + k)

    def at(self, per, k):
        return self.reg * per + (self.off * per + k)

    def exists(self):
        return not isinstance(self.reg, int) or 0 <= self.reg + self.off < B

    def index(self):
        return self.reg + self.off


def wait(eng, sem, value):
    if isinstance(value, int) and value <= 0:
        return
    eng.wait_ge(sem, value)


def build(nc, x, subj, zxyr, wcond, maa, wproj, wo, decay_heads, decay_rows, bonus, ln_wb, router_w,
          router_b, w1, b1, w2, b2, consts, out):
    wo_dram = nc.dram_tensor("wo_low", (P, KT, D), F32).ap()
    slots = nc.dram_tensor("slots", (2 * B * T, EW), F32).ap()
    ctx, attention_memory, experts_memory = ExitStack(), ExitStack(), ExitStack()
    with ctx:
        def sb(name, shape, dt=F32):
            return ctx.enter_context(nc.sbuf_tensor(name, shape, dt))

        def sb_a(name, shape, dt=F32):
            return attention_memory.enter_context(nc.sbuf_tensor(name, shape, dt))

        def sb_e(name, shape, dt=F32):
            return experts_memory.enter_context(nc.sbuf_tensor(name, shape, dt))

        def sem(name):
            return ctx.enter_context(nc.semaphore(name))

        cst = sb("cst", [P, CW])
        ones = sb("ones", [P, P])
        lnwb = sb("lnwb", [P, 2, KT])
        eps = sb("eps", [P, 1])
        maa_sb = sb("maa_sb", [P, 4, KT])
        rate_h = sb("rate_h", [P, 2, H])
        rate_p = sb("rate_p", [P, 2, KT])
        bonus_sb = sb("bonus_sb", [P, H])
        kpow = sb("kpow", [P, H])
        wpow = sb("wpow", [P, KT])
        zs = sb("zs", [P, 3, B])
        zq = sb("zq", [P, 2, B])
        rw_sb = sb("rw_sb", [P, KT, E])
        rb_sb = sb("rb_sb", [P, E])
        subj_sb = sb("subj_sb", [1, B], I32)
        lg = sb("lg", [P, 8, KT, E])
        rs = sb("rs", [P, 12, KT])
        cnt = sb("cnt", [P, E])
        base = sb("base", [P, E])
        trash = sb("trash", [P, KT])
        slot_i = sb("slot_i", [P, KT], I32)
        b1_sb = sb("b1_sb", [P, E, KT])
        tok_f = sb("tok_f", [P, 2, KT])
        tok_i = sb("tok_i", [P, 2, KT], I32)
        gate_e = sb("gate_e", [P, 2, KT])

        p_hi = sb_a("p_hi", [P, 4, KT, D], F32R)
        p_lo = sb_a("p_lo", [P, 4, KT, D], F32R)
        wo_hi = sb_a("wo_hi", [P, KT, D], F32R)
        with ExitStack() as overlaid:
            xw = overlaid.enter_context(nc.sbuf_tensor("xw", [P, 2, KT, T], F32))
        mix_hi = sb_a("mix_hi", [P, RING, T], F32R)
        mix_lo = sb_a("mix_lo", [P, RING, T], F32R)
        hs = sb_a("hs", [P, KT, T + 1])
        kr = sb_a("kr", [P, 2, KT, T])
        v_sb = sb_a("v_sb", [P, KT, D])
        decay = sb_a("decay", [P, KT, G, P])
        att = sb_a("att", [P, KT, G * P])
        with ExitStack() as overlaid:
            wo_raw = overlaid.enter_context(nc.sbuf_tensor("wo_raw", [P, KT, D], F32))
        with ExitStack() as overlaid:
            wo_lo = overlaid.enter_context(nc.sbuf_tensor("wo_lo", [P, KT, D], F32R))
        rbd = sb_a("rbd", [P, KT, G, P])
        rdec = sb_a("rdec", [P, 2, KT, P])
        kdec = sb_a("kdec", [P, D])
        state = sb_a("state", [P, 2, KT, P])
        st_new = kdec
        st_old = sb_a("st_old", [P, D])
        mixed = (kdec, st_old)
        with ExitStack() as overlaid:
            z_lo = overlaid.enter_context(nc.sbuf_tensor("z_lo", [P, KT, T], F32R))
        zt = sb_a("zt", [P, KT, T])
        z_hi = sb_a("z_hi", [P, KT, T], F32R)
        yc = sb_a("yc", [P, 2, D])
        blk_hi = sb_a("blk_hi", [P, P], F32R)
        with ExitStack() as overlaid:
            sq_lo = overlaid.enter_context(nc.sbuf_tensor("sq_lo", [P, 2, D], F32R))
        sq = sb_a("sq", [P, 2, D])
        x1h = sb_a("x1h", [P, KT + 2, D])
        du = sb_a("du", [P, KT, EW])
        rpow = sb_a("rpow", [P, KT, P])
        lv, lq = att[:, 0:2, :], att[:, 2:4, :]
        lh = rdec[:].rearrange("p c g q -> p c (g q)")
        dut = lh
        xw_flat = xw[:].rearrange("p a r t -> p (a r t)")
        du_alt = xw_flat[:, 0:KT * EW].rearrange("p (r c) -> p r c", r=KT)
        lh_alt = xw_flat[:, KT * EW:KT * EW + 2 * D].rearrange("p (n t) -> p n t", n=2)
        hs_flat = hs[:].rearrange("p k t -> p (k t)")
        lv_alt = hs_flat[:, 0:2 * D].rearrange("p (n t) -> p n t", n=2)
        lq_alt = hs_flat[:, 2 * D:4 * D].rearrange("p (n t) -> p n t", n=2)
        table_cst = yc[:, 0, 0:3 * P]
        vmean = sq[:, 0, 0:KT * H].rearrange("p (k h) -> p k h", k=KT)
        p_raw = (att[:], zt[:], x1h[:, 0:KT, :], kr[:, 1, :, :], wo_raw[:])
        attention_memory.close()

        w_raw = sb_e("w_raw", [P, 2, 2, KT, D])
        w_hi = sb_e("w_hi", [P, 2, 2, KT, D], F32R)
        sb_e("under_wo_hi", [P, KT, D])
        rows_sb = sb_e("rows_sb", [P, 2, KT * EW])
        w_lo = sb_e("w_lo", [P, 2, 2, KT, D], F32R)
        xt_hi = sb_e("xt_hi", [P, KT, CAP], F32R)
        xt_lo = sb_e("xt_lo", [P, KT, CAP], F32R)
        ht = sb_e("ht", [P, KT, CAP])
        ht_hi = sb_e("ht_hi", [P, KT, CAP], F32R)
        ht_lo = sb_e("ht_lo", [P, KT, CAP], F32R)
        res = sb_e("res", [P, 2, KT, D])
        b2_sb = sb_e("b2_sb", [P, 2, D])
        experts_memory.close()

        bank = [ctx.enter_context(nc.psum_tensor(f"bank{i}", [P, 512], F32)) for i in range(8)]
        LOW, HIGH = bank[:4], bank[4:]

        ident = cst[:, C_ID:C_ID + P]
        tri = cst[:, C_TRI:C_TRI + P]
        blk = cst[:, C_BLK:C_BLK + P]

        s_cst = sem("s_cst")
        s_cst2 = sem("s_cst2")
        s_subj = sem("s_subj")
        s_xw = [sem(f"s_xw{r}") for r in range(KT)]
        s_wp = [sem(f"s_wp{i}") for i in range(5)]
        s_resid = sem("s_resid")
        s_store = sem("s_store")
        s_halo = sem("s_halo")
        s_scat = sem("s_scat")
        s_init = sem("s_init")
        s_tab = sem("s_tab")
        s_exp = sem("s_exp")
        s_cond = sem("s_cond")
        s_used = sem("s_used")
        s_proj = sem("s_proj")
        s_o = sem("s_o")
        s_dtr = sem("s_dtr")
        s_log = sem("s_log")
        s_pre = sem("s_pre")
        s_sc = sem("s_sc")
        s_ktr = sem("s_ktr")
        s_kv = sem("s_kv")
        s_inter = sem("s_inter")
        s_pv = sem("s_pv")
        s_var = sem("s_var")
        s_wo_out = sem("s_wo_out")
        s_wo = sem("s_wo")
        s_zhi = sem("s_zhi")
        s_zlo = sem("s_zlo")
        s_rz = sem("s_rz")
        s_phi = sem("s_phi")
        s_mhi = sem("s_mhi")
        s_pev = sem("s_pev")
        s_hev = sem("s_hev")
        s_dev = sem("s_dev")
        s_sq = sem("s_sq")
        s_sqlo = sem("s_sqlo")
        s_blk = sem("s_blk")
        s_sd = sem("s_sd")
        s_aff = sem("s_aff")
        s_lq = sem("s_lq")
        s_rex = sem("s_rex")
        s_diff = sem("s_diff")
        s_mixed = sem("s_mixed")
        s_mix = sem("s_mix")
        s_plo = sem("s_plo")
        s_mask = sem("s_mask")
        s_kdec = sem("s_kdec")
        s_st = sem("s_st")
        s_nrm = sem("s_nrm")
        s_wv = sem("s_wv")
        s_x1 = sem("s_x1")
        s_lap = sem("s_lap")
        NR = 31
        s_rt = sem("s_rt")
        s_rdec = sem("s_rdec")
        s_wst = sem("s_wst")
        s_rbd = sem("s_rbd")
        s_z = sem("s_z")
        s_lv = sem("s_lv")
        s_act_on = sem("s_act_on")
        s_pool_on = sem("s_pool_on")
        s_we = [sem(f"s_we{i}") for i in range(2)]
        s_ein = [sem(f"s_ein{i}") for i in range(2)]
        s_add = [sem(f"s_add{i}") for i in range(2)]
        s_whi = sem("s_whi")
        s_wlo = sem("s_wlo")
        s_etr = sem("s_etr")
        s_xhi = sem("s_xhi")
        s_xlo = sem("s_xlo")
        s_up = sem("s_up")
        s_relu = sem("s_relu")
        s_hlo = sem("s_hlo")
        s_down = sem("s_down")
        s_b2 = sem("s_b2")
        s_gate = sem("s_gate")
        s_tok = sem("s_tok")

        block = ctx.enter_context(nc.Block())

        N_ZERO = 16 * (E + 2)
        N_TAB = 2 + 2 * H + 3
        n_cst, n_cst2 = 7 * 16, 5 * 16

        def used_wait(eng, b, p, tt):
            if tt < KT - 1:
                wait(eng, s_used, b.at(12, 3 * p + tt + 1))
            else:
                wait(eng, s_proj, b.at(16, 4 * p + 4))

        def z_chunk(tile, c):
            return tile[:].rearrange("p g (r q) -> p g r q", r=KT)[:, :, :, c * (P // KT):(c + 1) * (P // KT)]

        def du_of(b):
            return du_alt if is_before_last(b) else du[:]

        def lh_of(b):
            return lh_alt if is_last(b) or is_before_last(b) else lh

        def lv_of(b):
            return lv_alt if is_before_last(b) else lv

        def lq_of(b):
            return lq_alt if is_before_last(b) else lq

        def is_last(b):
            return isinstance(b.reg, int) and b.reg + b.off == B - 1

        def is_before_last(b):
            return isinstance(b.reg, int) and b.reg + b.off == B - 2

        def after_attention(eng, b):
            if is_last(b):
                eng.wait_ge(s_mixed, 16 * B)
            elif b.exists():
                eng.wait_ge(s_pv, b.at(16, 16))

        def attention_bodies(eng, body):
            for b in range(2):
                body(Step(0, b))
            with eng.Fori(0, B - 3) as i:
                body(Step(i, 2))
            for b in range(B - 1, B + 2):
                body(Step(0, b))

        def load_weights(sp, t, e):
            n = t.index() * 2 + e
            sp.dma_start(w_raw[:, e, 0, :, :],
                         w1[bass.ds(n, 1)].rearrange("a (k p) f -> p (a k) f", p=P)).then_inc(s_we[e], 16)
            sp.dma_start(w_raw[:, e, 1, :, :],
                         w2[bass.ds(n, 1)].rearrange("a (k p) f -> p (a k) f", p=P)).then_inc(s_we[e], 16)

        def load_rows(sp, t, e):
            n = t.index() * 2 + e
            sp.dma_start(rows_sb[:, e, :],
                         slots[bass.ds(n * CAP, CAP)].rearrange("(p r) c -> p (r c)", r=KT)).then_inc(s_ein[e], 16)
            sp.dma_start(b2_sb[:, e, :], b2[bass.ds(n, 1)].to_broadcast([P, D])).then_inc(s_ein[e], 16)

        @block.sync
        def _(sp):
            sp.dma_start(subj_sb[:], subj).then_inc(s_subj, 16)
            for r in range(KT):
                sp.dma_start(xw[:, 0, r, :], x[0].rearrange("(p r) t -> p r t", r=KT)[:, r, :]).then_inc(s_xw[r], 16)
            sp.wait_ge(s_subj, 16)

            def load_xw(b):
                s = sp.value_load(subj_sb[0:1, bass.ds(b.index(), 1)], min_val=0, max_val=wcond.shape[0] - 1)
                xs = x[bass.ds(b.index(), 1)].rearrange("a (p r) t -> (a p) r t", r=KT)
                ws = wcond[bass.ds(s, 1)].rearrange("a (p r) t -> (a p) r t", r=KT)
                for r in range(KT):
                    if (b - 1).exists():
                        used_wait(sp, b - 1, PG_, r)
                        sp.dma_start(xw[:, 0, r, :], xs[:, r, :]).then_inc(s_xw[r], 16)
                    sp.dma_start(xw[:, 1, r, :], ws[:, r, :]).then_inc(s_xw[r], 16)

            def load_p(p):
                src = wproj[p] if p < 4 else wo
                sp.dma_start(p_raw[p], src.rearrange("(k p) o -> p k o", p=P)).then_inc(s_wp[p], 16)

            load_xw(Step(0, 0))
            load_p(PV_)
            sp.dma_start(cst[:], consts[:, 0:CW]).then_inc(s_cst, 16)
            sp.dma_start(table_cst, consts[:, CW:CW + 3 * P]).then_inc(s_cst, 16)
            sp.dma_start(rate_h[:, 1, :], decay_heads.to_broadcast([P, H])).then_inc(s_cst, 16)
            sp.dma_start(rate_p[:, 1, :], decay_rows).then_inc(s_cst, 16)
            sp.dma_start(bonus_sb[:], bonus.to_broadcast([P, H])).then_inc(s_cst, 16)
            sp.dma_start(maa_sb[:], maa).then_inc(s_cst, 16)
            sp.dma_start(zs[:], zxyr.to_broadcast([P, 3, B])).then_inc(s_cst, 16)
            sp.dma_start(lnwb[:], ln_wb).then_inc(s_cst2, 16)
            sp.dma_start(rw_sb[:], router_w.rearrange("(k p) e -> p k e", p=P)).then_inc(s_cst2, 16)
            sp.dma_start(rb_sb[:], router_b.to_broadcast([P, E])).then_inc(s_cst2, 16)
            sp.dma_start(b1_sb[:], b1).then_inc(s_cst2, 16)
            sp.dma_start(trash[:], consts[:, C_TOK:C_TOK + KT]).then_inc(s_cst2, 16)
            for p in range(1, 5):
                load_p(p)
            sp.wait_ge(s_plo, PR_ + 1)

            sp.wait_ge(s_plo, 5)
            sp.dma_start(wo_dram, wo_lo[:].bitcast(F32)).then_inc(s_wo_out, 16)
            sp.wait_ge(s_wo_out, 16)

            def body(b):
                if (b - 1).exists():
                    wait(sp, s_lap, (b - 2).at(20, 20))
                    wait(sp, s_lv, (b - 2).at(4, 4))
                    wait(sp, s_lq, (b - 2).at(4, 4))
                    wait(sp, s_store, (b - 2).at(16, 16))
                    sp.dma_start(x1h[:, 1:KT + 1, :],
                                 x[bass.ds((b - 1).index(), 1)].rearrange("a (p r) t -> (a p) r t", r=KT)
                                 ).then_inc(s_resid, 16)
                if is_last(b - 1):
                    sp.wait_ge(s_proj, 16 * B)
                    for e in range(2):
                        load_weights(sp, Step(0, 0), e)
                if b.exists() and (b + 1).exists():
                    load_xw(b + 1)
                if (b - 1).exists():
                    sp.wait_ge(s_x1, (b - 1).at(4, 4))
                    sp.dma_start(out[bass.ds((b - 1).index() * T, T)].rearrange("(p r) t -> p r t", r=KT),
                                 x1h[:, 1:KT + 1, :]).then_inc(s_store, 16)
                    for lo, hi in ((1, 113), (113, P)):
                        sp.dma_start(x1h[lo:hi, 0, :], x1h[lo - 1:hi - 1, KT, :]).then_inc(s_halo, 16)
                    for lo, hi in ((0, 112), (112, P - 1)):
                        sp.dma_start(x1h[lo:hi, KT + 1, :], x1h[lo + 1:hi + 1, 1, :]).then_inc(s_halo, 16)
                    sp.dma_start(x1h[0:1, 0, :], x1h[0:1, 2, :]).then_inc(s_halo, 16)
                    sp.dma_start(x1h[P - 1:P, KT + 1, :], x1h[P - 1:P, KT - 1, :]).then_inc(s_halo, 16)
                if b.exists():
                    sp.wait_ge(s_sc, b.at(16, 16))
                    sp.dma_start(wo_lo[:].bitcast(F32), wo_dram).then_inc(s_wo, 16)

            for b in range(2):
                body(Step(0, b))
            with sp.Fori(0, B - 3) as i:
                body(Step(i, 2))
            for b in range(B - 1, B + 2):
                body(Step(0, b))

            sp.wait_ge(s_scat, 64 * B + N_ZERO)
            for e in range(2):
                load_rows(sp, Step(0, 0), e)
            with sp.Fori(0, E // 2 - 1) as i:
                for e in range(2):
                    sp.wait_ge(s_wlo, Step(i, 0).at(4, 2 * e + 2))
                    load_weights(sp, Step(i, 1), e)
                for e in range(2):
                    sp.wait_ge(s_etr, Step(i, 0).at(8, 4 * e + 4))
                    sp.wait_ge(s_tok, Step(i, 0).at(8, 4 * e + 4))
                    sp.wait_ge(s_b2, Step(i, 0).at(8, 4 * e + 4))
                    load_rows(sp, Step(i, 1), e)
            sp.wait_ge(s_store, 16 * B)

        @block.tensor
        def _(pe):
            def split_product(dst, lhs_hi, lhs_lo, rhs_hi, rhs_lo, start, stop):
                pe.matmul(dst, lhs_hi, rhs_hi, start=start, stop=False)
                pe.matmul(dst, lhs_hi, rhs_lo, start=False, stop=False)
                return pe.matmul(dst, lhs_lo, rhs_hi, start=False, stop=stop)

            def cond_tile(b, m, dst):
                for r in range(KT):
                    if m == 0:
                        pe.wait_ge(s_xw[r], b.at(32, 32))
                    last = pe.matmul(dst[:], xw[:, 0, r, m * P:(m + 1) * P], xw[:, 1, r, :], start=r == 0, stop=r == KT - 1)
                last.then_inc(s_cond, 1)

            def project(b, p, banks, free, between=None):
                pe.wait_ge(s_plo, p + 1)
                for tt in range(KT):
                    pe.wait_ge(s_mix, b.at(16, 4 * p + tt + 1))
                    j = (4 * p + tt) % RING
                    for m in range(KT):
                        if tt == 0:
                            free(m)
                        ms = slice(m * P, (m + 1) * P)
                        if p == PV_:
                            operands = (mix_hi[:, j, ms], mix_lo[:, j, ms], p_hi[:, p, tt, :], p_lo[:, p, tt, :])
                        else:
                            operands = (p_hi[:, p, tt, ms], p_lo[:, p, tt, ms], mix_hi[:, j, :], mix_lo[:, j, :])
                        ins = split_product(banks[m][:], *operands, tt == 0, tt == KT - 1)
                        if tt == KT - 1:
                            ins.then_inc(s_proj, 1)
                    if tt < KT - 1:
                        ins.then_inc(s_used, 1)
                    if between:
                        between(tt)

            def output_product(b):
                pe.wait_ge(s_wo, b.at(16, 16))
                pe.wait_ge(s_zlo, b.at(4, 4))
                for r in range(KT):
                    nxt = b + 1
                    if nxt.exists():
                        pe.wait_ge(s_pev, nxt.at(16, 4 * PR_ + r + 1))
                    else:
                        wait(pe, s_sd, b.at(4, 4))
                        wait(pe, s_st, b.at(5, 5))
                    for k in range(KT):
                        rows_r = slice(r * P, (r + 1) * P)
                        last = split_product(LOW[r][:], z_hi[:, k, rows_r], z_lo[:, k, rows_r], wo_hi[:, k, :],
                                             wo_lo[:, k, :], k == 0, k == KT - 1)
                    last.then_inc(s_o, 1)

            def du_transpose(b):
                if not is_last(b):
                    pe.wait_ge(s_lap, b.at(20, 20))
                    for k in range(KT):
                        if (b + 2).exists():
                            pe.wait_ge(s_pev, (b + 2).at(16, 4 * PG_ + k + 1))
                        else:
                            pe.wait_ge(s_mask, (b + 1).at(16, 16))
                        for r in range(KT):
                            last = pe.transpose(HIGH[k][:, r * P:(r + 1) * P], du_of(b)[:, r, k * P:(k + 1) * P], ident)
                        last.then_inc(s_dtr, 1)
                    return
                for n, r in enumerate(LAP_ORDER):
                    pe.wait_ge(s_lap, b.at(20, 5 * n + 5))
                    for k in range(KT):
                        if n == 0:
                            pe.wait_ge(s_dev, (b - 1).at(4, k + 1))
                        last = pe.transpose(HIGH[k][:, r * P:(r + 1) * P], du[:, r, k * P:(k + 1) * P], ident)
                        if n == KT - 1:
                            last.then_inc(s_dtr, 1)

            def logits(b, k):
                if k == 0:
                    if (b + 1).exists():
                        pe.wait_ge(s_x1, (b + 1).at(4, 1))
                    else:
                        pe.wait_ge(s_rt, (b - 1).at(NR, 12))
                    pe.wait_ge(s_cst2, n_cst2)
                pe.wait_ge(s_dev, b.at(4, k + 1))
                for r in range(KT):
                    last = pe.matmul(LOW[0][:, r * E:(r + 1) * E], dut[:, k % 2, r * P:(r + 1) * P],
                                     rw_sb[:, k, :], start=k == 0 and r == 0, stop=k == KT - 1,
                                     skip_group_check=True)
                last.then_inc(s_log, 1)

            def prefix(b):
                pe.wait_ge(s_rt, b.at(NR, 8))
                if (b + 1).exists():
                    pe.wait_ge(s_x1, (b + 1).at(4, 2))
                pe.matmul(LOW[1][:, 0:E], tri, cnt[:], start=True, stop=False, skip_group_check=True)
                pe.matmul(LOW[1][:, E:2 * E], ones[:], cnt[:], start=False, stop=True,
                          skip_group_check=True).then_inc(s_pre, 1)

            def scores(b, c):
                for g in range(KT):
                    if c > 0:
                        pe.wait_ge(s_mask, b.at(16, 4 * (c - 1) + g + 1))
                    elif (b - 2).exists():
                        pe.wait_ge(s_dev, (b - 2).at(4, g + 1))
                    else:
                        pe.wait_ge(s_pev, b.at(16, 4 * PG_ + g + 1))
                    if g == 0:
                        pe.wait_ge(s_rbd, b.at(16, 4 * c + 4))
                    pe.matmul(HIGH[g][:], kr[:, 0, g, c * P:(c + 1) * P],
                              rbd[:, g, :, :].rearrange("p i q -> p (i q)"), start=True,
                              stop=True).then_inc(s_sc, 1)
                    if c == 0 and (b - 2).exists():
                        logits(b - 2, g)

            def bank_of_state(b, c):
                if c > 0:
                    wait(pe, s_st, b.at(5, (1, 2)[c - 1]))
                elif (b - 1).exists():
                    pe.wait_ge(s_x1, (b - 1).at(4, 3))
                else:
                    pe.wait_ge(s_pev, b.at(16, 4 * PR_ + 3))

            def k_transpose(b, c):
                bank_of_state(b, c)
                for g in range(KT):
                    last = pe.transpose(LOW[2][:, g * P:(g + 1) * P], kr[:, 0, g, c * P:(c + 1) * P], ident)
                last.then_inc(s_ktr, 1)

            def state_product(b, c):
                pe.wait_ge(s_kdec, b.at(3, c + 1))
                for g in range(KT):
                    last = pe.matmul(LOW[2][:, g * P:(g + 1) * P], kdec[:, g * P:(g + 1) * P],
                                     v_sb[:, c, g * P:(g + 1) * P], start=True, stop=True)
                last.then_inc(s_kv, 1)

            def bank_of_y(b, c):
                if c >= 2:
                    pe.wait_ge(s_sd, b.at(4, c - 1))
                elif (b - 2).exists():
                    pe.wait_ge(s_rt, (b - 2).at(NR, 1 if c == 0 else 12))
                elif (b - 1).exists():
                    pe.wait_ge(s_x1, (b - 1).at(4, c + 1))
                else:
                    pe.wait_ge(s_pev, b.at(16, 4 * PR_ + c + 1))

            def from_state(b, c):
                bank_of_y(b, c)
                pe.wait_ge(s_st, b.at(5, (1, 3, 5)[c - 1]))
                pe.wait_ge(s_rdec, b.at(3, c))
                for g in range(KT):
                    last = pe.matmul(LOW[c % 2][:, g * P:(g + 1) * P], state[:, c % 2, g, :], rdec[:, c % 2, g, :],
                                     start=g == 0, stop=False, skip_group_check=True)
                last.then_inc(s_inter, 1)

            def from_scores(b, c):
                if c == 0:
                    bank_of_y(b, 0)
                for g in range(KT):
                    pe.wait_ge(s_mask, b.at(16, 4 * c + g + 1))
                    for i in range(G):
                        h0 = g * P + i * N
                        last = pe.matmul(LOW[c % 2][i * N:(i + 1) * N, g * P:(g + 1) * P], v_sb[:, c, h0:h0 + N],
                                         att[:, g, i * P:(i + 1) * P], start=c == 0 and g == 0,
                                         stop=g == KT - 1, skip_group_check=True)
                    last.then_inc(s_pv, 1)

            def variance(b, c):
                pe.wait_ge(s_sq, b.at(12, 3 * c + 3))
                pe.matmul(LOW[c % 2][:].rearrange("p (g r q) -> p g r q", g=KT, r=KT), blk_hi[:], z_chunk(z_hi, c),
                          start=True, stop=False)
                pe.wait_ge(s_sqlo, b.at(4, c + 1))
                pe.matmul(LOW[c % 2][:], blk_hi[:], sq_lo[:, c % 2, :], start=False, stop=True).then_inc(s_var, 1)

            def cond_bank(b, m):
                if m > 0:
                    pe.wait_ge(s_hev, (b + 1).at(4, m))
                elif (b - 1).exists():
                    pe.wait_ge(s_x1, (b - 1).at(4, 4))
                else:
                    pe.wait_ge(s_pev, b.at(16, 4 * PR_ + 4))

            def body(b):
                if b.exists():
                    def free_v(m):
                        wait(pe, s_mask, b.at(16, 0))

                    def free_k(m):
                        if not (b - 1).exists():
                            if m == 0:
                                pe.wait_ge(s_hev, 4)
                        elif m < 2:
                            pe.wait_ge(s_sd, (b - 1).at(4, m + 3))
                        elif m == 2:
                            pe.wait_ge(s_st, (b - 1).at(5, 5))
                        else:
                            pe.wait_ge(s_hev, b.at(4, 4))

                    def free_r(m):
                        pe.wait_ge(s_pev, b.at(16, 4 * PK_ + m + 1))

                    def free_g(m):
                        pe.wait_ge(s_pev, b.at(16, m + 1))

                    def between(tt):
                        if (b - 1).exists() and tt < 2:
                            variance(b - 1, KT - 2 + tt)

                    project(b, PV_, HIGH, free_v, between)
                else:
                    if (b - 1).exists():
                        variance(b - 1, KT - 1)
                if b.exists():
                    project(b, PK_, LOW, free_k)
                    project(b, PR_, LOW, free_r)
                if (b - 1).exists():
                    output_product(b - 1)
                if is_last(b - 1):
                    du_transpose(b - 2)
                    for k in range(KT):
                        logits(b - 2, k)
                    du_transpose(b - 1)
                    prefix(b - 2)
                if b.exists():
                    project(b, PG_, HIGH, free_g)
                if b.exists() and (b - 2).exists():
                    du_transpose(b - 2)
                if is_last(b - 2):
                    for k in range(KT):
                        logits(b - 2, k)
                    prefix(b - 2)
                if not b.exists():
                    return
                for c in range(KT):
                    if c == KT - 1 and (b + 1).exists():
                        cond_bank(b, c)
                        cond_tile(b + 1, c, LOW[3])
                    scores(b, c)
                    if c < KT - 1:
                        k_transpose(b, c)
                    if c > 0:
                        from_scores(b, c - 1)
                    if c < KT - 1 and (b + 1).exists():
                        cond_bank(b, c)
                        cond_tile(b + 1, c, LOW[3])
                    if c == 0 and (b - 2).exists():
                        prefix(b - 2)
                    if 0 < c < KT - 1:
                        variance(b, c - 1)
                    if c < KT - 1:
                        state_product(b, c)
                    if c > 0:
                        from_state(b, c)
                if is_last(b):
                    variance(b, KT - 2)
                from_scores(b, KT - 1)

            for r in range(KT):
                pe.wait_ge(s_xw[r], 32)
                for m in range(KT):
                    ins = pe.matmul(LOW[m][:], xw[:, 0, r, m * P:(m + 1) * P], xw[:, 1, r, :], start=r == 0,
                                    stop=r == KT - 1)
                    if r == KT - 1:
                        ins.then_inc(s_cond, 1)
            pe.wait_ge(s_cst, n_cst)
            pe.wait_ge(s_init, 2)
            pe.wait_ge(s_blk, 1)
            attention_bodies(pe, body)

            def e_transpose(t, e, first):
                pe.wait_ge(s_ein[e], t.at(32, 32))
                rows = rows_sb[:, e, :].rearrange("p (r c) -> p r c", r=KT)
                for k in range(KT):
                    if not first:
                        pe.wait_ge(s_relu, t.at(16, 8 * (e - 1) + 2 * k + 2))
                    for r in range(KT):
                        last = pe.transpose(LOW[k][:, r * P:(r + 1) * P], rows[:, r, k * P:(k + 1) * P], ident)
                    last.then_inc(s_etr, 1)

            def e_up(t, e):
                pe.wait_ge(s_wlo, t.at(4, 2 * e + 1))
                pe.wait_ge(s_xlo, t.at(8, 4 * e + 4))
                steps = [(k, m) for k in range(KT - 2) for m in range(KT)]
                steps += [(k, m) for m in range(KT) for k in (KT - 2, KT - 1)]
                for k, m in steps:
                    ins = split_product(LOW[m][:], w_hi[:, e, 0, k, m * P:(m + 1) * P],
                                        w_lo[:, e, 0, k, m * P:(m + 1) * P], xt_hi[:, k, :], xt_lo[:, k, :],
                                        k == 0, k == KT - 1)
                    if k == KT - 1:
                        ins.then_inc(s_up, 1)

            def e_down(t, e, part, first):
                if part == 0:
                    pe.wait_ge(s_wlo, t.at(4, 2 * e + 2))
                for m in (2 * part, 2 * part + 1):
                    pe.wait_ge(s_hlo, t.at(8, 4 * e + m + 1))
                    for r in range(KT):
                        if m == 0 and not first:
                            pe.wait_ge(s_b2, t.at(8, 4 * (e - 1) + r + 1))
                        ins = split_product(HIGH[r][:], ht_hi[:, m, r * P:(r + 1) * P],
                                            ht_lo[:, m, r * P:(r + 1) * P], w_hi[:, e, 1, m, :], w_lo[:, e, 1, m, :],
                                            m == 0, m == KT - 1)
                        if m == KT - 1:
                            ins.then_inc(s_down, 1)

            def pair(t, first, last):
                e_up(t, 0)
                e_down(t, 0, 0, first)
                e_transpose(t, 1, False)
                e_down(t, 0, 1, first)
                e_up(t, 1)
                e_down(t, 1, 0, False)
                if not last:
                    e_transpose(t + 1, 0, False)
                e_down(t, 1, 1, False)

            pe.wait_ge(s_dev, 4 * B)
            pe.wait_ge(s_rt, NR * B)
            e_transpose(Step(0, 0), 0, True)
            pair(Step(0, 0), True, False)
            with pe.Fori(0, E // 2 - 2) as i:
                pair(Step(i, 1), False, False)
            pair(Step(0, E // 2 - 1), False, True)

        @block.scalar
        def _(act):
            act.wait_ge(s_cst, n_cst)
            act.activation(rate_h[:, 0, :], rate_h[:, 1, :], ACT.Exp).then_inc(s_exp, 1)
            act.activation(rate_p[:, 0, :], rate_p[:, 1, :], ACT.Exp).then_inc(s_exp, 1)
            act.wait_ge(s_tab, 2)
            for h in range(H):
                act.activation(decay[:, h // G, h % G, :], table_cst[:, C_LAG:C_LAG + P], ACT.Exp,
                               scale=rate_h[:, 1, h:h + 1]).then_inc(s_exp, 1)
            act.activation(kpow[:], rate_h[:, 1, :], ACT.Exp, scale=cst[:, C_TAIL:C_TAIL + 1]).then_inc(s_exp, 1)
            for g in range(KT):
                act.activation(rpow[:, g, :], table_cst[:, C_Q:C_Q + P], ACT.Exp,
                               scale=rate_p[:, 1, g:g + 1]).then_inc(s_exp, 1)
            act.activation(wpow[:], rate_p[:, 1, :], ACT.Exp, scale=float(P)).then_inc(s_exp, 1)

            def h_evac(b, m, src):
                if m == 0:
                    wait(act, s_mix, (b - 1).at(16, 16))
                act.wait_ge(s_cond, b.at(4, m + 1))
                act.activation(hs[:, m, 1:T + 1], src[:], ACT.Copy).then_inc(s_hev, 1)

            def w_high(t, e, w):
                if w == 0:
                    act.wait_ge(s_we[e], t.at(32, 32))
                act.activation(w_hi[:, e, w, :, :], w_raw[:, e, w, :, :], ACT.Copy).then_inc(s_whi, 1)

            def mix_high(b, t):
                j = t - RING
                if t == 0:
                    act.wait_ge(s_cond, b.at(4, 4))
                used_wait(act, b if j >= 0 else b - 1, (j % 16) // 4, j % 4)
                act.wait_ge(s_mixed, b.at(16, t + 1))
                act.activation(mix_hi[:, t % RING, :], mixed[t % 2][:], ACT.Copy).then_inc(s_mhi, 1)

            def p_high(p):
                if p == PV_:
                    act.wait_ge(s_wv, 3)
                else:
                    act.wait_ge(s_wp[p], 16)
                act.activation(p_hi[:, p, :, :] if p < 4 else wo_hi[:], p_raw[p], ACT.Copy).then_inc(s_phi, 1)

            act.wait_ge(s_init, 2)
            act.activation(blk_hi[:], blk, ACT.Copy).then_inc(s_blk, 1)
            p_high(PV_)
            for m in range(KT):
                h_evac(Step(0, 0), m, LOW[m])

            for t in range(KT):
                mix_high(Step(0, 0), t)
            p_high(PK_)

            def proj_evac(b, p, banks):
                for m in range(KT):
                    act.wait_ge(s_proj, b.at(16, 4 * p + m + 1))
                    if m == 0:
                        if p == PV_:
                            wait(act, s_pv, b.at(16, 0))
                        if p == PR_:
                            wait(act, s_rbd, b.at(16, 0))
                            act.wait_ge(s_plo, PG_ + 1)
                        if p == PG_:
                            wait(act, s_o, b.at(4, 0))
                    if p == PG_:
                        act.activation(zt[:, m, :].rearrange("p (r q) -> p r q", r=KT),
                                       banks[m][:].rearrange("p (q r) -> p r q", r=KT), ACT.Gelu).then_inc(s_pev, 1)
                    else:
                        o = v_sb[:, m, :] if p == PV_ else kr[:, p - PK_, m, :]
                        act.activation(o, banks[m][:], ACT.Copy).then_inc(s_pev, 1)

            def lap_factor(b, n):
                if n == 0:
                    act.wait_ge(s_x1, b.at(4, 4))
                    after_attention(act, b + 1)
                if n >= 2:
                    act.wait_ge(s_lap, b.at(20, 5 * (n - 2) + 5))
                act.sem_inc(s_act_on, 1)
                act.wait_ge(s_tab, N_TAB)
                act.activation(lq_of(b)[:, n % 2, :], x1h[:, LAP_ORDER[n] + 1, :], ACT.Identity,
                               bias=zq[:, 1, bass.ds(b.index(), 1)],
                               scale=zq[:, 0, bass.ds(b.index(), 1)]).then_inc(s_lq, 1)

            def du_evac(b):
                for k in range(KT):
                    act.wait_ge(s_dtr, b.at(4, k + 1))
                    if k >= 2:
                        act.wait_ge(s_log, b.at(4, k - 1))
                    act.activation(dut[:, k % 2, :], HIGH[k][:], ACT.Copy).then_inc(s_dev, 1)

            def body(b):
                now, before, last = b.exists(), (b - 1).exists(), (b - 2).exists()
                lap = last and now
                if now:
                    mix_high(b, 4)
                    mix_high(b, 5)
                if before:
                    deviation(b - 1, KT - 1)
                if lap:
                    lap_factor(b - 2, 0)
                    lap_factor(b - 2, 1)
                if before:
                    z_high(b - 1, 1)
                if now and not before:
                    p_high(PR_)
                if now:
                    proj_evac(b, PV_, HIGH)
                    mix_high(b, 6)
                    mix_high(b, 7)
                if before:
                    affine(b - 1, KT - 2)
                elif now:
                    p_high(PG_)
                if now:
                    mix_high(b, 8)
                    mix_high(b, 9)
                if now:
                    proj_evac(b, PK_, LOW)
                if before:
                    affine(b - 1, KT - 1)
                if now:
                    mix_high(b, 10)
                    mix_high(b, 11)
                if now and not before:
                    p_high(4)
                if before:
                    z_high(b - 1, 2)
                    z_high(b - 1, 3)
                if lap:
                    lap_factor(b - 2, 2)
                if now:
                    proj_evac(b, PR_, LOW)
                    mix_high(b, 12)
                    mix_high(b, 13)
                if now:
                    mix_high(b, 14)
                    mix_high(b, 15)
                if lap:
                    lap_factor(b - 2, 3)
                if now:
                    r_spread(b, 0)
                    proj_evac(b, PG_, HIGH)
                if is_before_last(b - 1):
                    lap_factor(b - 1, 0)
                    lap_factor(b - 1, 1)
                if is_last(b - 1):
                    lap_factor(b - 1, 0)
                    lap_factor(b - 1, 1)
                if last:
                    du_evac(b - 2)
                if is_last(b - 1):
                    lap_factor(b - 1, 2)
                    lap_factor(b - 1, 3)
                if last:
                    act.wait_ge(s_rt, (b - 2).at(NR, 3))
                    act.activation(lg[:, 2, :, :], lg[:, 1, :, :], ACT.Exp).then_inc(s_rex, 1)
                if not now and not before:
                    act.wait_ge(s_pv, 16 * B)
                    for e in range(2):
                        for w in range(2):
                            w_high(Step(0, 0), e, w)
                if b.exists():
                    for c in range(KT):
                        v_mix = c == KT - 1 and (b + 1).exists()
                        if v_mix:
                            h_evac(b + 1, c, LOW[3])
                            mix_high(b + 1, 0)
                            mix_high(b + 1, 1)
                        if c > 0 and is_last(b):
                            squares(b, c - 1)
                        if c >= 2:
                            affine(b, c - 2)
                        if c > 0 and not is_last(b):
                            squares(b, c - 1)
                        if v_mix:
                            mix_high(b + 1, 2)
                            mix_high(b + 1, 3)
                        if c == KT - 1:
                            z_high(b, 0)
                        if c < KT - 1:
                            r_spread(b, c + 1)
                        if is_last(b) and 0 < c < KT - 1:
                            lap_factor(b - 1, c + 1)
                        if c < KT - 1 and (b + 1).exists():
                            h_evac(b + 1, c, LOW[3])
                        if c > 0:
                            deviation(b, c - 1)
                    squares(b, KT - 1)

            def r_spread(b, c):
                act.wait_ge(s_pev, b.at(16, 12))
                act.wait_ge(s_rz, b.at(1, 1))
                wait(act, s_sc, b.at(16, 4 * c))
                for i in range(G):
                    hp = slice(i * N, (i + 1) * N)
                    act.activation(rbd[hp, :, i, :], kr[hp, 1, :, c * P:(c + 1) * P], ACT.Copy).then_inc(s_rbd, 1)

            def squares(b, c):
                act.wait_ge(s_pv, b.at(16, 4 * c + 4))
                if c >= 2:
                    act.wait_ge(s_z, b.at(4, c - 1))
                else:
                    wait(act, s_z, b.at(4, c - 2 + 1))
                act.activation(sq[:, c % 2, :], LOW[c % 2][:], ACT.Square).then_inc(s_sq, 1)
                act.activation(z_chunk(z_hi, c), LOW[c % 2][:].rearrange("p (g r q) -> p g r q", g=KT, r=KT),
                               ACT.Square).then_inc(s_sq, 1)
                act.activation(yc[:, c % 2, :], LOW[c % 2][:], ACT.Copy).then_inc(s_sq, 1)

            def deviation(b, c):
                act.wait_ge(s_var, b.at(4, c + 1))
                act.activation(sq[:, c % 2, :], LOW[c % 2][:], ACT.Sqrt, bias=eps[:], scale=1.0 / N).then_inc(s_sd, 1)

            def z_high(b, c):
                act.wait_ge(s_z, b.at(4, c + 1))
                act.activation(z_chunk(z_hi, c), z_chunk(zt, c), ACT.Copy).then_inc(s_zhi, 1)

            def affine(b, c):
                act.wait_ge(s_nrm, b.at(8, 2 * c + 2))
                for g in range(KT):
                    y = yc[:, c % 2, g * P:(g + 1) * P]
                    act.activation(y, y, ACT.Identity, bias=lnwb[:, 1, g:g + 1], scale=lnwb[:, 0, g:g + 1]).then_inc(s_aff, 1)

            attention_bodies(act, body)

            def e_evac(t, e):
                for k in range(KT):
                    act.wait_ge(s_etr, t.at(8, 4 * e + k + 1))
                    act.activation(xt_hi[:, k, :], LOW[k][:], ACT.Copy).then_inc(s_xhi, 1)

            def e_relu(t, e, first):
                for m in range(KT):
                    act.wait_ge(s_up, t.at(8, 4 * e + m + 1))
                    if m == 0 and not first:
                        act.wait_ge(s_down, t.at(8, 4 * e))
                    act.sem_inc(s_act_on, 1)
                    act.wait_ge(s_cst2, n_cst2)
                    b1_col = b1_sb[:, bass.ds(t.index() * 2 + e, 1), m]
                    act.activation(ht[:, m, :], LOW[m][:], ACT.Relu, bias=b1_col).then_inc(s_relu, 1)
                    act.activation(ht_hi[:, m, :], LOW[m][:], ACT.Relu, bias=b1_col).then_inc(s_relu, 1)

            def pair(t, last):
                for e in range(2):
                    e_relu(t, e, isinstance(t.reg, int) and t.off == 0 and e == 0)
                    if not last:
                        act.wait_ge(s_up, t.at(8, 4 * e + 4))
                        w_high(t + 1, e, 0)
                    if e == 0:
                        e_evac(t, 1)
                    elif not last:
                        e_evac(t + 1, 0)
                    if not last:
                        act.wait_ge(s_down, t.at(8, 4 * e + 4))
                        w_high(t + 1, e, 1)

            e_evac(Step(0, 0), 0)
            pair(Step(0, 0), False)
            with act.Fori(0, E // 2 - 2) as i:
                pair(Step(i, 1), False)
            pair(Step(0, E // 2 - 1), True)

        @block.vector
        def _(dve):
            dve.memset(hs[:, :, 0:1], 0.0).then_inc(s_init, 1)
            dve.memset(ones[:], 1.0).then_inc(s_init, 1)
            dve.memset(base[:], 1.0).then_inc(s_init, 1)
            dve.memset(du[:], 0.0).then_inc(s_init, 1)
            dve.memset(eps[:], GN_EPS).then_inc(s_init, 1)
            dve.wait_ge(s_cst, n_cst)
            dve.wait_ge(s_exp, 2)
            dve.tensor_scalar(rate_h[:, 1, :], rate_h[:, 0, :], HUGE_RATE, -1.0, ALU.min, ALU.mult).then_inc(s_tab, 1)
            dve.tensor_scalar(rate_p[:, 1, :], rate_p[:, 0, :], HUGE_RATE, -1.0, ALU.min, ALU.mult).then_inc(s_tab, 1)
            def tables(part):
                for h in range(H if part == 0 else 0):
                    d = decay[:, h // G, h % G, :]
                    dve.wait_ge(s_exp, 2 + h + 1)
                    dve.tensor_tensor(d, d, table_cst[:, C_GT:C_GT + P], ALU.mult).then_inc(s_tab, 1)
                if part == 0:
                    return
                for h in range(H):
                    d = decay[:, h // G, h % G, :]
                    dve.wait_ge(s_tab, 2 + h + 1)
                    dve.scalar_tensor_tensor(d, ident, bonus_sb[:, h:h + 1], d, ALU.mult, ALU.add).then_inc(s_tab, 1)
                n_tab = N_TAB - 3
                dve.tensor_scalar(zq[:, 0, :], zs[:, 2, :], -1.0, None, ALU.mult).then_inc(s_tab, 1)
                dve.tensor_tensor(zq[:, 1, :], zs[:, 0, :], zs[:, 1, :], ALU.add).then_inc(s_tab, 1)
                dve.wait_ge(s_tab, n_tab + 2)
                dve.scalar_tensor_tensor(zq[:, 1, :], zq[:, 1, :], -2.0, zs[:, 2, :], ALU.mult, ALU.add).then_inc(s_tab, 1)

            def mixed_tile(b, t):
                p, tt = t // 4, t % 4
                m = mixed[t % 2][:]
                dve.wait_ge(s_diff, b.at(16, t + 1))
                dve.scalar_tensor_tensor(m, m, maa_sb[:, p, tt:tt + 1], hs[:, tt, 1:T + 1],
                                         ALU.mult, ALU.add).then_inc(s_mixed, 1)

            def mixed_low(b, t):
                dve.wait_ge(s_mhi, b.at(16, t + 1))
                dve.tensor_tensor(mix_lo[:, t % RING, :], mixed[t % 2][:], mix_hi[:, t % RING, :].bitcast(F32),
                                  ALU.subtract).then_inc(s_mix, 1)

            def p_low(p):
                dve.wait_ge(s_phi, p + 1)
                hi, lo = (p_hi[:, p, :, :], p_lo[:, p, :, :]) if p < 4 else (wo_hi[:], wo_lo[:])
                dve.tensor_tensor(lo, p_raw[p], hi.bitcast(F32),
                                  ALU.subtract).then_inc(s_plo, 1)

            def laplacian(b, n):
                r = LAP_ORDER[n]
                y = x1h[:, r + 1, :]
                s = b.index()
                lhr, lvr, lqr = lh_of(b)[:, n % 2, :], lv_of(b)[:, n % 2, :], lq_of(b)[:, n % 2, :]
                if n == 0:
                    after_attention(dve, b + 1)
                if n == 0 and (is_last(b) or is_before_last(b)):
                    dve.wait_ge(s_x1, b.at(4, 4))
                dve.tensor_tensor(lhr[:, 1:D - 1], y[:, 0:D - 2], y[:, 2:D], ALU.add).then_inc(s_lap, 1)
                dve.tensor_scalar(lhr[:, 0:D:D - 1], y[:, 1:D - 1:D - 3], 2.0, None, ALU.mult).then_inc(s_lap, 1)
                dve.wait_ge(s_lq, b.at(4, n + 1))
                dve.tensor_tensor(lqr, lqr, y, ALU.mult).then_inc(s_lap, 1)
                dve.wait_ge(s_lap, b.at(20, 5 * n + 3))
                dve.scalar_tensor_tensor(lqr, lhr, zs[:, 0, bass.ds(s, 1)], lqr, ALU.mult, ALU.add).then_inc(s_lap, 1)
                dve.wait_ge(s_lap, b.at(20, 5 * n + 4))
                dve.wait_ge(s_lv, b.at(4, n + 1))
                dve.scalar_tensor_tensor(du_of(b)[:, r, 0:D], lvr, zs[:, 1, bass.ds(s, 1)], lqr, ALU.mult,
                                         ALU.add).then_inc(s_lap, 1)

            def residual(b):
                dve.wait_ge(s_resid, b.at(16, 16))
                for r in range(KT):
                    dve.wait_ge(s_o, b.at(4, r + 1))
                    dve.tensor_tensor(x1h[:, r + 1, :], LOW[r][:], x1h[:, r + 1, :], ALU.add).then_inc(s_x1, 1)

            def bc_e(v):
                return v.unsqueeze(2).to_broadcast([P, KT, E])

            def bc_r(v):
                return v.unsqueeze(1).to_broadcast([P, KT, E])

            def router(b, part):
                n = [8 * part]

                def step(ins):
                    n[0] += 1
                    ins.then_inc(s_rt, 1)
                    return n[0]

                def after(k):
                    dve.wait_ge(s_rt, b.at(NR, k))

                L, S_, X_, EQ, CA, MK, PO, W_ = (lg[:, i, :, :] for i in range(8))
                mx, cm, se, gate, pn, en, keep, slot = (rs[:, i, :] for i in range(8))
                if part == 0:
                    dve.wait_ge(s_log, b.at(4, 4))
                    a = step(dve.tensor_tensor(L, LOW[0][:, 0:KT * E].rearrange("p (r e) -> p r e", r=KT),
                                               bc_r(rb_sb[:]), ALU.add))
                    after(a)
                    a = step(dve.tensor_reduce(mx, L, AX.X, ALU.max))
                    after(a)
                    step(dve.tensor_tensor(S_, L, bc_e(mx), ALU.subtract))
                    a = step(dve.tensor_tensor(EQ, L, bc_e(mx), ALU.is_equal))
                    after(a)
                    a = step(dve.tensor_tensor(CA, EQ, bc_r(cst[:, C_PRI:C_PRI + E]), ALU.mult))
                    after(a)
                    a = step(dve.tensor_reduce(cm, CA, AX.X, ALU.max))
                    after(a)
                    a = step(dve.tensor_tensor(MK, CA, bc_e(cm), ALU.is_equal))
                    after(a)
                    a = step(dve.tensor_reduce(cnt[:], MK.rearrange("p r e -> p e r"), AX.X, ALU.add))
                    assert a == 8
                    return
                dve.wait_ge(s_rex, b.at(1, 1))
                a = step(dve.tensor_reduce(se, X_, AX.X, ALU.add))
                after(a)
                step(dve.reciprocal(gate, se))
                dve.wait_ge(s_pre, b.at(1, 1))
                step(dve.tensor_tensor(PO[:, 0, :], LOW[1][:, 0:E], base[:], ALU.add))
                after(11)
                a = step(dve.tensor_tensor(base[:], LOW[1][:, E:2 * E], base[:], ALU.add))
                assert a == 12
                for r in range(1, KT):
                    after(a)
                    a = step(dve.tensor_tensor(PO[:, r, :], PO[:, r - 1, :], MK[:, r - 1, :], ALU.add))
                after(a)
                a = step(dve.tensor_tensor(W_, MK, PO, ALU.mult))
                after(a)
                a = step(dve.tensor_reduce(pn, W_, AX.X, ALU.add))
                after(a)
                a = step(dve.tensor_tensor(W_, MK, bc_r(cst[:, C_EOFF:C_EOFF + E]), ALU.mult))
                after(a)
                a = step(dve.tensor_reduce(en, W_, AX.X, ALU.add))
                after(a)
                step(dve.tensor_scalar(keep, pn, float(CAP), None, ALU.is_lt))
                a = step(dve.tensor_tensor(slot, pn, en, ALU.add))
                after(a)
                a = step(dve.tensor_tensor(slot, slot, trash[:], ALU.subtract))
                after(a)
                a = step(dve.tensor_tensor(slot, slot, keep, ALU.mult))
                after(a)
                if is_last(b):
                    dve.wait_ge(s_scat, 64 * (B - 1) + N_ZERO)
                else:
                    dve.wait_ge(s_scat, b.at(64, N_ZERO))
                a = step(dve.tensor_tensor(slot_i[:], slot, trash[:], ALU.add))
                assert a == 24
                step(dve.tensor_scalar(du_of(b)[:, :, META_TOKEN], trash[:], 1.0 - B * T, None, ALU.add))
                after(25)
                step(dve.tensor_scalar(trash[:], trash[:], float(T), None, ALU.add))
                step(dve.tensor_copy(du_of(b)[:, :, META_GATE], gate))
                for r in range(KT):
                    step(dve.tensor_scalar(du_of(b)[:, r, 0:D], du_of(b)[:, r, 0:D], gate[:, r:r + 1], None, ALU.mult))
                assert n[0] == NR

            def mask(b, c, i):
                dve.wait_ge(s_sc, b.at(16, 4 * c + i + 1))
                if c > 0:
                    dve.wait_ge(s_pv, b.at(16, 4 * (c - 1) + i + 1))
                else:
                    wait(dve, s_pv, b.at(16, i - 3))
                dve.tensor_tensor(att[:, i, :], HIGH[i][:], decay[:, i, :, :].rearrange("p h q -> p (h q)"),
                                  ALU.mult).then_inc(s_mask, 1)

            def k_decay(b, c):
                dve.wait_ge(s_ktr, b.at(3, c + 1))
                wait(dve, s_kv, b.at(3, c))
                dve.tensor_tensor(kdec[:].rearrange("p (h n) -> p h n", n=N), LOW[2][:].rearrange("p (h n) -> p h n", n=N),
                                  kpow[:].unsqueeze(2).to_broadcast([P, H, N]), ALU.mult).then_inc(s_kdec, 1)

            def state_step(b, c):
                dve.wait_ge(s_kv, b.at(3, c + 1))
                new = st_new[:] if c else state[:, 1, :, :].rearrange("p g q -> p (g q)")
                if c == 0:
                    wait(dve, s_inter, b.at(3, 0))
                    wait(dve, s_wst, b.at(2, 0))
                dve.tensor_tensor(new.rearrange("p (g q) -> p g q", g=KT), LOW[2][:].rearrange("p (g q) -> p g q", g=KT),
                                  blk.unsqueeze(1).to_broadcast([P, KT, P]), ALU.mult).then_inc(s_st, 1)
                if c:
                    dve.wait_ge(s_st, b.at(5, 2 * c))
                    dve.wait_ge(s_wst, b.at(2, c))
                    dst = state[:, (c + 1) % 2, :, :].rearrange("p g q -> p (g q)")
                    dve.tensor_tensor(dst, st_new[:], st_old[:], ALU.add).then_inc(s_st, 1)

            def w_low(t, e, w):
                dve.wait_ge(s_whi, t.at(4, 2 * e + w + 1))
                dve.tensor_tensor(w_lo[:, e, w, :, :], w_raw[:, e, w, :, :], w_hi[:, e, w, :, :].bitcast(F32),
                                  ALU.subtract).then_inc(s_wlo, 1)

            def z_low(b, c):
                dve.wait_ge(s_zhi, b.at(4, c + 1))
                dve.tensor_tensor(z_chunk(z_lo, c), z_chunk(zt, c), z_chunk(z_hi, c).bitcast(F32),
                                   ALU.subtract).then_inc(s_zlo, 1)

            def sq_low(b, c):
                dve.wait_ge(s_sq, b.at(12, 3 * c + 2))
                dve.tensor_tensor(sq_lo[:, c % 2, :].rearrange("p (g r q) -> p g r q", g=KT, r=KT),
                                  sq[:, c % 2, :].rearrange("p (g r q) -> p g r q", g=KT, r=KT),
                                  z_chunk(z_hi, c).bitcast(F32), ALU.subtract).then_inc(s_sqlo, 1)

            def divide(b, c):
                dve.wait_ge(s_sd, b.at(4, c + 1))
                dve.reciprocal(sq[:, c % 2, :], sq[:, c % 2, :]).then_inc(s_nrm, 1)
                dve.wait_ge(s_nrm, b.at(8, 2 * c + 1))
                dve.tensor_tensor(yc[:, c % 2, :], yc[:, c % 2, :], sq[:, c % 2, :], ALU.mult).then_inc(s_nrm, 1)

            def body(b):
                now, before, last = b.exists(), (b - 1).exists(), (b - 2).exists()
                if last and not is_last(b - 2):
                    dve.wait_ge(s_halo, (b - 2).at(96, 96))
                    dve.wait_ge(s_scat, (b - 2).at(64, N_ZERO))
                for t in range(4, 16, 2):
                    if now:
                        mixed_tile(b, t)
                        mixed_tile(b, t + 1)
                        mixed_low(b, t)
                        mixed_low(b, t + 1)
                    if before and t == 8:
                        z_low(b - 1, 1)
                        if is_last(b - 1):
                            laplacian(b - 2, 3)
                    if before and t == 10:
                        z_low(b - 1, 2)
                        z_low(b - 1, 3)
                    if t < 8:
                        if before:
                            divide(b - 1, KT - 2 if t == 4 else KT - 1)
                        elif now:
                            p_low(PR_ if t == 4 else PG_)
                    elif last and now:
                        for n in ((), (0,), (1,), (2, 3))[(t - 8) // 2]:
                            laplacian(b - 2, n)
                    elif now and not before and t == 10:
                        p_low(4)
                    elif now and not before and t == 12:
                        tables(0)
                if now:
                    if before:
                        dve.wait_ge(s_o, (b - 1).at(4, 4))
                    else:
                        dve.wait_ge(s_wo_out, 16)
                    dve.memset(rbd[:], 0.0).then_inc(s_rz, 1)
                if now and not before:
                    tables(1)
                if before:
                    residual(b - 1)
                if is_before_last(b - 1):
                    dve.wait_ge(s_proj, 16 * B)
                    dve.memset(du_alt[:, :, META_TOKEN + 1:EW], 0.0).then_inc(s_init, 1)
                    laplacian(b - 1, 0)
                    laplacian(b - 1, 1)
                if is_last(b - 1):
                    for n in range(KT):
                        laplacian(b - 1, n)
                    router(b - 2, 0)
                    router(b - 2, 1)
                if last and now:
                    router(b - 2, 0)
                if is_last(b - 2):
                    router(b - 2, 0)
                    router(b - 2, 1)
                    for e in range(2):
                        for w in range(2):
                            w_low(Step(0, 0), e, w)
                if not now:
                    return
                for c in range(KT):
                    v_mix = c == KT - 1 and (b + 1).exists()
                    for i in range(G):
                        if v_mix and i == 0:
                            mixed_low(b + 1, 0)
                        mask(b, c, i)
                        if i == 0 and c < KT - 1:
                            k_decay(b, c)
                        if i == 1 and 0 < c < KT - 1:
                            sq_low(b, c - 1)
                    if c == KT - 1:
                        if v_mix:
                            mixed_low(b + 1, 1)
                        sq_low(b, c - 1)
                    if v_mix:
                        mixed_tile(b + 1, 2)
                        mixed_tile(b + 1, 3)
                        mixed_low(b + 1, 2)
                        mixed_low(b + 1, 3)
                    if c == KT - 1:
                        z_low(b, 0)
                        if is_last(b):
                            laplacian(b - 1, 2)
                    if c < KT - 1:
                        state_step(b, c)
                    if 0 < c < KT - 1:
                        divide(b, c - 1)
                    if c == KT - 2 and (b + 1).exists():
                        mixed_tile(b + 1, 0)
                        mixed_tile(b + 1, 1)
                    if c == 0 and last:
                        router(b - 2, 1)
                sq_low(b, KT - 1)

            dve.wait_ge(s_cst2, n_cst2)
            wv = p_raw[PV_].rearrange("p k (h n) -> p k h n", n=N)
            dve.wait_ge(s_wp[PV_], 16)
            dve.tensor_reduce(vmean, wv, AX.X, ALU.add).then_inc(s_wv, 1)
            dve.wait_ge(s_wv, 1)
            dve.tensor_scalar(vmean, vmean, 1.0 / N, None, ALU.mult).then_inc(s_wv, 1)
            dve.wait_ge(s_wv, 2)
            dve.tensor_tensor(wv, wv, vmean.unsqueeze(3).to_broadcast([P, KT, H, N]), ALU.subtract).then_inc(s_wv, 1)
            p_low(PV_)
            for t in (0, 2):
                mixed_tile(Step(0, 0), t)
                mixed_tile(Step(0, 0), t + 1)
                mixed_low(Step(0, 0), t)
                mixed_low(Step(0, 0), t + 1)
            p_low(PK_)
            attention_bodies(dve, body)

            def tokens(t, e):
                rows = rows_sb[:, e, :].rearrange("p (r c) -> p r c", r=KT)
                dve.wait_ge(s_ein[e], t.at(32, 32))
                wait(dve, s_add[e], t.at(64, 0))
                dve.tensor_scalar(tok_f[:, e, :], rows[:, :, META_TOKEN], 0.0, None, ALU.is_equal).then_inc(s_tok, 1)
                dve.wait_ge(s_tok, t.at(8, 4 * e + 1))
                dve.tensor_tensor(tok_f[:, e, :], tok_f[:, e, :],
                                  cst[:, C_TRASH + e * KT:C_TRASH + (e + 1) * KT], ALU.mult).then_inc(s_tok, 1)
                dve.tensor_copy(gate_e[:, e, :], rows[:, :, META_GATE]).then_inc(s_tok, 1)
                dve.wait_ge(s_tok, t.at(8, 4 * e + 3))
                dve.scalar_tensor_tensor(tok_i[:, e, :], tok_f[:, e, :], -1.0, rows[:, :, META_TOKEN], ALU.add,
                                         ALU.add).then_inc(s_tok, 1)

            def x_low(t, e):
                for k in range(KT):
                    dve.wait_ge(s_xhi, t.at(8, 4 * e + k + 1))
                    dve.tensor_tensor(xt_lo[:, k, :], LOW[k][:], xt_hi[:, k, :].bitcast(F32),
                                      ALU.subtract).then_inc(s_xlo, 1)

            def hidden_low(t, e):
                for m in range(KT):
                    dve.wait_ge(s_relu, t.at(16, 8 * e + 2 * m + 2))
                    dve.tensor_tensor(ht_lo[:, m, :], ht[:, m, :], ht_hi[:, m, :].bitcast(F32),
                                      ALU.subtract).then_inc(s_hlo, 1)

            def results(t, e):
                for r in range(KT):
                    dve.wait_ge(s_down, t.at(8, 4 * e + r + 1))
                    dve.tensor_tensor(res[:, e, r, :], HIGH[r][:], b2_sb[:, e, :], ALU.add).then_inc(s_b2, 1)
                for r in range(KT):
                    dve.wait_ge(s_b2, t.at(8, 4 * e + r + 1))
                    dve.tensor_scalar(res[:, e, r, :], res[:, e, r, :], gate_e[:, e, r:r + 1], None,
                                      ALU.mult).then_inc(s_gate, 1)

            def pair(t, last):
                for e in range(2):
                    tokens(t, e)
                    hidden_low(t, e)
                    if not last:
                        w_low(t + 1, e, 0)
                    if e == 0:
                        x_low(t, 1)
                    elif not last:
                        x_low(t + 1, 0)
                    results(t, e)
                    if not last:
                        w_low(t + 1, e, 1)

            x_low(Step(0, 0), 0)
            pair(Step(0, 0), False)
            with dve.Fori(0, E // 2 - 2) as i:
                pair(Step(i, 1), False)
            pair(Step(0, E // 2 - 1), True)

        @block.gpsimd
        def _(pool):
            pool.wait_ge(s_cst2, n_cst2)
            pool.wait_ge(s_exp, 2 + H + 1 + KT + 1)

            def difference(b, t):
                if t < KT:
                    pool.wait_ge(s_hev, b.at(4, t + 1))
                    if t == 0 and (b - 1).exists():
                        pool.wait_ge(s_st, (b - 1).at(5, 5))
                if t >= 2:
                    pool.wait_ge(s_mix, b.at(16, t - 1))
                elif (b - 1).exists():
                    pool.wait_ge(s_mix, b.at(16, t - 1))
                pool.tensor_tensor(mixed[t % 2][:], hs[:, t % 4, 0:T], hs[:, t % 4, 1:T + 1], ALU.subtract).then_inc(s_diff, 1)

            def vertical(b, n):
                r = LAP_ORDER[n]
                if (is_last(b) or is_before_last(b)) and r in (1, 2):
                    pool.wait_ge(s_x1, b.at(4, r + 2))
                else:
                    pool.wait_ge(s_halo, b.at(96, 96))
                if n == 0:
                    after_attention(pool, b + 1)
                    if is_last(b):
                        pool.wait_ge(s_lap, 20 * (B - 1))
                if n >= 2:
                    pool.wait_ge(s_lap, b.at(20, 5 * (n - 2) + 5))
                pool.tensor_tensor(lv_of(b)[:, n % 2, :], x1h[:, r, :], x1h[:, r + 2, :], ALU.add).then_inc(s_lv, 1)

            def r_decay(b, c):
                pool.wait_ge(s_pev, b.at(16, 12))
                if c == 1 and (b - 2).exists():
                    pool.wait_ge(s_log, (b - 2).at(4, 4))
                if c >= 3:
                    pool.wait_ge(s_inter, b.at(3, c - 2))
                else:
                    wait(pool, s_inter, b.at(3, 0))
                pool.tensor_tensor(rdec[:, c % 2, :, :], kr[:, 1, :, c * P:(c + 1) * P], rpow[:], ALU.mult).then_inc(s_rdec, 1)

            def state_decay(b, c):
                pool.wait_ge(s_st, b.at(5, 2 * c - 1))
                pool.tensor_tensor(st_old[:].rearrange("p (g q) -> p g q", g=KT), state[:, c % 2, :, :],
                                   wpow[:].unsqueeze(2).to_broadcast([P, KT, P]), ALU.mult).then_inc(s_wst, 1)

            def z_product(b, c):
                pool.wait_ge(s_aff, b.at(16, 4 * c + 4))
                pool.wait_ge(s_pev, b.at(16, 16))
                pool.tensor_tensor(z_chunk(zt, c), yc[:, c % 2, :].rearrange("p (g q r) -> p g r q", g=KT, r=KT),
                                   z_chunk(zt, c), ALU.mult).then_inc(s_z, 1)

            def store_zeros():
                pool.wait_ge(s_init, 4)
                for r in range(KT):
                    pool.wait_ge(s_xw[r], 64)
                for e in range(E):
                    pool.dma_start(slots[e * CAP:(e + 1) * CAP].rearrange("(p r) c -> p r c", r=KT), du[:]).then_inc(s_scat, 16)
                for e in range(2):
                    at = B * T + e * CAP
                    pool.dma_start(out[at:at + CAP].rearrange("(p r) c -> p r c", r=KT), du[:, :, 0:D]).then_inc(s_scat, 16)

            def scatter(b):
                pool.wait_ge(s_rt, b.at(NR, NR))
                pool.sem_inc(s_pool_on, 1)
                pool.wait_ge(s_scat, N_ZERO)
                for r in range(KT):
                    pool.indirect_dma_start(slots, bass.IndirectOffsetOnAxis(slot_i[:, r:r + 1], 0),
                                            du_of(b)[:, r, :], None).then_inc(s_scat, 16)

            def body(b):
                now, before, last = b.exists(), (b - 1).exists(), (b - 2).exists()
                if now:
                    for t in range(4, 10):
                        difference(b, t)
                lap = last and now
                if lap:
                    vertical(b - 2, 0)
                    vertical(b - 2, 1)
                if before:
                    z_product(b - 1, 2)
                if now:
                    difference(b, 10)
                    difference(b, 11)
                if before:
                    z_product(b - 1, 3)
                if now:
                    difference(b, 12)
                    difference(b, 13)
                if lap:
                    vertical(b - 2, 2)
                if now:
                    difference(b, 14)
                    difference(b, 15)
                if lap:
                    vertical(b - 2, 3)
                if now and not before:
                    store_zeros()
                if is_before_last(b - 1):
                    vertical(b - 1, 0)
                    vertical(b - 1, 1)
                if now:
                    r_decay(b, 1)
                    r_decay(b, 2)
                if is_last(b - 1):
                    for n in range(KT):
                        vertical(b - 1, n)
                if last:
                    scatter(b - 2)
                if now:
                    state_decay(b, 1)
                    r_decay(b, 3)
                    if is_last(b):
                        vertical(b - 1, 2)
                    z_product(b, 0)
                    state_decay(b, 2)
                    if is_last(b):
                        vertical(b - 1, 3)
                    if (b + 1).exists():
                        difference(b + 1, 0)
                        difference(b + 1, 1)
                    z_product(b, 1)
                    if (b + 1).exists():
                        difference(b + 1, 2)
                        difference(b + 1, 3)

            for t in range(KT):
                difference(Step(0, 0), t)
            attention_bodies(pool, body)

            def add_rows(t, e):
                pool.wait_ge(s_tok, t.at(8, 4 * e + 4))
                for r in range(KT):
                    pool.wait_ge(s_gate, t.at(8, 4 * e + r + 1))
                    pool.sem_inc(s_pool_on, 1)
                    pool.wait_ge(s_store, 16 * B)
                    pool.indirect_dma_start(out, bass.IndirectOffsetOnAxis(tok_i[:, e, r:r + 1], 0),
                                            res[:, e, r, :], None, compute_op=ALU.add).then_inc(s_add[e], 16)

            with pool.Fori(0, E // 2) as i:
                for e in range(2):
                    add_rows(Step(i, 0), e)
            for e in range(2):
                pool.wait_ge(s_add[e], 64 * (E // 2))


def kernel(x, itok_B_0_30, condB_zX, condB_zY, condB_zR, L0_cond_weights, L0_attn_time_maa_k, L0_attn_time_maa_v,
           L0_attn_time_maa_r, L0_attn_time_maa_g, L0_attn_time_decay, L0_attn_time_faaaa, L0_attn_Wr, L0_attn_Wk,
           L0_attn_Wv, L0_attn_Wg, L0_attn_Wo, L0_attn_ln_w, L0_attn_ln_b, L0_ffn_Wr, L0_ffn_br, L0_ffn_W1,
           L0_ffn_b1, L0_ffn_W2, L0_ffn_b2):
    import concourse.bacc as bacc
    from concourse.bass_utils import run_bass_kernel_spmd

    def channels(a):
        return np.asarray(a).reshape(KT, P).T

    maas = (L0_attn_time_maa_v, L0_attn_time_maa_k, L0_attn_time_maa_r, L0_attn_time_maa_g)
    projections = (L0_attn_Wv, L0_attn_Wk, L0_attn_Wr, L0_attn_Wg)
    arrays = {
        "x": x,
        "subj": np.asarray(itok_B_0_30).reshape(1, B),
        "zxyr": np.stack([condB_zX, condB_zY, condB_zR])[None],
        "wcond": L0_cond_weights,
        "maa": np.stack([channels(a) for a in maas], axis=1),
        "wproj": np.stack([np.asarray(a).T for a in projections]),
        "wo": np.asarray(L0_attn_Wo).T,
        "decay_heads": np.asarray(L0_attn_time_decay).reshape(1, H),
        "decay_rows": np.repeat(np.asarray(L0_attn_time_decay).reshape(KT, G).T, N, axis=0),
        "bonus": np.asarray(L0_attn_time_faaaa).reshape(1, H),
        "ln_wb": np.stack([channels(a) for a in (L0_attn_ln_w, L0_attn_ln_b)], axis=1),
        "router_w": L0_ffn_Wr,
        "router_b": np.asarray(L0_ffn_br).reshape(1, E),
        "w1": L0_ffn_W1,
        "b1": np.asarray(L0_ffn_b1).reshape(E, KT, P).transpose(2, 0, 1),
        "w2": L0_ffn_W2,
        "b2": L0_ffn_b2,
        "consts": shape_constants(),
    }
    arrays = {f"in_{k}": np.ascontiguousarray(v) for k, v in arrays.items()}
    nc = bacc.Bacc("TRN2", target_bir_lowering=False, num_devices=1)
    args = [nc.dram_tensor(k, a.shape, mybir.dt.from_np(a.dtype), kind="ExternalInput").ap()
            for k, a in arrays.items()]
    out = nc.dram_tensor("out_rows", (B * T + TRASH_ROWS, D), F32, kind="ExternalOutput").ap()
    build(nc, *args, out)
    result = run_bass_kernel_spmd(nc, [arrays], core_ids=[0])
    return result.results[0]["out_rows"][:B * T].reshape(B, T, D)
```
